# Optimizing a Trainium2 kernel written in Bass

```python
import numpy as np
import jax
import jax.numpy as jnp

def _softmax(x, axis=-1):
    return jax.nn.softmax(x, axis=axis)

def _gelu(x):
    return jax.nn.gelu(x, approximate=True)

def _silu(x):
    return jax.nn.silu(x)

def _sigmoid(x):
    return jax.nn.sigmoid(x)

def _layernorm(x, axis=-1, eps=1e-05):
    m = jnp.mean(x, axis=axis, keepdims=True)
    v = jnp.var(x, axis=axis, keepdims=True)
    return (x - m) / jnp.sqrt(v + eps)

def _scatter_add(tgt, idx, src, axis=0):
    return tgt.at[idx].add(src)

def _segment_sum(src, seg, n):
    return jax.ops.segment_sum(src, seg, n)
kernel_name = 'mk_xattn_ffn_d2_seqx_r8_40475f'

def setup_inputs(seed: int=0):
    np.random.seed(seed)
    _w = jnp.asarray

    def _rec_inputs():
        import jax
        import jax.numpy as jnp
        _rk = jax.random.key(seed)
        x = 0.002226 + 0.9996 * jax.random.normal(jax.random.fold_in(_rk, 1), (4, 256, 128), jnp.float32)
        _lenS = 256 - jax.random.randint(jax.random.fold_in(_rk, 7), (4,), 0, max(1, 256 // 4) + 1, jnp.int32)
        _lenS2 = 512 - jax.random.randint(jax.random.fold_in(_rk, 8), (4,), 0, max(1, 512 // 4) + 1, jnp.int32)
        _ctx_1024P = jax.random.normal(jax.random.fold_in(_rk, 11), (4, 16, 128), jnp.float32)
        _ctx_1024c = jax.random.dirichlet(jax.random.fold_in(_rk, 511), 0.3 * jnp.ones((16,), jnp.float32), (4, 512))
        _ctx_1024t = jnp.einsum('bsk,bkd->bsd', _ctx_1024c, _ctx_1024P)
        _ctx_1024t = _ctx_1024t * jax.lax.rsqrt(jnp.mean(jnp.square(_ctx_1024t)) + 1e-12) * 0.953939
        ctx_1024 = -0.000125008 + 0.999885 * (_ctx_1024t + 0.3 * jax.random.normal(jax.random.fold_in(_rk, 611), (4, 512, 128), jnp.float32))
        return (x, ctx_1024)
    x, ctx_1024 = _rec_inputs()

    def _L0_xattn_setup():
        import jax, jax.numpy as jnp
        import numpy as np
        EPS = 1e-05

        def layer_norm(x, g, b):
            mu = jnp.mean(x, axis=-1, keepdims=True)
            var = jnp.var(x, axis=-1, keepdims=True)
            return (x - mu) * jax.lax.rsqrt(var + EPS) * g + b
        key = jax.random.key(seed)
        ks = jax.random.split(key, 8)
        dim, heads, dim_head = (128, 16, 64)
        inner = heads * dim_head
        b, n, m = (8, 512, 64)
        s = dim ** (-0.5)
        return {'x': jax.random.normal(ks[0], (b, n, dim), jnp.float32), 'latents': jax.random.normal(ks[1], (b, m, dim), jnp.float32), 'ln_m_g': jnp.ones((dim,), jnp.float32), 'ln_m_b': jnp.zeros((dim,), jnp.float32), 'ln_l_g': jnp.ones((dim,), jnp.float32), 'ln_l_b': jnp.zeros((dim,), jnp.float32), 'Wq': jax.random.normal(ks[2], (dim, inner), jnp.float32) * s, 'Wkv': jax.random.normal(ks[3], (dim, 2 * inner), jnp.float32) * s, 'Wout': jax.random.normal(ks[4], (inner, dim), jnp.float32) * s}
    _L0_xattn_all = _L0_xattn_setup()
    _L0_xattn_in = {k: v for k, v in _L0_xattn_all.items() if k in ('ln_m_g', 'ln_m_b', 'ln_l_g', 'ln_l_b', 'Wq', 'Wkv', 'Wout')}
    del _L0_xattn_all

    def _L0_ffn_setup():
        import jax, jax.numpy as jnp
        import numpy as np
        D_MODEL = 128
        HIDDEN = 512
        NUM_EXPERTS = 8
        TOP_K = 2
        key = jax.random.key(seed)
        k_x, k_g, k_in, k_out = jax.random.split(key, 4)
        bound_in = 1.0 / HIDDEN
        bound_out = 1.0 / D_MODEL
        x = jax.random.normal(k_x, (2, 256, D_MODEL), dtype=jnp.float32)
        w_gate = jax.random.uniform(k_g, (NUM_EXPERTS, D_MODEL), dtype=jnp.float32, minval=-D_MODEL ** (-0.5), maxval=D_MODEL ** (-0.5))
        w_in = jax.random.uniform(k_in, (NUM_EXPERTS, HIDDEN, D_MODEL), dtype=jnp.float32, minval=-bound_in, maxval=bound_in)
        w_out = jax.random.uniform(k_out, (NUM_EXPERTS, D_MODEL, HIDDEN), dtype=jnp.float32, minval=-bound_out, maxval=bound_out)
        return {'x': x, 'w_gate': w_gate, 'w_in': w_in, 'w_out': w_out}
    _L0_ffn_all = _L0_ffn_setup()
    _L0_ffn_in = {k: v for k, v in _L0_ffn_all.items() if k in ('w_gate', 'w_in', 'w_out')}
    del _L0_ffn_all

    def _L1_xattn_setup():
        import jax, jax.numpy as jnp
        import numpy as np
        EPS = 1e-06

        def _rmsnorm(x, w, eps=EPS):
            x32 = x.astype(jnp.float32)
            var = jnp.mean(x32 * x32, axis=-1, keepdims=True)
            return (x32 * jax.lax.rsqrt(var + eps)).astype(x.dtype) * w
        key = jax.random.key(seed)
        ks = jax.random.split(key, 6)
        B, S, K, H = (4, 256, 64, 128)
        return {'hidden_states': jax.random.normal(ks[0], (B, S, H), jnp.float32), 'memory_state': jax.random.normal(ks[1], (B, K, H), jnp.float32), 'q_w': jax.random.normal(ks[2], (H, H), jnp.float32) * (1.0 / np.sqrt(H)), 'k_w': jax.random.normal(ks[3], (H, H), jnp.float32) * (1.0 / np.sqrt(H)), 'norm_w': jnp.ones((H,), jnp.float32), 'gate_w': jax.random.normal(ks[4], (H, H), jnp.float32) * 0.02, 'gate_b': jnp.zeros((H,), jnp.float32)}
    _L1_xattn_all = _L1_xattn_setup()
    _L1_xattn_in = {k: v for k, v in _L1_xattn_all.items() if k in ('q_w', 'k_w', 'norm_w', 'gate_w', 'gate_b')}
    del _L1_xattn_all

    def _L1_ffn_setup():
        import jax, jax.numpy as jnp
        import numpy as np
        B, S, H = (8, 128, 128)
        FF = 512
        E = 8
        TOP_K = 2
        LN_EPS = 1e-12

        def _layernorm(x, w, b):
            mu = jnp.mean(x, axis=-1, keepdims=True)
            var = jnp.mean(jnp.square(x - mu), axis=-1, keepdims=True)
            return (x - mu) * jax.lax.rsqrt(var + LN_EPS) * w + b
        key = jax.random.key(seed)
        ks = jax.random.split(key, 8)
        sc_h = 1.0 / np.sqrt(H)
        sc_ff = 1.0 / np.sqrt(FF)
        return {'hidden_states': jax.random.normal(ks[0], (B, S, H), jnp.float32), 'router_w': jax.random.normal(ks[1], (E, H), jnp.float32) * sc_h, 'router_b': jnp.zeros((E,), jnp.float32), 'w1': jax.random.normal(ks[2], (E, FF, H), jnp.float32) * sc_h, 'b1': jax.random.normal(ks[3], (E, FF), jnp.float32) * 0.01, 'w2': jax.random.normal(ks[4], (E, H, FF), jnp.float32) * sc_ff, 'b2': jax.random.normal(ks[5], (E, H), jnp.float32) * 0.01, 'ln_w': jnp.ones((H,), jnp.float32), 'ln_b': jnp.zeros((H,), jnp.float32)}
    _L1_ffn_all = _L1_ffn_setup()
    _L1_ffn_in = {k: v for k, v in _L1_ffn_all.items() if k in ('router_w', 'router_b', 'w1', 'b1', 'w2', 'b2', 'ln_w', 'ln_b')}
    del _L1_ffn_all
    return {'x': x, 'ctx_1024': ctx_1024, 'L0_xattn_ln_m_g': _L0_xattn_in['ln_m_g'], 'L0_xattn_ln_m_b': _L0_xattn_in['ln_m_b'], 'L0_xattn_ln_l_g': _L0_xattn_in['ln_l_g'], 'L0_xattn_ln_l_b': _L0_xattn_in['ln_l_b'], 'L0_xattn_Wq': _L0_xattn_in['Wq'], 'L0_xattn_Wkv': _L0_xattn_in['Wkv'], 'L0_xattn_Wout': _L0_xattn_in['Wout'], 'L0_ffn_w_gate': _L0_ffn_in['w_gate'], 'L0_ffn_w_in': _L0_ffn_in['w_in'], 'L0_ffn_w_out': _L0_ffn_in['w_out'], 'L1_xattn_q_w': _L1_xattn_in['q_w'], 'L1_xattn_k_w': _L1_xattn_in['k_w'], 'L1_xattn_norm_w': _L1_xattn_in['norm_w'], 'L1_xattn_gate_w': _L1_xattn_in['gate_w'], 'L1_xattn_gate_b': _L1_xattn_in['gate_b'], 'L1_ffn_router_w': _L1_ffn_in['router_w'], 'L1_ffn_router_b': _L1_ffn_in['router_b'], 'L1_ffn_w1': _L1_ffn_in['w1'], 'L1_ffn_b1': _L1_ffn_in['b1'], 'L1_ffn_w2': _L1_ffn_in['w2'], 'L1_ffn_b2': _L1_ffn_in['b2'], 'L1_ffn_ln_w': _L1_ffn_in['ln_w'], 'L1_ffn_ln_b': _L1_ffn_in['ln_b']}

def reference(x, ctx_1024, L0_xattn_ln_m_g, L0_xattn_ln_m_b, L0_xattn_ln_l_g, L0_xattn_ln_l_b, L0_xattn_Wq, L0_xattn_Wkv, L0_xattn_Wout, L0_ffn_w_gate, L0_ffn_w_in, L0_ffn_w_out, L1_xattn_q_w, L1_xattn_k_w, L1_xattn_norm_w, L1_xattn_gate_w, L1_xattn_gate_b, L1_ffn_router_w, L1_ffn_router_b, L1_ffn_w1, L1_ffn_b1, L1_ffn_w2, L1_ffn_b2, L1_ffn_ln_w, L1_ffn_ln_b):
    import jax
    import jax.numpy as jnp

    def _L0_xattn_ref(x, latents, ln_m_g, ln_m_b, ln_l_g, ln_l_b, Wq, Wkv, Wout):
        import jax, jax.numpy as jnp
        import numpy as np
        EPS = 1e-05

        def layer_norm(x, g, b):
            mu = jnp.mean(x, axis=-1, keepdims=True)
            var = jnp.var(x, axis=-1, keepdims=True)
            return (x - mu) * jax.lax.rsqrt(var + EPS) * g + b
        heads, dim_head = (16, 64)
        scale = dim_head ** (-0.5)
        x = layer_norm(x, ln_m_g, ln_m_b)
        lat = layer_norm(latents, ln_l_g, ln_l_b)
        b, m, _ = lat.shape
        q = lat @ Wq
        kv_input = jnp.concatenate([x, lat], axis=1)
        kv = kv_input @ Wkv
        k, v = jnp.split(kv, 2, axis=-1)

        def split_heads(t):
            return t.reshape(t.shape[0], t.shape[1], heads, dim_head).transpose(0, 2, 1, 3)
        q, k, v = (split_heads(q), split_heads(k), split_heads(v))
        dots = jnp.einsum('bhid,bhjd->bhij', q, k) * scale
        attn = jax.nn.softmax(dots, axis=-1)
        out = jnp.einsum('bhij,bhjd->bhid', attn, v)
        out = out.transpose(0, 2, 1, 3).reshape(b, m, heads * dim_head)
        return out @ Wout

    def _L0_ffn_ref(x, w_gate, w_in, w_out):
        import jax, jax.numpy as jnp
        import numpy as np
        D_MODEL = 128
        HIDDEN = 512
        NUM_EXPERTS = 8
        TOP_K = 2
        B, S, D = x.shape
        E = w_in.shape[0]
        xt = x.reshape(-1, D)
        logits = (xt @ w_gate.T).astype(jnp.float32)
        top_logits, top_idx = jax.lax.top_k(logits, TOP_K)
        top_gates = jax.nn.softmax(top_logits, axis=-1).astype(x.dtype)
        gates = (jax.nn.one_hot(top_idx, E, dtype=x.dtype) * top_gates[..., None]).sum(axis=1)
        y = jnp.zeros_like(xt)
        for e in range(E):
            h = xt @ w_in[e].T
            y = y + gates[:, e:e + 1] * (h @ w_out[e].T)
        return y.reshape(B, S, D)

    def _L1_xattn_ref(hidden_states, memory_state, q_w, k_w, norm_w, gate_w, gate_b):
        import jax, jax.numpy as jnp
        import numpy as np
        EPS = 1e-06

        def _rmsnorm(x, w, eps=EPS):
            x32 = x.astype(jnp.float32)
            var = jnp.mean(x32 * x32, axis=-1, keepdims=True)
            return (x32 * jax.lax.rsqrt(var + eps)).astype(x.dtype) * w
        B, S, H = hidden_states.shape
        K = memory_state.shape[1]
        scale = 1.0 / np.sqrt(H)
        normed = _rmsnorm(hidden_states, norm_w)
        v_pool = jnp.concatenate([normed, memory_state], axis=1)
        q = jnp.einsum('bsh,oh->bso', normed, q_w)
        k = jnp.einsum('bth,oh->bto', v_pool, k_w)
        logits = jnp.einsum('bsd,btd->bst', q, k) * scale
        local = jnp.tril(jnp.ones((S, S), bool))
        mask = jnp.concatenate([local, jnp.ones((S, K), bool)], axis=1)
        logits = jnp.where(mask[None], logits, -jnp.inf)
        attn = jax.nn.softmax(logits, axis=-1)
        h_tilde = jnp.einsum('bst,bth->bsh', attn, v_pool)
        alpha = jax.nn.sigmoid(jnp.einsum('bsh,oh->bso', hidden_states, gate_w) + gate_b)
        return (1.0 - alpha) * hidden_states + alpha * h_tilde

    def _L1_ffn_ref(hidden_states, router_w, router_b, w1, b1, w2, b2, ln_w, ln_b):
        import jax, jax.numpy as jnp
        import numpy as np
        B, S, H = (8, 128, 128)
        FF = 512
        E = 8
        TOP_K = 2
        LN_EPS = 1e-12

        def _layernorm(x, w, b):
            mu = jnp.mean(x, axis=-1, keepdims=True)
            var = jnp.mean(jnp.square(x - mu), axis=-1, keepdims=True)
            return (x - mu) * jax.lax.rsqrt(var + LN_EPS) * w + b
        b, s, h = hidden_states.shape
        flat = hidden_states.reshape(-1, h)
        logits = flat @ router_w.T + router_b
        topk_vals, topk_idx = jax.lax.top_k(logits, TOP_K)
        topk_w = jax.nn.softmax(topk_vals, axis=-1)
        out = jnp.zeros_like(flat)
        n_exp = w1.shape[0]
        for e in range(n_exp):
            cw = jnp.sum(jnp.where(topk_idx == e, topk_w, 0.0), axis=-1)
            y = jax.nn.gelu(flat @ w1[e].T + b1[e], approximate=False)
            y = y @ w2[e].T + b2[e]
            out = out + y * cw[:, None]
        out = out.reshape(b, s, h) + hidden_states
        return _layernorm(out, ln_w, ln_b)
    x = x + _L0_xattn_ref(ctx_1024, _layernorm(x, axis=-1), L0_xattn_ln_m_g, L0_xattn_ln_m_b, L0_xattn_ln_l_g, L0_xattn_ln_l_b, L0_xattn_Wq, L0_xattn_Wkv, L0_xattn_Wout)
    x = x + _L0_ffn_ref(_layernorm(x, axis=-1), L0_ffn_w_gate, L0_ffn_w_in, L0_ffn_w_out)
    x = x + _L1_xattn_ref(_layernorm(x, axis=-1), ctx_1024, L1_xattn_q_w, L1_xattn_k_w, L1_xattn_norm_w, L1_xattn_gate_w, L1_xattn_gate_b)
    x = x + _L1_ffn_ref(_layernorm(x, axis=-1), L1_ffn_router_w, L1_ffn_router_b, L1_ffn_w1, L1_ffn_b1, L1_ffn_w2, L1_ffn_b2, L1_ffn_ln_w, L1_ffn_ln_b)
    return x

_drawn_inputs = setup_inputs


def setup_inputs(seed=0):
    import zlib

    import numpy as np

    out = dict(_drawn_inputs(seed))
    spreads = {'L0_xattn_ln_m_g': (1.0, 0.2),
     'L0_xattn_ln_m_b': (0.0, 0.1),
     'L0_xattn_ln_l_g': (1.0, 0.2),
     'L0_xattn_ln_l_b': (0.0, 0.1),
     'L1_xattn_norm_w': (1.0, 0.6),
     'L1_xattn_gate_b': (0.0, 0.46),
     'L1_ffn_router_b': (0.0, 0.1),
     'L1_ffn_ln_w': (1.0, 0.2),
     'L1_ffn_ln_b': (0.0, 0.1)}
    factors = {'L0_ffn_w_gate': 8.0,
     'L0_ffn_w_in': 8.0,
     'L0_ffn_w_out': 8.0,
     'L1_ffn_b1': 36.694,
     'L1_ffn_b2': 24.392}
    for name, (base, spread) in spreads.items():
        noise = np.random.default_rng([zlib.crc32(name.encode()), seed]).standard_normal(out[name].shape)
        drawn = base * np.exp(spread * noise) if base else spread * noise
        out[name] = jnp.asarray(drawn.astype(out[name].dtype))
    for name, factor in factors.items():
        out[name] = (out[name] * factor).astype(out[name].dtype)
    return out
```

```python
import concourse.bass as bass
from concourse import mybir
from contextlib import ExitStack

B, SQ, SC, D = 4, 256, 512, 128
P = 128
NT = B * SQ // P
CT = SC // P
QT = SQ // P
KT = CT + QT
NK = KT * P
HEADS, DH = 16, 64
NPAIR = HEADS // 2
ITEMS = HEADS * B
E, TOPK, FF = 8, 2, 512
FT = FF // P
LN_EPS = 1e-5
RMS_EPS = 1e-6
LN2_EPS = 1e-12
HEAD_SCALE = DH ** -0.5
SCALE1 = D ** -0.5
MASKED = -1e30


def transformer_program(nc, A, out):
    F32, F16, U32 = mybir.dt.float32, mybir.dt.float16, mybir.dt.uint32
    ALU = mybir.AluOpType
    ACT = mybir.ActivationFunctionType
    AX = mybir.AxisListType

    ctx = ExitStack()
    with ctx:
        def sb(name, shape, dt=F32):
            return ctx.enter_context(nc.sbuf_tensor(name, shape, dt))

        def sem(name):
            return ctx.enter_context(nc.semaphore(name))

        def at(start, size):
            return bass.ds(start, size)

        ident = sb("ident", [P, P])
        causal = sb("causal", [P, QT, SQ])
        minus_half = sb("minus_half", [P, B * KT])
        iota_e = sb("iota_e", [P, NT, E])
        x_cur = sb("x_cur", [P, NT, D])
        ctx_sb = sb("ctx_sb", [P, B, CT, D])
        ln_rows = sb("ln_rows", [P, 4, D])
        kvf = sb("kvf", [P, B, KT, D])
        kv = sb("kv", [P, 4, B * NK], F16)
        kvh, kvl = (kv[:, i, :].rearrange("p (b i d) -> p b i d", b=B, i=KT) for i in range(2))
        kth, ktl = (kv[:, i, :].rearrange("p (b n) -> p b n", b=B) for i in (2, 3))
        w0 = sb("w0", [P, 4 * HEADS * DH])
        wq_sb = w0[:, 0:HEADS * DH]
        wkv_sb = w0[:, HEADS * DH:3 * HEADS * DH]
        wout_sb = w0[:, 3 * HEADS * DH:4 * HEADS * DH].rearrange("p (a d) -> p a d", a=NPAIR)
        wqkvT = sb("wqkvT", [P, 2, 3, P])
        ab_all = sb("ab_all", [P, HEADS, 4, P], F16)
        ab = sb("ab", [P, 2, 4, P], F16)
        qkh = sb("qkh", [P, 2, SQ], F16)
        qkl = sb("qkl", [P, 2, SQ], F16)
        probs = sb("probs", [P, 2, NK])
        pth = sb("pth", [P, 2, KT, SQ], F16)
        ptl = sb("ptl", [P, 2, KT, SQ], F16)
        yh = sb("yh", [P, 2, SQ], F16)
        yl = sb("yl", [P, 2, SQ], F16)
        neg_max = sb("neg_max", [P, 2])
        den = sb("den", [P, 2 * E, 1])
        rden = sb("rden", [P, 2 * E, 1])
        stats = sb("stats", [P, B * KT, 6])
        mv = sb("mv", [P, B * KT, 2])
        var_e = sb("var_e", [P, B * KT])
        rstd = sb("rstd", [P, B * KT])
        rstd2 = sb("rstd2", [P, NT])
        tmp8 = sb("tmp8", [P, NT])
        w_in_sb = sb("w_in_sb", [P, E, FT, D])
        w_out_sb = w0[:, :].rearrange("p (e f) -> p e f", e=E)
        woT = sb("woT", [P, 2, FT, D])
        moe0 = sb("moe0", [P, E, D])
        small = sb("small", [E, 3 * D])
        wgT = sb("wgT", [P, 2, E])
        b1n = sb("b1n", [E * FT, P])
        b1T = sb("b1T", [P, E * FT])
        b1c = sb("b1c", [P, 2, FT])
        xn = sb("xn", [P, NT, D])
        xT = sb("xT", [P, NT * P])
        logits = sb("logits", [P, NT, E])
        top8 = sb("top8", [P, NT, 8])
        idx8 = sb("idx8", [P, NT, 8], U32)
        idxf = sb("idxf", [P, NT, 8])
        g12 = sb("g12", [P, 3, NT])
        hit = sb("hit", [P, 2, NT, E])
        gates = sb("gates", [P, NT, E])
        rows1 = sb("rows1", [P, 4, D])
        rb_row = sb("rb_row", [P, E])
        qk1w = sb("qk1w", [P, 3, D])
        A1 = sb("A1", [P, D])
        gwT = sb("gwT", [P, D])
        kv32 = kv[:, :, :].rearrange("p a n -> p (a n)").bitcast(F32)
        ctxT = kv32[:, 0:B * SC].rearrange("p (b n) -> p b n", b=B)
        normT, q1T = (kv32[:, B * SC + i * NT * P:B * SC + (i + 1) * NT * P] for i in range(2))
        normed, alpha = (kv32[:, B * SC + i * NT * P:B * SC + (i + 1) * NT * P].rearrange("p (t d) -> p t d", t=NT)
                         for i in (2, 3))
        pt1 = sb("pt1", [P, 2, KT, P])
        w1n = sb("w1n", [P, 2, FT, D])
        w2n = sb("w2n", [P, 2, FF])
        w1Th = sb("w1Th", [P, 2, FF], F16)
        w1Tl = sb("w1Tl", [P, 2, FF], F16)
        w2Th = sb("w2Th", [P, 2, FT * D], F16)
        w2Tl = sb("w2Tl", [P, 2, FT * D], F16)
        xTh = sb("xTh", [P, NT * P], F16)
        xTl = sb("xTl", [P, NT * P], F16)
        hf = sb("hf", [P, 2, 512])
        hh, hl = (ab_all[:, 8 * i:8 * i + 8, :, :].rearrange("p (c f) a n -> p c f (a n)", c=2) for i in range(2))
        gT = sb("gT", [E, NT * P])
        acc4 = sb("acc4", [P, NT, D])

        ps = ctx.enter_context(nc.psum_tensor("ps", [P, 8, 512], F32))

        def bank(i, lo=0, hi=512):
            return ps[:, i, lo:hi]

        S_PS = [ps[:, 0:2, :].rearrange("p a n -> p (a n)"), ps[:, 2:4, :].rearrange("p a n -> p (a n)")]
        PT_PS = ps[:, 4:6, :].rearrange("p a n -> p (a n)")
        AB_PS = [ps[:, 2 + 2 * i:4 + 2 * i, 0:2 * P].rearrange("p h (a n) -> p h a n", a=2) for i in range(2)]
        Y_PS = bank(6, 0, SQ)
        QK_PS = bank(7, 0, SQ)
        O_PS = bank(7, SQ, 512)

        d_x, d_wq, d_wkv, d_wout, d_ln = (sem(n) for n in ("d_x", "d_wq", "d_wkv", "d_wout", "d_ln"))
        d_ctx = [sem(f"d_ctx{b}") for b in range(B)]
        d_win, d_wo0, d_small, d_rows1, d_qk1w = (sem(n) for n in ("d_win", "d_wo0", "d_small", "d_rows1", "d_qk1w"))
        d_w1 = [sem("d_w1a"), sem("d_w1b")]
        d_w2 = [sem("d_w2a"), sem("d_w2b")]
        d_out = sem("d_out")
        s_const, s_v, s_xcur = sem("s_const"), sem("s_v"), sem("s_xcur")
        s_ve, s_r1, s_we, s_r2, s_xhat = (sem(n) for n in ("s_ve", "s_r1", "s_we", "s_r2", "s_xhat"))
        s_gm, s_aff, s_kvh, s_kvl = (sem(n) for n in ("s_gm", "s_aff", "s_kvh", "s_kvl"))
        s_wT_mm, s_wT, s_ab_mm, s_abh, s_abl = (sem(n) for n in ("s_wT_mm", "s_wT", "s_ab_mm", "s_abh", "s_abl"))
        s_kt_mm, s_kth, s_ktl = (sem(n) for n in ("s_kt_mm", "s_kth", "s_ktl"))
        s_ab, s_qk, s_qkh, s_qkl = (sem(n) for n in ("s_ab", "s_qk", "s_qkh", "s_qkl"))
        s_S, s_max, s_exp, s_T, s_pth, s_ptl = (sem(n) for n in ("s_S", "s_max", "s_exp", "s_T", "s_pth", "s_ptl"))
        s_Y, s_yh, s_yl, s_O, s_rden, s_acc = (sem(n) for n in ("s_Y", "s_yh", "s_yl", "s_O", "s_rden", "s_acc"))

        def load(eng, dst, src, s):
            eng.dma_start(dst, src).then_inc(s, 16)

        ctx_v = A["ctx_1024"].rearrange("b (i p) d -> p b i d", p=P)
        w1_v = A["L1_ffn_w1"].rearrange("e (t p) d -> p e t d", p=P)
        w2_v = A["L1_ffn_w2"].rearrange("e p f -> p e f")

        e0_wT, e0_m, e0_mc = (sem(n) for n in ("e0_wT", "e0_m", "e0_mc"))
        e0_wTc = [sem("e0_wTc_dve"), sem("e0_wTc_act")]
        c1_mm, c1_c = sem("c1_mm"), sem("c1_c")
        n_ve, n_r, n_xn, n_T, n_Tc = (sem(n) for n in ("n_ve", "n_r", "n_xn", "n_T", "n_Tc"))
        g_mm, g_d, g_e, g_ok = (sem(n) for n in ("g_mm", "g_d", "g_e", "g_ok"))
        f0_mm, f0_c = sem("f0_mm"), sem("f0_c")
        l1_ve, l1_r, l1_we, l1_r2, l1_hid, l1_nrm = (sem(n) for n in ("l1_ve", "l1_r", "l1_we", "l1_r2", "l1_hid", "l1_nrm"))
        l1_T, l1_Tc, l1_z, l1_zb, l1_al, l1_q, l1_qc = (sem(n) for n in ("l1_T", "l1_Tc", "l1_z", "l1_zb", "l1_al", "l1_q", "l1_qc"))
        a_S, a_max, a_exp, a_T, a_Tc, a_O, a_fin = (sem(n) for n in ("a_S", "a_max", "a_exp", "a_T", "a_Tc", "a_O", "a_fin"))
        f1_wT, f1_wh, f1_wl, f1_U, f1_gelu, f1_hh, f1_hl, f1_V, f1_acc = (
            sem(n) for n in ("f1_wT", "f1_wh", "f1_wl", "f1_U", "f1_gelu", "f1_hh", "f1_hl", "f1_V", "f1_acc"))
        f1_gT, f1_gTc, f1_b2, f1_b2c, f1_xh, f1_xl = (sem(n) for n in ("f1_gT", "f1_gTc", "f1_b2", "f1_b2c", "f1_xh", "f1_xl"))
        f1_b1 = sem("f1_b1")
        z_fin = sem("z_fin")

        block = ctx.enter_context(nc.Block())

        @block.sync
        def _(sp):
            load(sp, wq_sb[:, :], A["L0_xattn_Wq"], d_wq)
            load(sp, wkv_sb[:, :], A["L0_xattn_Wkv"], d_wkv)
            load(sp, wout_sb[:, :, :], A["L0_xattn_Wout"].rearrange("(a p) d -> p a d", p=P), d_wout)
            load(sp, w_in_sb[:, :, :, :], A["L0_ffn_w_in"].rearrange("e (t p) d -> p e t d", p=P), d_win)
            sp.wait_ge(s_ab_mm, NPAIR)
            load(sp, w_out_sb[:, :, :], A["L0_ffn_w_out"].rearrange("e p f -> p e f"), d_wo0)
            load(sp, qk1w[:, 0, :], A["L1_xattn_q_w"], d_qk1w)
            load(sp, qk1w[:, 1, :], A["L1_xattn_k_w"], d_qk1w)
            load(sp, qk1w[:, 2, :], A["L1_xattn_gate_w"], d_qk1w)
            for e in range(2):
                load(sp, w1n[:, e, :, :], w1_v[:, e, :, :], d_w1[e])
                load(sp, w2n[:, e, :], w2_v[:, e, :], d_w2[e])
            with sp.Fori(1, E // 2) as i:
                for e in range(2):
                    sp.wait_ge(f1_wT, i * 4 + (2 * e - 2))
                    load(sp, w1n[:, e, :, :], w1_v[:, at(i * 2 + e, 1), :, :].rearrange("p a t d -> p (a t) d"), d_w1[e])
                    load(sp, w2n[:, e, :], w2_v[:, at(i * 2 + e, 1), :].rearrange("p a f -> p (a f)"), d_w2[e])
            out_v = out.rearrange("b (j p) d -> p (b j) d", p=P)
            for c in range(2):
                sp.wait_ge(z_fin, c + 1)
                load(sp, out_v[:, 4 * c:4 * c + 4, :], acc4[:, 4 * c:4 * c + 4, :], d_out)
            sp.wait_ge(d_out, 32)

        @block.gpsimd
        def _(pool):
            pool.memset(ident[:, :], 0.0).then_inc(s_const, 1)
            pool.memset(causal[:, :, :], 0.0).then_inc(s_const, 1)
            pool.wait_ge(s_const, 2)
            pool.affine_select(out=ident[:, :], in_=ident[:, :], compare_op=ALU.not_equal, fill=1.0, base=0,
                               pattern=[[-1, P]], channel_multiplier=1).then_inc(s_const, 1)
            pool.affine_select(out=causal[:, :, :], in_=causal[:, :, :], compare_op=ALU.is_ge, fill=MASKED, base=0,
                               pattern=[[P, QT], [-1, SQ]], channel_multiplier=1).then_inc(s_const, 1)
            pool.memset(minus_half[:, :], -0.5).then_inc(s_const, 1)
            pool.iota(iota_e[:, :, :], pattern=[[0, NT], [1, E]], base=0, channel_multiplier=0,
                      allow_small_or_imprecise_dtypes=True).then_inc(s_const, 1)
            pool.wait_ge(s_const, 5)
            pool.wait_ge(s_ve, 1)
            pool.tensor_tensor(rstd[:, :], var_e[:, :], minus_half[:, :], ALU.pow).then_inc(s_r1, 1)
            pool.wait_ge(s_we, 1)
            pool.tensor_tensor(rstd2[:, :], tmp8[:, :], minus_half[:, 0:NT], ALU.pow).then_inc(s_r2, 1)
            pool.wait_ge(d_ln, 64)
            for b in range(B):
                pool.wait_ge(s_xhat, b + 1)
                for k, (lo, hi) in enumerate(((0, CT), (CT, KT))):
                    v = kvf[:, b, lo:hi, :]
                    g = ln_rows[:, 2 * k, :].unsqueeze(1).broadcast_to([P, hi - lo, D])
                    pool.tensor_tensor(v, v, g, ALU.mult).then_inc(s_gm, 1)
                pool.wait_ge(s_gm, 2 * b + 2)
                for k, (lo, hi) in enumerate(((0, CT), (CT, KT))):
                    v = kvf[:, b, lo:hi, :]
                    h = ln_rows[:, 2 * k + 1, :].unsqueeze(1).broadcast_to([P, hi - lo, D])
                    pool.tensor_tensor(v, v, h, ALU.add).then_inc(s_aff, 1)
            for h in range(HEADS):
                if h % 2 == 0:
                    pool.wait_ge(s_abh, h // 2 + 1)
                    pool.wait_ge(s_abl, h // 2 + 1)
                if h >= 2:
                    pool.wait_ge(s_O, B * (h - 1))
                pool.tensor_copy(ab[:, h % 2, :, :].bitcast(U32), ab_all[:, h, :, :].bitcast(U32)).then_inc(s_ab, 1)
            pool.wait_ge(n_ve, 1)
            pool.tensor_tensor(rstd[:, 0:NT], var_e[:, 0:NT], minus_half[:, 0:NT], ALU.pow).then_inc(n_r, 1)
            pool.wait_ge(l1_ve, 1)
            pool.tensor_tensor(rstd[:, 0:NT], var_e[:, 0:NT], minus_half[:, 0:NT], ALU.pow).then_inc(l1_r, 1)
            pool.wait_ge(l1_we, 1)
            pool.tensor_tensor(rstd2[:, :], tmp8[:, :], minus_half[:, 0:NT], ALU.pow).then_inc(l1_r2, 1)
            for k in (2, 3):
                pool.wait_ge(n_ve, k)
                pool.tensor_tensor(rstd[:, 0:NT], var_e[:, 0:NT], minus_half[:, 0:NT], ALU.pow).then_inc(n_r, 1)




        @block.scalar
        def _(act):
            for b in range(B):
                load(act, ctx_sb[:, b, :, :], ctx_v[:, b, :, :], d_ctx[b])
            load(act, x_cur[:, :, :], A["x"].rearrange("b (j p) d -> p (b j) d", p=P), d_x)
            for i, name in enumerate(("ln_m_g", "ln_m_b", "ln_l_g", "ln_l_b")):
                load(act, ln_rows[:, i, :], A["L0_xattn_" + name].partition_broadcast(P), d_ln)
            for i, name in enumerate(("L0_ffn_w_gate", "L1_ffn_router_w", "L1_ffn_b2")):
                load(act, small[:, i * D:(i + 1) * D], A[name], d_small)
            load(act, b1n[:, :], A["L1_ffn_b1"].rearrange("e (t p) -> (e t) p", p=P), d_small)
            for i, name in enumerate(("L1_xattn_norm_w", "L1_xattn_gate_b", "L1_ffn_ln_w", "L1_ffn_ln_b")):
                load(act, rows1[:, i, :], A[name].partition_broadcast(P), d_rows1)
            load(act, rb_row[:, :], A["L1_ffn_router_b"].partition_broadcast(P), d_rows1)

            for p in range(NPAIR):
                act.wait_ge(s_wT_mm, p + 1)
                if p >= 2:
                    act.wait_ge(s_ab_mm, p - 1)
                nc.scalar.copy(wqkvT[:, p % 2, :, :], bank(p % 2, 0, 384).rearrange("p (a n) -> p a n", a=3)).then_inc(s_wT, 1)
                act.wait_ge(s_ab_mm, p + 1)
                nc.scalar.copy(ab_all[:, 2 * p:2 * p + 2, 0::2, :],
                               AB_PS[p % 2]).then_inc(s_abh, 1)
            for b in range(B):
                act.wait_ge(s_aff, 2 * b + 2)
                nc.scalar.copy(kvh[:, b, :, :], kvf[:, b, :, :]).then_inc(s_kvh, 1)
                for k, (lo, hi) in enumerate(((0, 512), (512, NK))):
                    act.wait_ge(s_kt_mm, 2 * b + k + 1)
                    nc.scalar.copy(kth[:, b, lo:hi], bank(4 + k, 0, hi - lo)).then_inc(s_kth, 1)

            def hi_part(n, prev, j):
                act.wait_ge(s_T, n * 2 + (j + 1))
                nc.scalar.copy(pth[:, prev % 2, :, at(j * P, P)],
                               PT_PS[:, 0:NK].rearrange("p (i q) -> p i q", i=KT)).then_inc(s_pth, 1)

            def exponentials(n, k, j, first):
                act.wait_ge(s_max, n * 2 + (j + 1))
                if not first:
                    act.wait_ge(s_T, n * 2 + (j - 1))
                nc.scalar.activation(probs[:, j, :], S_PS[j][:, 0:NK], ACT.Exp, bias=neg_max[:, j:j + 1],
                                     accum_out=den[:, 2 * (k % 8) + j, :]).then_inc(s_exp, 1)

            def act_item(n, k, first=0, last=False):
                if first >= 1 or first is False:
                    pass
                have1, have2 = not (first == 1), first not in (1, 2)
                if have1:
                    hi_part(n - 1, k - 1, 1)
                exponentials(n, k, 0, not have1)
                if have2:
                    act.wait_ge(s_Y, n - 1)
                    nc.scalar.copy(yh[:, k % 2, :], Y_PS).then_inc(s_yh, 1)
                if not last:
                    act.wait_ge(s_qk, n + 2)
                    nc.scalar.activation(qkh[:, (k + 1) % 2, :], QK_PS, ACT.Copy, scale=HEAD_SCALE).then_inc(s_qkh, 1)
                hi_part(n, k, 0)
                exponentials(n, k, 1, not have1)

            act.wait_ge(s_qk, 1)
            nc.scalar.activation(qkh[:, 0, :], QK_PS, ACT.Copy, scale=HEAD_SCALE).then_inc(s_qkh, 1)
            for k in range(8):
                act_item(k, k, first=min(k + 1, 3))
            with act.Fori(1, ITEMS // 8 - 1) as p:
                for k in range(8):
                    act_item(p * 8 + k, k)
            for k in range(8):
                act_item(ITEMS - 8 + k, k, last=k == 7)
            hi_part(ITEMS - 1, 7, 1)
            for n in (ITEMS - 2, ITEMS - 1):
                act.wait_ge(s_Y, n + 1)
                nc.scalar.copy(yh[:, n % 2, :], Y_PS).then_inc(s_yh, 1)

            for e in range(1, E, 2):
                act.wait_ge(e0_wT, e + 1)
                if e >= 3:
                    act.wait_ge(e0_m, e - 1)
                nc.scalar.copy(woT[:, 1, :, :], bank(1).rearrange("p (t n) -> p t n", t=FT)).then_inc(e0_wTc[1], 1)
            for c in range(2):
                act.wait_ge(e0_m, 4 * c + 4)
                nc.scalar.copy(moe0[:, 4 * c:4 * c + 4, :], bank(2 + c).rearrange("p (e n) -> p e n", e=4)).then_inc(e0_mc, 1)
            for b in range(B):
                act.wait_ge(c1_mm, b + 1)
                nc.scalar.copy(ctxT[:, b, :], bank(4 + b % 2)).then_inc(c1_c, 1)
            act.wait_ge(c1_mm, B + 1)
            nc.scalar.copy(wgT[:, :, :], bank(6, 0, 2 * E).rearrange("p (a n) -> p a n", a=2)).then_inc(c1_c, 1)
            nc.scalar.copy(b1T[:, :], bank(6, 16, 16 + E * FT)).then_inc(c1_c, 1)
            nc.scalar.copy(gwT[:, :], bank(6, 128, 256)).then_inc(c1_c, 1)
            nc.scalar.copy(A1[:, :], bank(6, 256, 384)).then_inc(c1_c, 1)

            def norm_T(k, dst):
                for c in range(2):
                    act.wait_ge(n_T, 2 * k + c + 1)
                    nc.scalar.copy(dst[:, 512 * c:512 * c + 512], bank(c)).then_inc(n_Tc, 1)

            def gate_exp(k):
                act.wait_ge(g_d, k + 1)
                nc.scalar.activation(g12[:, 2, :], g12[:, 0, :], ACT.Exp).then_inc(g_e, 1)

            norm_T(0, xT)
            gate_exp(0)

            for c in range(4):
                act.wait_ge(l1_T, c + 1)
                dst = xT if c < 2 else normT
                nc.scalar.copy(dst[:, 512 * (c % 2):512 * (c % 2) + 512], bank(c % 2)).then_inc(l1_Tc, 1)
            for c in range(2):
                act.wait_ge(l1_q, c + 1)
                nc.scalar.activation(q1T[:, 512 * c:512 * c + 512], bank(4 + c), ACT.Copy, scale=SCALE1).then_inc(l1_qc, 1)
            act.wait_ge(l1_zb, 2)
            nc.scalar.activation(alpha[:, :, :], alpha[:, :, :], ACT.Tanh, scale=0.5).then_inc(l1_al, 1)
            for u in range(NT):
                act.wait_ge(a_max, u + 1)
                if u >= 2:
                    act.wait_ge(a_T, u - 1)
                nc.scalar.activation(probs[:, u % 2, :], S_PS[u % 2][:, 0:NK], ACT.Exp, bias=neg_max[:, u % 2:u % 2 + 1],
                                     accum_out=den[:, u, :]).then_inc(a_exp, 1)
                act.wait_ge(a_T, u + 1)
                if u >= 2:
                    act.wait_ge(a_O, u - 1)
                nc.scalar.copy(pt1[:, u % 2, :, :], PT_PS[:, 0:NK].rearrange("p (i q) -> p i q", i=KT)).then_inc(a_Tc, 1)

            norm_T(1, xT)
            for c in range(2):
                nc.scalar.wait_ge(n_Tc, 3 + c)
                nc.scalar.copy(xTh[:, 512 * c:512 * c + 512], xT[:, 512 * c:512 * c + 512]).then_inc(f1_xh, 1)
            gate_exp(1)
            for c in range(2):
                act.wait_ge(f1_gT, c + 1)
                nc.scalar.copy(gT[:, 512 * c:512 * c + 512], ps[0:E, c, :]).then_inc(f1_gTc, 1)

            def act_expert(e, s, i):
                nc.scalar.copy(b1c[:, s, :], b1T[:, at(e * FT, FT)]).then_inc(f1_b1, 1)
                for w, dst in enumerate((w1Th, w2Th)):
                    act.wait_ge(f1_wT, e * 2 + (w + 1))
                    nc.scalar.copy(dst[:, s, :], bank(w)).then_inc(f1_wh, 1)
                act.wait_ge(f1_b1, e + 1)
                for c in range(2):
                    for f in range(FT):
                        m = e * 8 + (4 * c + f)
                        act.wait_ge(f1_U, m + 1)
                        if i or s or c or f >= 2:
                            act.wait_ge(f1_hl, m - 1)
                        nc.scalar.activation(hf[:, f % 2, :], bank(2 + f % 2), ACT.Gelu,
                                             bias=b1c[:, s, f:f + 1]).then_inc(f1_gelu, 1)

            for s in range(2):
                act_expert(s, s, 0)
            with act.Fori(1, E // 2) as i:
                for s in range(2):
                    act_expert(i * 2 + s, s, 1)

        @block.vector
        def _(dve):
            chain = [0]

            def link(ins):
                chain[0] += 1
                ins.then_inc(s_v, 1)
                dve.wait_ge(s_v, chain[0])

            def tile_stats(src, i):
                nc.vector.bn_stats(stats[:, i, :], src).then_inc(s_v, 1)
                chain[0] += 1

            def aggregate(count):
                dve.wait_ge(s_v, chain[0])
                for i in range(count):
                    nc.vector.bn_aggr(mv[:, i, :], stats[:, i, :]).then_inc(s_v, 1)
                    chain[0] += 1
                dve.wait_ge(s_v, chain[0])

            for b in range(B):
                dve.wait_ge(d_ctx[b], 16)
                for i in range(CT):
                    tile_stats(ctx_sb[:, b, i, :], b * KT + i)
            dve.wait_ge(d_x, 16)
            for b in range(B):
                for j in range(QT):
                    tile_stats(x_cur[:, QT * b + j, :], b * KT + CT + j)
            aggregate(B * KT)
            nc.vector.tensor_scalar(var_e[:, :], mv[:, :, 1], LN_EPS, None, ALU.add).then_inc(s_ve, 1)
            dve.wait_ge(s_r1, 1)
            r4 = rstd[:, :].rearrange("p (b i) -> p b i", b=B)[:, :, CT:KT]
            v4 = mv[:, :, 1].rearrange("p (b i) -> p b i", b=B)[:, :, CT:KT]
            t4 = tmp8[:, :].rearrange("p (b i) -> p b i", b=B)
            link(nc.vector.tensor_tensor(t4, v4, r4, ALU.mult))
            link(nc.vector.tensor_tensor(t4, t4, r4, ALU.mult))
            nc.vector.tensor_scalar(tmp8[:, :], tmp8[:, :], LN_EPS, None, ALU.add).then_inc(s_we, 1)
            dve.wait_ge(s_r2, 1)
            link(nc.vector.tensor_tensor(r4, r4, rstd2[:, :].rearrange("p (b i) -> p b i", b=B), ALU.mult))
            for b in range(B):
                for i in range(KT):
                    src = ctx_sb[:, b, i, :] if i < CT else x_cur[:, QT * b + i - CT, :]
                    k = b * KT + i
                    ins = nc.vector.tensor_scalar(kvf[:, b, i, :], src, mv[:, k, 0:1], rstd[:, k:k + 1],
                                                  ALU.subtract, ALU.mult)
                ins.then_inc(s_xhat, 1)
            for p in range(NPAIR):
                dve.wait_ge(s_abh, p + 1)
                nc.vector.tensor_tensor(ab_all[:, 2 * p:2 * p + 2, 1::2, :],
                                        AB_PS[p % 2],
                                        ab_all[:, 2 * p:2 * p + 2, 0::2, :], ALU.subtract).then_inc(s_abl, 1)
            for b in range(B):
                dve.wait_ge(s_kvh, b + 1)
                nc.vector.tensor_tensor(kvl[:, b, :, :], kvf[:, b, :, :], kvh[:, b, :, :], ALU.subtract).then_inc(s_kvl, 1)
                for k, (lo, hi) in enumerate(((0, 512), (512, NK))):
                    dve.wait_ge(s_kth, 2 * b + k + 1)
                    nc.vector.tensor_tensor(ktl[:, b, lo:hi], bank(4 + k, 0, hi - lo), kth[:, b, lo:hi],
                                            ALU.subtract).then_inc(s_ktl, 1)

            def maximum(n, j, first):
                dve.wait_ge(s_S, n * 2 + (j + 1))
                if not first:
                    dve.wait_ge(s_exp, n * 2 + (j - 1))
                nc.vector.tensor_reduce(neg_max[:, j:j + 1], S_PS[j][:, 0:NK], op=ALU.max, axis=AX.X,
                                        negate=True).then_inc(s_max, 1)

            def lo_part(n, prev, j):
                dve.wait_ge(s_pth, n * 2 + (j + 1))
                nc.vector.tensor_tensor(ptl[:, prev % 2, :, at(j * P, P)],
                                        PT_PS[:, 0:NK].rearrange("p (i q) -> p i q", i=KT),
                                        pth[:, prev % 2, :, at(j * P, P)], ALU.subtract).then_inc(s_ptl, 1)

            def y_lo(n, k):
                dve.wait_ge(s_yh, n + 1)
                nc.vector.tensor_tensor(yl[:, k % 2, :], Y_PS, yh[:, k % 2, :], ALU.subtract).then_inc(s_yl, 1)

            def qk_lo(n, k):
                dve.wait_ge(s_qkh, n + 1)
                nc.vector.scalar_tensor_tensor(qkl[:, k % 2, :], QK_PS, HEAD_SCALE, qkh[:, k % 2, :],
                                               ALU.mult, ALU.subtract).then_inc(s_qkl, 1)

            def accumulate(n, k):
                b = k % B
                dve.wait_ge(s_exp, n * 2 + 2)
                nc.vector.reciprocal(rden[:, 2 * (k % 8):2 * (k % 8) + 2, 0], den[:, 2 * (k % 8):2 * (k % 8) + 2, 0]).then_inc(s_rden, 1)
                dve.wait_ge(s_O, n + 1)
                dve.wait_ge(s_rden, n + 1)
                for j in range(QT):
                    if k >= B or not isinstance(n, int):
                        dve.wait_ge(s_acc, n * 2 + (j - 2 * B + 1))
                    t = x_cur[:, QT * b + j, :]
                    nc.vector.scalar_tensor_tensor(t, O_PS[:, j * P:(j + 1) * P], rden[:, 2 * (k % 8) + j, :], t,
                                                   ALU.mult, ALU.add).then_inc(s_acc, 1)

            def dve_item(n, k, first=0, last=False):
                have1, have2 = not (first == 1), first not in (1, 2)
                maximum(n, 0, not have1)
                if have1:
                    lo_part(n - 1, k - 1, 1)
                if have2:
                    y_lo(n - 2, k)
                if not last:
                    qk_lo(n + 1, k + 1)
                maximum(n, 1, not have1)
                lo_part(n, k, 0)
                if have2:
                    accumulate(n - 2, (k - 2) % 8)

            qk_lo(0, 0)
            for k in range(8):
                dve_item(k, k, first=min(k + 1, 3))
            with dve.Fori(1, ITEMS // 8 - 1) as p:
                for k in range(8):
                    dve_item(p * 8 + k, k)
            for k in range(8):
                dve_item(ITEMS - 8 + k, k, last=k == 7)
            lo_part(ITEMS - 1, 7, 1)
            for n in (ITEMS - 2, ITEMS - 1):
                y_lo(n, n)
                accumulate(n, n % 8 + 8 * (n >= 8))
            dve.wait_ge(s_acc, 2 * ITEMS)

            def norm_stats(src, eps, s):
                for t in range(NT):
                    tile_stats(src[:, t, :], t)
                aggregate(NT)
                nc.vector.tensor_scalar(var_e[:, 0:NT], mv[:, 0:NT, 1], eps, None, ALU.add).then_inc(s, 1)

            def norm_apply(dst, src, s, halves=True):
                for t in range(NT):
                    ins = nc.vector.tensor_scalar(dst[:, t, :], src[:, t, :], mv[:, t, 0:1], rstd[:, t:t + 1],
                                                  ALU.subtract, ALU.mult)
                    ins.then_inc(s, 1)

            def route(k, bias):
                dve.wait_ge(g_mm, k + 1)
                lg = bank(3, 0, NT * E).rearrange("p (t e) -> p t e", t=NT)
                if bias:
                    dve.wait_ge(d_rows1, 80)
                    link(nc.vector.tensor_tensor(logits[:, :, :], lg, rb_row[:, :].unsqueeze(1).broadcast_to([P, NT, E]), ALU.add))
                else:
                    link(nc.vector.tensor_copy(logits[:, :, :], lg))
                for t in range(NT):
                    ins = nc.vector.max(top8[:, t, :], logits[:, t, :])
                    ins.then_inc(s_v, 1)
                    chain[0] += 1
                dve.wait_ge(s_v, chain[0])
                nc.vector.tensor_tensor(g12[:, 0, :], top8[:, :, 1], top8[:, :, 0], ALU.subtract).then_inc(g_d, 1)
                for t in range(NT):
                    ins = nc.vector.max_index(idx8[:, t, :], top8[:, t, :], logits[:, t, :])
                    ins.then_inc(s_v, 1)
                    chain[0] += 1
                dve.wait_ge(s_v, chain[0])
                link(nc.vector.tensor_copy(idxf[:, :, :], idx8[:, :, :]))
                dve.wait_ge(g_e, k + 1)
                link(nc.vector.tensor_scalar(g12[:, 0, :], g12[:, 2, :], 1.0, None, ALU.add))
                link(nc.vector.reciprocal(g12[:, 0, :], g12[:, 0, :]))
                link(nc.vector.tensor_tensor(g12[:, 1, :], g12[:, 2, :], g12[:, 0, :], ALU.mult))
                for r in range(2):
                    link(nc.vector.tensor_tensor(hit[:, r, :, :], iota_e[:, :, :],
                                                 idxf[:, :, r:r + 1].broadcast_to([P, NT, E]), ALU.is_equal))
                    link(nc.vector.tensor_tensor(hit[:, r, :, :], hit[:, r, :, :],
                                                 g12[:, r, :].unsqueeze(2).broadcast_to([P, NT, E]), ALU.mult))
                link(nc.vector.tensor_tensor(gates[:, :, :], hit[:, 0, :, :], hit[:, 1, :, :], ALU.add))

            for e in range(0, E, 2):
                dve.wait_ge(e0_wT, e + 1)
                if e >= 2:
                    dve.wait_ge(e0_m, e - 1)
                nc.vector.tensor_copy(woT[:, 0, :, :], bank(0).rearrange("p (t n) -> p t n", t=FT)).then_inc(e0_wTc[0], 1)
            norm_stats(x_cur, LN_EPS, n_ve)
            dve.wait_ge(n_r, 1)
            norm_apply(xn, x_cur, n_xn)
            dve.wait_ge(s_const, 6)
            route(0, False)
            done = 0
            for t in range(NT):
                for c in range(2):
                    dve.wait_ge(f0_mm, 2 * t + c + 1)
                    for e in range(4):
                        ins = nc.vector.scalar_tensor_tensor(
                            x_cur[:, t, :], bank(4 + (2 * t + c) % 4, e * D, (e + 1) * D),
                            gates[:, t, 4 * c + e:4 * c + e + 1], x_cur[:, t, :], ALU.mult, ALU.add)
                        done += 1
                        ins.then_inc(f0_c, 1)
                        dve.wait_ge(f0_c, done)

            norm_stats(x_cur, LN_EPS, l1_ve)
            dve.wait_ge(l1_r, 1)
            link(nc.vector.tensor_tensor(tmp8[:, :], mv[:, 0:NT, 1], rstd[:, 0:NT], ALU.mult))
            link(nc.vector.tensor_tensor(tmp8[:, :], tmp8[:, :], rstd[:, 0:NT], ALU.mult))
            nc.vector.tensor_scalar(tmp8[:, :], tmp8[:, :], RMS_EPS, None, ALU.add).then_inc(l1_we, 1)
            norm_apply(xn, x_cur, l1_hid)
            dve.wait_ge(l1_r2, 1)
            dve.wait_ge(d_rows1, 80)
            dve.wait_ge(l1_hid, NT)
            for t in range(NT):
                nc.vector.scalar_tensor_tensor(normed[:, t, :], xn[:, t, :], rstd2[:, t:t + 1], rows1[:, 0, :],
                                               ALU.mult, ALU.mult).then_inc(l1_nrm, 1)
            for c in range(2):
                dve.wait_ge(l1_z, c + 1)
                nc.vector.tensor_tensor(alpha[:, 4 * c:4 * c + 4, :], bank(6 + c).rearrange("p (t n) -> p t n", t=4),
                                        rows1[:, 1, :].unsqueeze(1).broadcast_to([P, 4, D]), ALU.add).then_inc(l1_zb, 1)
            link(nc.vector.tensor_tensor(x_cur[:, :, :], x_cur[:, :, :], xn[:, :, :], ALU.add))
            dve.wait_ge(l1_al, 1)
            link(nc.vector.tensor_scalar(alpha[:, :, :], alpha[:, :, :], 0.5, 0.5, ALU.mult, ALU.add))

            def finish1(u):
                link(nc.vector.reciprocal(rden[:, u, :], den[:, u, :]))
                dve.wait_ge(a_O, u + 1)
                link(nc.vector.scalar_tensor_tensor(acc4[:, u, :], bank(6 + u % 2, 0, D), rden[:, u, :], xn[:, u, :],
                                                    ALU.mult, ALU.subtract))
                link(nc.vector.tensor_tensor(acc4[:, u, :], acc4[:, u, :], alpha[:, u, :], ALU.mult))
                link(nc.vector.tensor_tensor(x_cur[:, u, :], x_cur[:, u, :], acc4[:, u, :], ALU.add))
                nc.vector.tensor_copy(acc4[:, u, 0:1], x_cur[:, u, 0:1]).then_inc(a_fin, 1)

            for u in range(NT):
                dve.wait_ge(a_S, u + 1)
                if u >= 2:
                    dve.wait_ge(a_exp, u - 1)
                loc = S_PS[u % 2][:, SC:NK]
                link(nc.vector.tensor_tensor(loc, loc, causal[:, u % 2, :], ALU.add))
                nc.vector.tensor_reduce(neg_max[:, u % 2:u % 2 + 1], S_PS[u % 2][:, 0:NK], op=ALU.max, axis=AX.X,
                                        negate=True).then_inc(a_max, 1)
                if u >= 1:
                    dve.wait_ge(a_exp, u)
                    finish1(u - 1)
            dve.wait_ge(a_exp, NT)
            finish1(NT - 1)

            norm_stats(x_cur, LN_EPS, n_ve)
            dve.wait_ge(n_r, 2)
            norm_apply(xn, x_cur, n_xn)
            for c in range(2):
                dve.wait_ge(f1_xh, c + 1)
                nc.vector.tensor_tensor(xTl[:, 512 * c:512 * c + 512], xT[:, 512 * c:512 * c + 512],
                                        xTh[:, 512 * c:512 * c + 512], ALU.subtract).then_inc(f1_xl, 1)
            route(1, True)
            nc.vector.tensor_copy(tmp8[:, 0:1], gates[:, 0, 0:1]).then_inc(g_ok, 1)
            for c in range(2):
                dve.wait_ge(f1_b2, c + 1)
                nc.vector.tensor_tensor(acc4[:, 4 * c:4 * c + 4, :], bank(4 + c).rearrange("p (t n) -> p t n", t=4),
                                        xn[:, 4 * c:4 * c + 4, :], ALU.add).then_inc(f1_b2c, 1)
            dve.wait_ge(f1_b2c, 2)

            def low_weights(e, s):
                for w, (hi, lo) in enumerate(((w1Th, w1Tl), (w2Th, w2Tl))):
                    dve.wait_ge(f1_wh, e * 2 + (w + 1))
                    nc.vector.tensor_tensor(lo[:, s, :], bank(w), hi[:, s, :], ALU.subtract).then_inc(f1_wl, 1)

            def low_hidden(e, c, first):
                for f in range(FT):
                    m = e * 8 + (4 * c + f)
                    dve.wait_ge(f1_gelu, m + 1)
                    if not first:
                        dve.wait_ge(f1_V, e * 8 + (4 * c - 4))
                    nc.vector.tensor_copy(hh[:, c, f, :], hf[:, f % 2, :]).then_inc(f1_hh, 1)
                    dve.wait_ge(f1_hh, m + 1)
                    nc.vector.tensor_tensor(hl[:, c, f, :], hf[:, f % 2, :], hh[:, c, f, :], ALU.subtract).then_inc(f1_hl, 1)

            def add_expert(e, c, first):
                for q in range(4):
                    t = 4 * c + q
                    dve.wait_ge(f1_V, e * 8 + (t + 1))
                    if not first:
                        dve.wait_ge(f1_acc, e * 8 + (t - 7))
                    nc.vector.scalar_tensor_tensor(
                        acc4[:, t, :], bank(4 + t % 4, 0, D), gates[:, t, at(e, 1)], acc4[:, t, :],
                        ALU.mult, ALU.add).then_inc(f1_acc, 1)

            def dve_expert(e, s, i):
                low_weights(e, s)
                low_hidden(e, 0, i == 0 and s == 0)
                if i or s:
                    add_expert(e - 1, 1, i == 0 and s <= 1)
                low_hidden(e, 1, i == 0 and s == 0)
                add_expert(e, 0, i == 0 and s == 0)

            for s in range(2):
                dve_expert(s, s, 0)
            with dve.Fori(1, E // 2) as i:
                for s in range(2):
                    dve_expert(i * 2 + s, s, 1)
            add_expert(E - 1, 1, False)
            dve.wait_ge(f1_acc, E * NT)

            norm_stats(acc4, LN2_EPS, n_ve)
            dve.wait_ge(n_r, 3)
            norm_apply(acc4, acc4, n_xn)
            dve.wait_ge(n_xn, 3 * NT)
            for c in range(2):
                v = acc4[:, 4 * c:4 * c + 4, :]
                w, bias = (rows1[:, r, :].unsqueeze(1).broadcast_to([P, 4, D]) for r in (2, 3))
                link(nc.vector.tensor_tensor(v, v, w, ALU.mult))
                link(nc.vector.tensor_tensor(v, v, bias, ALU.add))
                nc.vector.tensor_tensor(v, v, x_cur[:, 4 * c:4 * c + 4, :], ALU.add).then_inc(z_fin, 1)

        @block.tensor
        def _(pe):
            mm = nc.tensor.matmul

            def transpose(dst, src):
                return nc.tensor.transpose(dst, src, ident[:, :])

            pe.wait_ge(s_const, 4)
            pe.wait_ge(d_wq, 16)
            pe.wait_ge(d_wkv, 16)
            pe.wait_ge(d_wout, 16)

            def weights_T(p):
                if p >= 2:
                    pe.wait_ge(s_wT, p - 1)
                c = p * P
                transpose(bank(p % 2, 0, 128), wq_sb[:, c:c + P])
                transpose(bank(p % 2, 128, 256), wkv_sb[:, c:c + P])
                transpose(bank(p % 2, 256, 384), wkv_sb[:, HEADS * DH + c:HEADS * DH + c + P]).then_inc(s_wT_mm, 1)

            def weights_AB(p):
                pe.wait_ge(s_wT, p + 1)
                if p >= 2:
                    pe.wait_ge(s_abl, p - 1)
                for h in range(2):
                    r = slice(DH * h, DH * h + DH)
                    wT = wqkvT[r, p % 2, :, :]
                    mm(AB_PS[p % 2][:, h, 0, :], wT[:, 0, :], wT[:, 1, :], start=True, stop=True)
                    last = mm(AB_PS[p % 2][:, h, 1, :], wT[:, 2, :], wout_sb[r, p, :],
                              start=True, stop=True)
                last.then_inc(s_ab_mm, 1)

            weights_T(0)
            for p in range(NPAIR):
                if p + 1 < NPAIR:
                    weights_T(p + 1)
                weights_AB(p)
            pe.wait_ge(s_abl, NPAIR)
            for b in range(B):
                pe.wait_ge(s_aff, 2 * b + 2)
                for k, (lo, hi) in enumerate(((0, CT), (CT, KT))):
                    if b >= 1:
                        pe.wait_ge(s_ktl, 2 * b + k - 1)
                    for i in range(lo, hi):
                        last = transpose(bank(4 + k, (i - lo) * P, (i - lo + 1) * P), kvf[:, b, i, :])
                    last.then_inc(s_kt_mm, 1)

            def queries(n, k):
                hs, b = (k // B) % 2, k % B
                if k % B == 0:
                    pe.wait_ge(s_ab, (n // B + 1) if isinstance(n, int) else head_count(n, k))
                lat = slice(SC, NK)
                mm(QK_PS, ab[:, hs, 0, :], kth[:, b, lat], start=True, stop=False)
                mm(QK_PS, ab[:, hs, 0, :], ktl[:, b, lat], start=False, stop=False)
                mm(QK_PS, ab[:, hs, 1, :], kth[:, b, lat], start=False, stop=True).then_inc(s_qk, 1)

            heads_before = [None]

            def head_count(n, k):
                return heads_before[0] + (k // B + 1)

            def scores(n, k, j, first):
                b = k % B
                if j == 0:
                    pe.wait_ge(s_qkh, n + 1)
                    pe.wait_ge(s_qkl, n + 1)
                if not first:
                    pe.wait_ge(s_exp, n * 2 + (j - 1))
                q = slice(j * P, j * P + P)
                for w, keys, start in ((qkh, kth, True), (qkh, ktl, False), (qkl, kth, False)):
                    for lo, hi in ((0, 512), (512, NK)):
                        last = mm(S_PS[j][:, lo:hi], w[:, k % 2, q], keys[:, b, lo:hi], start=start,
                                  stop=w is qkl, skip_group_check=True)
                last.then_inc(s_S, 1)

            def probs_T(n, j, first):
                pe.wait_ge(s_exp, n * 2 + (j + 1))
                if not first:
                    pe.wait_ge(s_ptl, n * 2 + j)
                for i in range(KT):
                    last = transpose(PT_PS[:, i * P:(i + 1) * P], probs[:, j, i * P:(i + 1) * P])
                last.then_inc(s_T, 1)

            def attend(n, k, half, first):
                b = k % B
                if half == 0:
                    pe.wait_ge(s_ptl, n * 2 + 2)
                    if not first:
                        pe.wait_ge(s_yl, n)
                for i in range(3 * half, 3 * half + 3):
                    mm(Y_PS, kvh[:, b, i, :], pth[:, k % 2, i, :], start=i == 0, stop=False, skip_group_check=True)
                    mm(Y_PS, kvh[:, b, i, :], ptl[:, k % 2, i, :], start=False, stop=False, skip_group_check=True)
                    last = mm(Y_PS, kvl[:, b, i, :], pth[:, k % 2, i, :], start=False, stop=i == KT - 1, skip_group_check=True)
                if half:
                    last.then_inc(s_Y, 1)

            def project(n, k, first=False):
                hs = (k // B) % 2
                pe.wait_ge(s_yl, n + 1)
                if not first:
                    pe.wait_ge(s_acc, n * 2)
                for j in range(QT):
                    o, q = O_PS[:, j * P:(j + 1) * P], slice(j * P, j * P + P)
                    mm(o, yh[:, k % 2, q], ab[:, hs, 2, :], start=True, stop=False)
                    mm(o, yh[:, k % 2, q], ab[:, hs, 3, :], start=False, stop=False)
                    last = mm(o, yl[:, k % 2, q], ab[:, hs, 2, :], start=False, stop=True)
                last.then_inc(s_O, 1)

            def pe_item(n, k, first=0, last=False):
                have1, have2 = not (first == 1), first not in (1, 2)
                scores(n, k, 0, not have1)
                if have1:
                    probs_T(n - 1, 1, False)
                if have2:
                    attend(n - 2, (k - 2) % 8, 1, False)
                if not last:
                    if have2 and not (isinstance(n, int) and n < 3):
                        pe.wait_ge(s_acc, n * 2 - 4)
                    queries(n + 1, k + 1)
                scores(n, k, 1, not have1)
                probs_T(n, 0, not have1)
                if have1:
                    attend(n - 1, (k - 1) % 8, 0, first == 2)
                if have2:
                    pe.wait_ge(s_qkl, n + 2 if not last else ITEMS)
                    project(n - 2, (k - 2) % 8, first == 3 and k == 2)

            for b in range(B):
                pe.wait_ge(s_ktl, 2 * b + 2)
                pe.wait_ge(s_kvl, b + 1)
            queries(0, 0)
            for k in range(8):
                pe_item(k, k, first=min(k + 1, 3))
            with pe.Fori(1, ITEMS // 8 - 1) as p:
                heads_before[0] = p * 2
                for k in range(8):
                    pe_item(p * 8 + k, k)
            for k in range(8):
                pe_item(ITEMS - 8 + k, k, last=k == 7)
            probs_T(ITEMS - 1, 1, False)
            attend(ITEMS - 2, 6, 1, False)
            attend(ITEMS - 1, 7, 0, False)
            project(ITEMS - 2, 6)
            attend(ITEMS - 1, 7, 1, False)
            project(ITEMS - 1, 7)

            pe.wait_ge(d_win, 16)
            pe.wait_ge(d_wo0, 16)
            pe.wait_ge(s_exp, 2 * ITEMS)

            def wout_T(e):
                if e >= 2:
                    pe.wait_ge(e0_wTc[e % 2], e // 2)
                for f in range(FT):
                    last = transpose(bank(e % 2, f * P, (f + 1) * P), w_out_sb[:, e, f * P:(f + 1) * P])
                last.then_inc(e0_wT, 1)

            wout_T(0)
            for e in range(E):
                if e + 1 < E:
                    wout_T(e + 1)
                pe.wait_ge(e0_wTc[e % 2], e // 2 + 1)
                for f in range(FT):
                    last = mm(bank(2 + e // 4, (e % 4) * D, (e % 4 + 1) * D), w_in_sb[:, e, f, :], woT[:, e % 2, f, :],
                              start=f == 0, stop=f == FT - 1)
                last.then_inc(e0_m, 1)
            pe.wait_ge(s_ptl, 2 * ITEMS)
            for b in range(B):
                if b >= 2:
                    pe.wait_ge(c1_c, b - 1)
                for i in range(CT):
                    last = transpose(bank(4 + b % 2, i * P, (i + 1) * P), ctx_sb[:, b, i, :])
                last.then_inc(c1_mm, 1)
            pe.wait_ge(d_small, 64)
            pe.wait_ge(d_qk1w, 48)
            pe.wait_ge(s_yl, ITEMS)
            nc.tensor.transpose(bank(6, 0, E), small[:, 0:D], ident[0:E, 0:E])
            nc.tensor.transpose(bank(6, E, 2 * E), small[:, D:2 * D], ident[0:E, 0:E])
            nc.tensor.transpose(bank(6, 16, 16 + E * FT), b1n[:, :], ident[0:E * FT, 0:E * FT])
            transpose(bank(6, 128, 256), qk1w[:, 2, :])
            mm(bank(6, 256, 384), qk1w[:, 0, :], qk1w[:, 1, :], start=True, stop=True).then_inc(c1_mm, 1)

            def norm_T(k, need):
                for c in range(2):
                    pe.wait_ge(n_xn, need + 4 * c + 4)
                    for q in range(4):
                        last = transpose(bank(c, q * P, (q + 1) * P), xn[:, 4 * c + q, :])
                    last.then_inc(n_T, 1)

            def router(k):
                for t in range(NT):
                    if t % 4 == 0:
                        pe.wait_ge(n_Tc, 2 * k + t // 4 + 1)
                    last = mm(bank(3, t * E, (t + 1) * E), xT[:, t * P:(t + 1) * P], wgT[:, k, :], start=True, stop=True)
                last.then_inc(g_mm, 1)

            for s in e0_wTc:
                pe.wait_ge(s, E // 2)
            norm_T(0, 0)
            pe.wait_ge(c1_c, B + 4)
            pe.wait_ge(e0_mc, 2)
            router(0)
            pe.wait_ge(s_acc, 2 * ITEMS)
            for t in range(NT):
                for c in range(2):
                    r = 2 * t + c
                    if r >= 4:
                        pe.wait_ge(f0_c, 4 * (r - 3))
                    mm(bank(4 + r % 4), xT[:, t * P:(t + 1) * P], moe0[:, 4 * c:4 * c + 4, :].rearrange("p e n -> p (e n)"),
                       start=True, stop=True).then_inc(f0_mm, 1)

            for c in range(4):
                if c < 2:
                    pe.wait_ge(l1_hid, 4 * c + 4)
                else:
                    pe.wait_ge(l1_nrm, 4 * c - 4)
                    pe.wait_ge(l1_Tc, c - 1)
                src = xn if c < 2 else normed
                for q in range(4):
                    last = transpose(bank(c % 2, q * P, (q + 1) * P), src[:, 4 * (c % 2) + q, :])
                last.then_inc(l1_T, 1)
            pe.wait_ge(f0_c, 8 * NT)
            for c in range(2):
                pe.wait_ge(l1_Tc, c + 1)
                for q in range(4):
                    t = 4 * c + q
                    last = mm(bank(6 + c, q * D, (q + 1) * D), xT[:, t * P:(t + 1) * P], gwT[:, :], start=True, stop=True)
                last.then_inc(l1_z, 1)
            for c in range(2):
                pe.wait_ge(l1_Tc, c + 3)
                mm(bank(4 + c), A1[:, :], normT[:, 512 * c:512 * c + 512], start=True, stop=True).then_inc(l1_q, 1)
            pe.wait_ge(l1_Tc, 4)
            pe.wait_ge(g_d, 1)

            def scores1(u):
                b, sp = u // 2, S_PS[u % 2]
                if u >= 2:
                    pe.wait_ge(a_exp, u - 1)
                pe.wait_ge(l1_qc, u // 4 + 1)
                mm(sp[:, 0:SC], q1T[:, u * P:(u + 1) * P], ctxT[:, b, :], start=True, stop=True)
                mm(sp[:, SC:NK], q1T[:, u * P:(u + 1) * P], normT[:, b * SQ:(b + 1) * SQ], start=True, stop=True).then_inc(a_S, 1)

            def probs_T1(u):
                pe.wait_ge(a_exp, u + 1)
                if u == 0:
                    pe.wait_ge(l1_qc, 2)
                else:
                    pe.wait_ge(a_Tc, u)
                for i in range(KT):
                    last = transpose(PT_PS[:, i * P:(i + 1) * P], probs[:, u % 2, i * P:(i + 1) * P])
                last.then_inc(a_T, 1)

            def attend1(u):
                b = u // 2
                pe.wait_ge(a_Tc, u + 1)
                if u < 2:
                    pe.wait_ge(l1_zb, 2)
                else:
                    pe.wait_ge(a_fin, u - 1)
                for i in range(KT):
                    v = ctx_sb[:, b, i, :] if i < CT else normed[:, QT * b + i - CT, :]
                    last = mm(bank(6 + u % 2, 0, D), pt1[:, u % 2, i, :], v, start=i == 0, stop=i == KT - 1)
                last.then_inc(a_O, 1)

            scores1(0)
            for u in range(NT):
                if u + 1 < NT:
                    scores1(u + 1)
                probs_T1(u)
                attend1(u)

            pe.wait_ge(a_exp, NT)
            norm_T(1, NT)
            router(1)
            pe.wait_ge(g_ok, 1)
            for c in range(2):
                pe.wait_ge(n_Tc, 3 + c)
                for q in range(4):
                    last = transpose(ps[0:E, c, q * P:(q + 1) * P], gates[:, 4 * c + q, :])
                last.then_inc(f1_gT, 1)
            pe.wait_ge(a_fin, NT)
            for c in range(2):
                pe.wait_ge(f1_gTc, c + 1)
                for q in range(4):
                    t = 4 * c + q
                    last = mm(bank(4 + c, q * D, (q + 1) * D), gT[:, t * P:(t + 1) * P], small[:, 2 * D:3 * D], start=True, stop=True)
                last.then_inc(f1_b2, 1)

            def expert_T(e, s, i, first):
                pe.wait_ge(d_w1[s], i * 16 + 16)
                if not first:
                    pe.wait_ge(f1_wl, e * 2 - 1)
                for f in range(FT):
                    last = transpose(bank(0, f * P, (f + 1) * P), w1n[:, s, f, :])
                last.then_inc(f1_wT, 1)
                pe.wait_ge(d_w2[s], i * 16 + 16)
                if not first:
                    pe.wait_ge(f1_wl, e * 2)
                for f in range(FT):
                    last = transpose(bank(1, f * P, (f + 1) * P), w2n[:, s, f * P:(f + 1) * P])
                last.then_inc(f1_wT, 1)

            def up(e, s, c, first):
                if c == 0:
                    pe.wait_ge(f1_wl, e * 2 + 2)
                tok = slice(512 * c, 512 * c + 512)
                for f in range(FT):
                    if not (first and c == 0 and f < 2):
                        pe.wait_ge(f1_gelu, e * 8 + (4 * c + f - 1))
                    fs = slice(f * P, f * P + P)
                    mm(bank(2 + f % 2), w1Th[:, s, fs], xTh[:, tok], start=True, stop=False)
                    mm(bank(2 + f % 2), w1Th[:, s, fs], xTl[:, tok], start=False, stop=False)
                    mm(bank(2 + f % 2), w1Tl[:, s, fs], xTh[:, tok], start=False, stop=True).then_inc(f1_U, 1)

            def down(e, s, c, first):
                pe.wait_ge(f1_hl, e * 8 + (4 * c + 4))
                for q in range(4):
                    t = 4 * c + q
                    if not (first and c == 0):
                        pe.wait_ge(f1_acc, e * 8 + (t - 3))
                    o, tok = bank(4 + q, 0, D), slice(q * P, q * P + P)
                    for f in range(FT):
                        w = slice(f * D, f * D + D)
                        mm(o, hh[:, c, f, tok], w2Th[:, s, w], start=f == 0, stop=False)
                        mm(o, hh[:, c, f, tok], w2Tl[:, s, w], start=False, stop=False)
                        last = mm(o, hl[:, c, f, tok], w2Th[:, s, w], start=False, stop=f == FT - 1)
                    last.then_inc(f1_V, 1)

            pe.wait_ge(f1_xl, 2)
            pe.wait_ge(f1_gTc, 2)
            pe.wait_ge(f1_b2c, 2)

            def pe_expert(e, s, i, static):
                expert_T(e, s, i, static and s == 0)
                up(e, s, 0, static and s == 0)
                if not (static and s == 0):
                    down(e - 1, 1 - s, 1, static and s == 0)
                up(e, s, 1, static and s == 0)
                down(e, s, 0, static and s == 0)

            for s in range(2):
                pe_expert(s, s, 0, True)
            with pe.Fori(1, E // 2) as i:
                for s in range(2):
                    pe_expert(i * 2 + s, s, i, False)
            down(E - 1, 1, 1, False)


_INS = ['x', 'ctx_1024', 'L0_xattn_ln_m_g', 'L0_xattn_ln_m_b', 'L0_xattn_ln_l_g', 'L0_xattn_ln_l_b',
        'L0_xattn_Wq', 'L0_xattn_Wkv', 'L0_xattn_Wout', 'L0_ffn_w_gate', 'L0_ffn_w_in', 'L0_ffn_w_out',
        'L1_xattn_q_w', 'L1_xattn_k_w', 'L1_xattn_norm_w', 'L1_xattn_gate_w', 'L1_xattn_gate_b',
        'L1_ffn_router_w', 'L1_ffn_router_b', 'L1_ffn_w1', 'L1_ffn_b1', 'L1_ffn_w2', 'L1_ffn_b2',
        'L1_ffn_ln_w', 'L1_ffn_ln_b']


def kernel(**inputs):
    import numpy as _np
    import concourse.bacc as _bacc
    from concourse import mybir as _mybir
    from concourse.bass_utils import run_bass_kernel_spmd as _run

    nc = _bacc.Bacc("TRN2", target_bir_lowering=False, num_devices=1)
    arrays, aps = {}, {}
    for name in _INS:
        a = _np.ascontiguousarray(inputs[name])
        arrays[f"in_{name}"] = a
        aps[name] = nc.dram_tensor(f"in_{name}", a.shape, _mybir.dt.from_np(a.dtype), kind="ExternalInput").ap()
    out = nc.dram_tensor("out_0", (B, SQ, D), _mybir.dt.float32, kind="ExternalOutput").ap()
    transformer_program(nc, aps, out)
    r = _run(nc, [arrays], core_ids=[0])
    return r.results[0]["out_0"]
```

```python
import concourse.bass as bass
from concourse import mybir
from contextlib import ExitStack

B, SQ, SC, D = 4, 256, 512, 128
P = 128
NT = B * SQ // P
CT = SC // P
QT = SQ // P
KT = CT + QT
NK = KT * P
HEADS, DH = 16, 64
NPAIR = HEADS // 2
FIRST_PAIRS = 2
WARM_UP = 28
KEY_PARTS = ((0, SC), (SC, NK))
ITEMS = HEADS * B
E, TOPK, FF = 8, 2, 512
E_VECTOR = 5
FT = FF // P
LN_EPS = 1e-5
RMS_EPS = 1e-6
LN2_EPS = 1e-12
HEAD_SCALE = DH ** -0.5
SCALE1 = D ** -0.5
MASKED = -1e30


def transformer_program(nc, A, out):
    F32, F16, U32 = mybir.dt.float32, mybir.dt.float16, mybir.dt.uint32
    ALU = mybir.AluOpType
    ACT = mybir.ActivationFunctionType
    AX = mybir.AxisListType

    ctx = ExitStack()
    with ctx:
        def sb(name, shape, dt=F32):
            return ctx.enter_context(nc.sbuf_tensor(name, shape, dt))

        def sem(name):
            return ctx.enter_context(nc.semaphore(name))

        def at(start, size):
            return bass.ds(start, size)

        ident = sb("ident", [P, P])
        causal = sb("causal", [P, P])
        minus_half = sb("minus_half", [P, B * KT])
        iota_e = sb("iota_e", [P, NT, E])
        x_cur = sb("x_cur", [P, NT, D])
        ctx_sb = sb("ctx_sb", [P, B, CT, D])
        ln_rows = sb("ln_rows", [P, 4, D])
        kvf = sb("kvf", [P, B, KT, D])
        kv = sb("kv", [P, 4, B * NK], F16)
        kvh, kvl = (kv[:, i, :].rearrange("p (b i d) -> p b i d", b=B, i=KT) for i in range(2))
        kth, ktl = (kv[:, i, :].rearrange("p (b n) -> p b n", b=B) for i in (2, 3))
        w0 = sb("w0", [P, 4 * HEADS * DH])
        wq_sb = w0[:, 0:HEADS * DH]
        wkv_sb = w0[:, HEADS * DH:3 * HEADS * DH]
        wout_sb = w0[:, 3 * HEADS * DH:4 * HEADS * DH].rearrange("p (a d) -> p a d", a=NPAIR)
        wqkvT = sb("wqkvT", [P, 2, 3, P])
        ab_all = sb("ab_all", [P, HEADS, 4, P], F16)
        ab = sb("ab", [P, 2, 4, P], F16)
        qkh = sb("qkh", [P, 2, SQ], F16)
        qkl = sb("qkl", [P, 2, SQ], F16)
        probs = sb("probs", [P, 2, NK])
        pth = sb("pth", [P, 2, KT, SQ], F16)
        ptl = sb("ptl", [P, 2, KT, SQ], F16)
        yh = sb("yh", [P, 2, SQ], F16)
        yl = sb("yl", [P, 2, SQ], F16)
        neg_max = sb("neg_max", [P, 2])
        den = sb("den", [P, 2 * E, 1])
        rden = sb("rden", [P, 2 * E, 1])
        stats = sb("stats", [P, B * KT, 6])
        mv = sb("mv", [P, B * KT, 2])
        var_e = sb("var_e", [P, B * KT])
        rstd = sb("rstd", [P, B * KT])
        rstd2 = sb("rstd2", [P, NT])
        tmp8 = sb("tmp8", [P, NT])
        w_in_sb = sb("w_in_sb", [P, E, FT, D])
        w_out_sb = w0[:, :].rearrange("p (e f) -> p e f", e=E)
        woT = sb("woT", [P, 2, FT, D])
        moe0h = sb("moe0h", [P, E, D], F16)
        moe0l = sb("moe0l", [P, E, D], F16)
        small = sb("small", [E, 2 * D])
        wgT = sb("wgT", [P, 2, E])
        b1n = sb("b1n", [E * FT, P])
        b1T = sb("b1T", [P, E * FT])
        b1c = sb("b1c", [P, 2, FT])
        xn = sb("xn", [P, NT, D])
        xT = sb("xT", [P, NT * P])
        logits = sb("logits", [P, NT, E])
        top8 = sb("top8", [P, NT, 8])
        idx8 = sb("idx8", [P, NT, 8], U32)
        idxf = sb("idxf", [P, NT, 8])
        g12 = sb("g12", [P, 3, NT])
        scaled = sb("scaled", [P, 2, E // 2, D])
        hit = sb("hit", [P, 2, NT, E])
        gates = sb("gates", [P, NT, E])
        rows1 = sb("rows1", [P, 4, D])
        rb_row = sb("rb_row", [P, E])
        qk1w = sb("qk1w", [P, 3, D])
        A1 = sb("A1", [P, D])
        gwT = sb("gwT", [P, D])
        kv32 = kv[:, :, :].rearrange("p a n -> p (a n)").bitcast(F32)
        ctxT = kv32[:, 0:B * SC].rearrange("p (b n) -> p b n", b=B)
        normT, q1T = (kv32[:, B * SC + i * NT * P:B * SC + (i + 1) * NT * P] for i in range(2))
        normed, alpha = (kv32[:, B * SC + i * NT * P:B * SC + (i + 1) * NT * P].rearrange("p (t d) -> p t d", t=NT)
                         for i in (2, 3))
        pt1 = sb("pt1", [P, 2, KT, P])
        w1n = sb("w1n", [P, 2, FT, D])
        w2n = sb("w2n", [P, 2, FF])
        w1Th = sb("w1Th", [P, 2, FF], F16)
        w1Tl = sb("w1Tl", [P, 2, FF], F16)
        w2Th = sb("w2Th", [P, 2, FT * D], F16)
        w2Tl = sb("w2Tl", [P, 2, FT * D], F16)
        xTh = sb("xTh", [P, NT * P], F16)
        xTl = sb("xTl", [P, NT * P], F16)
        hf = sb("hf", [P, FT, 512])
        gelu_first = sb("gelu_first", [P, FT])
        hh, hl = (ab_all[:, 8 * i:8 * i + 8, :, :].rearrange("p (c f) a n -> p c f (a n)", c=2) for i in range(2))
        gT = sb("gT", [NT * E, P])
        b2d = sb("b2d", [NT * E, NT, D])
        xb = sb("xb", [P, NT, D])
        acc4 = sb("acc4", [P, NT, D])

        ps = ctx.enter_context(nc.psum_tensor("ps", [P, 8, 512], F32))

        def bank(i, lo=0, hi=512):
            return ps[:, i, lo:hi]

        S_PS = [ps[:, 0:2, :].rearrange("p a n -> p (a n)"), ps[:, 2:4, :].rearrange("p a n -> p (a n)")]
        PT_PS = ps[:, 4:6, :].rearrange("p a n -> p (a n)")

        def hidden_bank(g, f):
            return (7, 3, 6, 2)[f] if g is None else (2, 3, 6)[(g * FT + f) % 3]
        AB_PS = [ps[:, 2 + 2 * i:4 + 2 * i, 0:2 * P].rearrange("p h (a n) -> p h a n", a=2) for i in range(2)]
        Y_PS = bank(6, 0, SQ)
        QK_PS = bank(7, 0, SQ)
        O_PS = bank(7, SQ, 512)

        d_x, d_w_first, d_w_rest, d_ln = (sem(n) for n in ("d_x", "d_w_first", "d_w_rest", "d_ln"))
        d_ctx = [sem(f"d_ctx{b}") for b in range(B)]
        d_win, d_wo0, d_small, d_rows1, d_qk1w = (sem(n) for n in ("d_win", "d_wo0", "d_small", "d_rows1", "d_qk1w"))
        d_w1 = [sem("d_w1a"), sem("d_w1b")]
        d_w2 = [sem("d_w2a"), sem("d_w2b")]
        d_out = sem("d_out")
        s_const, s_v, s_xcur = sem("s_const"), sem("s_v"), sem("s_xcur")
        s_ve, s_r1, s_we, s_r2 = (sem(n) for n in ("s_ve", "s_r1", "s_we", "s_r2"))
        s_kv0, s_xhat, s_gm, s_kv, s_kvh, s_kvl = (sem(n) for n in ("s_kv0", "s_xhat", "s_gm", "s_kv", "s_kvh", "s_kvl"))

        def key_tiles(u):
            return CT + 1 + u % 2

        def keys_bank(b, k):
            return (7, 6, 5, 4)[k + 2 * (b == B - 1)]

        def wait_keys(eng, b, parts):
            if b:
                eng.wait_ge(s_kv, 2 * b - 2 + parts)
            else:
                eng.wait_ge(s_kv0, parts)
        s_wT_mm, s_wT, s_ab_mm, s_abh, s_abl = (sem(n) for n in ("s_wT_mm", "s_wT", "s_ab_mm", "s_abh", "s_abl"))
        s_kt_mm, s_kth, s_ktl = (sem(n) for n in ("s_kt_mm", "s_kth", "s_ktl"))
        s_ab, s_qk, s_qkh, s_qkl = (sem(n) for n in ("s_ab", "s_qk", "s_qkh", "s_qkl"))
        s_S, s_max, s_exp, s_T, s_pth, s_ptl = (sem(n) for n in ("s_S", "s_max", "s_exp", "s_T", "s_pth", "s_ptl"))
        s_Y, s_yh, s_yl, s_O, s_rden, s_acc = (sem(n) for n in ("s_Y", "s_yh", "s_yl", "s_O", "s_rden", "s_acc"))

        def load(eng, dst, src, s):
            eng.dma_start(dst, src).then_inc(s, 16)

        ctx_v = A["ctx_1024"].rearrange("b (i p) d -> p b i d", p=P)
        w1_v = A["L1_ffn_w1"].rearrange("e (t p) d -> p e t d", p=P)
        w2_v = A["L1_ffn_w2"].rearrange("e p f -> p e f")

        e0_wT, e0_m, e0_mc = (sem(n) for n in ("e0_wT", "e0_m", "e0_mc"))
        e0_wTc = sem("e0_wTc")
        c1_mm, c1_c = sem("c1_mm"), sem("c1_c")
        n_ve, n_r, n_xn, n_T, n_Tc = (sem(n) for n in ("n_ve", "n_r", "n_xn", "n_T", "n_Tc"))
        g_mm, g_d, g_e, g_ok = (sem(n) for n in ("g_mm", "g_d", "g_e", "g_ok"))
        e0_ml, e0_xh, e0_xl = sem("e0_ml"), sem("e0_xh"), sem("e0_xl")
        f0_mm, f0_c, f0_s, f0_p, f0_x = (sem(n) for n in ("f0_mm", "f0_c", "f0_s", "f0_p", "f0_x"))

        def bank0(t, c):
            return (4 + 2 * t + c) % 8
        l1_ve, l1_r, l1_we, l1_r2, l1_hid, l1_nrm = (sem(n) for n in ("l1_ve", "l1_r", "l1_we", "l1_r2", "l1_hid", "l1_nrm"))
        l1_T, l1_Tc, l1_z, l1_zb, l1_al, l1_q, l1_qc = (sem(n) for n in ("l1_T", "l1_Tc", "l1_z", "l1_zb", "l1_al", "l1_q", "l1_qc"))
        a_S, a_max, a_exp, a_T, a_Tc, a_O, a_fin = (sem(n) for n in ("a_S", "a_max", "a_exp", "a_T", "a_Tc", "a_O", "a_fin"))
        f1_wT, f1_wh, f1_wl, f1_U, f1_gelu, f1_hh, f1_hl, f1_V, f1_acc = (
            sem(n) for n in ("f1_wT", "f1_wh", "f1_wl", "f1_U", "f1_gelu", "f1_hh", "f1_hl", "f1_V", "f1_acc"))
        f1_gT, f1_gTc, f1_b2, f1_b2c, f1_xh, f1_xl = (sem(n) for n in ("f1_gT", "f1_gTc", "f1_b2", "f1_b2c", "f1_xh", "f1_xl"))
        f1_b1, f1_g0 = sem("f1_b1"), sem("f1_g0")
        d_b2, s_b2z, z_xb, z_s = sem("d_b2"), sem("s_b2z"), sem("z_xb"), sem("z_s")
        z_fin = sem("z_fin")

        block = ctx.enter_context(nc.Block())

        @block.sync
        def _(sp):
            wout_v = A["L0_xattn_Wout"].rearrange("(a p) d -> p a d", p=P)
            for lo, hi, s in ((0, FIRST_PAIRS, d_w_first), (FIRST_PAIRS, NPAIR, d_w_rest)):
                if lo:
                    sp.wait_ge(d_x, 16)
                load(sp, wq_sb[:, lo * P:hi * P], A["L0_xattn_Wq"][:, lo * P:hi * P], s)
                wkv_v = A["L0_xattn_Wkv"].rearrange("p (a n) -> p a n", a=2)
                load(sp, wkv_sb.rearrange("p (a n) -> p a n", a=2)[:, :, lo * P:hi * P], wkv_v[:, :, lo * P:hi * P], s)
                load(sp, wout_sb[:, lo:hi, :], wout_v[:, lo:hi, :], s)
            sp.wait_ge(d_w_rest, 48)
            for i, name in enumerate(("L0_ffn_w_gate", "L1_ffn_router_w")):
                load(sp, small[:, i * D:(i + 1) * D], A[name], d_small)
            load(sp, b1n[:, :], A["L1_ffn_b1"].rearrange("e (t p) -> (e t) p", p=P), d_small)
            for i, name in enumerate(("L1_xattn_norm_w", "L1_xattn_gate_b", "L1_ffn_ln_w", "L1_ffn_ln_b")):
                load(sp, rows1[:, i, :], A[name].partition_broadcast(P), d_rows1)
            load(sp, rb_row[:, :], A["L1_ffn_router_b"].partition_broadcast(P), d_rows1)
            load(sp, qk1w[:, 0, :], A["L1_xattn_q_w"], d_qk1w)
            load(sp, qk1w[:, 1, :], A["L1_xattn_k_w"], d_qk1w)
            load(sp, qk1w[:, 2, :], A["L1_xattn_gate_w"], d_qk1w)
            load(sp, w_in_sb[:, :, :, :], A["L0_ffn_w_in"].rearrange("e (t p) d -> p e t d", p=P), d_win)
            sp.wait_ge(s_ab_mm, NPAIR)
            load(sp, w_out_sb, A["L0_ffn_w_out"].rearrange("e p f -> p e f"), d_wo0)
            for e in range(2):
                load(sp, w1n[:, e, :, :], w1_v[:, e, :, :], d_w1[e])
                load(sp, w2n[:, e, :], w2_v[:, e, :], d_w2[e])
            sp.wait_ge(s_b2z, 1)
            for t in range(NT):
                load(sp, b2d[t * E:(t + 1) * E, t, :], A["L1_ffn_b2"], d_b2)
            with sp.Fori(1, E // 2) as i:
                for e in range(2):
                    sp.wait_ge(f1_wT, i * 4 + (2 * e - 2))
                    load(sp, w1n[:, e, :, :], w1_v[:, at(i * 2 + e, 1), :, :].rearrange("p a t d -> p (a t) d"), d_w1[e])
                    load(sp, w2n[:, e, :], w2_v[:, at(i * 2 + e, 1), :].rearrange("p a f -> p (a f)"), d_w2[e])
            out_v = out.rearrange("b (j p) d -> p (b j) d", p=P)
            for c in range(4):
                sp.wait_ge(z_fin, 2 * c + 2)
                load(sp, out_v[:, 2 * c:2 * c + 2, :], acc4[:, 2 * c:2 * c + 2, :], d_out)
            sp.wait_ge(d_out, 64)

        @block.gpsimd
        def _(pool):
            pool.memset(ident[:, :], 0.0).then_inc(s_const, 1)
            pool.memset(minus_half[:, :], -0.5).then_inc(s_const, 1)
            pool.wait_ge(s_const, 2)
            pool.affine_select(out=ident[:, :], in_=ident[:, :], compare_op=ALU.not_equal, fill=1.0, base=0,
                               pattern=[[-1, P]], channel_multiplier=1).then_inc(s_const, 1)

            def rsqrt(dst, src, s):
                pool.tensor_tensor(dst, src, minus_half[:, 0:src.shape[1]], ALU.pow).then_inc(s, 1)

            def head_weights(h):
                if h % 2 == 0:
                    pool.wait_ge(s_abh, h // 2 + 1)
                    pool.wait_ge(s_abl, h // 2 + 1)
                if h >= 2:
                    pool.wait_ge(s_O, B * (h - 1))
                pool.tensor_copy(ab[:, h % 2, :, :].bitcast(U32), ab_all[:, h, :, :].bitcast(U32)).then_inc(s_ab, 1)

            def first_rsqrt(b):
                pool.wait_ge(s_ve, b + 1)
                rsqrt(rstd[:, b * KT:(b + 1) * KT], var_e[:, b * KT:(b + 1) * KT], s_r1)

            def second_rsqrt(b):
                pool.wait_ge(s_we, b + 1)
                rsqrt(rstd2[:, QT * b:QT * b + QT], tmp8[:, QT * b:QT * b + QT], s_r2)

            def affine(b):
                parts = ((0, CT), (CT, KT))
                for k, (lo, hi) in enumerate(parts):
                    pool.wait_ge(s_xhat, 2 * b + k - 1)
                    v = kvf[:, b, lo:hi, :]
                    g = ln_rows[:, 2 * k, :].unsqueeze(1).broadcast_to([P, hi - lo, D])
                    pool.tensor_tensor(v, v, g, ALU.mult).then_inc(s_gm, 1)
                for k, (lo, hi) in enumerate(parts):
                    pool.wait_ge(s_gm, 2 * b + k - 1)
                    v = kvf[:, b, lo:hi, :]
                    h = ln_rows[:, 2 * k + 1, :].unsqueeze(1).broadcast_to([P, hi - lo, D])
                    pool.tensor_tensor(v, v, h, ALU.add).then_inc(s_kv, 1)

            first_rsqrt(0)
            first_rsqrt(1)
            second_rsqrt(0)
            second_rsqrt(1)
            first_rsqrt(2)
            affine(1)
            head_weights(0)
            second_rsqrt(2)
            first_rsqrt(3)
            affine(2)
            second_rsqrt(3)
            affine(3)
            for b in range(B):
                pool.wait_ge(s_kvh, b + 1)
                pool.tensor_tensor(kvl[:, b, :, :], kvf[:, b, :, :], kvh[:, b, :, :], ALU.subtract).then_inc(s_kvl, 1)
            pool.memset(causal[:, :], 0.0).then_inc(s_const, 1)
            head_weights(1)
            pool.wait_ge(s_const, 4)
            pool.affine_select(out=causal[:, :], in_=causal[:, :], compare_op=ALU.is_ge, fill=MASKED, base=0,
                               pattern=[[-1, P]], channel_multiplier=1).then_inc(s_const, 1)
            pool.iota(iota_e[:, :, :], pattern=[[0, NT], [1, E]], base=0, channel_multiplier=0,
                      allow_small_or_imprecise_dtypes=True).then_inc(s_const, 1)
            pool.memset(b2d[:, :, :], 0.0).then_inc(s_b2z, 1)
            for h in range(2, HEADS):
                head_weights(h)
            def rsqrt_half(c, src_sem, count, dst_sem, dst=rstd, src=var_e):
                pool.wait_ge(src_sem, count)
                rsqrt(dst[:, 4 * c:4 * c + 4], src[:, 4 * c:4 * c + 4], dst_sem)

            def add_scaled(t):
                v = scaled[:, t % 2, :, :]
                for i in range(2):
                    pool.wait_ge(f0_s, 4 * t + 3 + i)
                    if i:
                        pool.wait_ge(f0_p, 2 * t + 1)
                    pool.tensor_tensor(v[:, 1, :], v[:, 1, :], v[:, 2 + i, :], ALU.add).then_inc(f0_p, 1)
                pool.wait_ge(f0_p, 2 * t + 2)
                pool.wait_ge(f0_c, 2 * E_VECTOR * (t // 2 + 1))
                pool.tensor_tensor(x_cur[:, t, :], x_cur[:, t, :], v[:, 1, :], ALU.add).then_inc(f0_x, 1)

            for c in range(2):
                rsqrt_half(c, n_ve, c + 1, n_r)
            for t in range(5):
                add_scaled(t)
            rsqrt_half(0, l1_ve, 1, l1_r)
            add_scaled(5)
            rsqrt_half(0, l1_we, 1, l1_r2, rstd2, tmp8)
            add_scaled(6)
            add_scaled(7)
            rsqrt_half(1, l1_ve, 2, l1_r)
            rsqrt_half(1, l1_we, 2, l1_r2, rstd2, tmp8)
            for c in range(2):
                rsqrt_half(c, n_ve, 3 + c, n_r)
            pool.wait_ge(a_fin, NT)
            pool.tensor_tensor(xb[:, :, :], x_cur[:, :, :], rows1[:, 3, :].unsqueeze(1).broadcast_to([P, NT, D]),
                               ALU.add).then_inc(z_xb, 1)
            rsqrt_half(0, n_ve, 5, n_r)
            for q in range(2):
                pool.wait_ge(n_ve, 6 + q)
                v = slice(4 + 2 * q, 6 + 2 * q)
                rsqrt(rstd[:, v], var_e[:, v], n_r)

        @block.scalar
        def _(act):
            load(act, x_cur[:, :, :], A["x"].rearrange("b (j p) d -> p (b j) d", p=P), d_x)
            for b in range(B):
                load(act, ctx_sb[:, b, :, :], ctx_v[:, b, :, :], d_ctx[b])
                if b == 0:
                    for i, name in enumerate(("ln_m_g", "ln_m_b", "ln_l_g", "ln_l_b")):
                        load(act, ln_rows[:, i, :], A["L0_xattn_" + name].partition_broadcast(P), d_ln)

            def weights_T(p):
                act.wait_ge(s_wT_mm, p + 1)
                if p >= 2:
                    act.wait_ge(s_ab_mm, p - 1)
                nc.scalar.copy(wqkvT[:, p % 2, :, :], bank(p % 2, 0, 384).rearrange("p (a n) -> p a n", a=3)).then_inc(s_wT, 1)

            def kv_high(b):
                wait_keys(act, b, 2)
                nc.scalar.copy(kvh[:, b, :, :], kvf[:, b, :, :]).then_inc(s_kvh, 1)

            def keys_T_high(b, k):
                act.wait_ge(s_kt_mm, 2 * b + k + 1)
                lo, hi = KEY_PARTS[k]
                nc.scalar.copy(kth[:, b, lo:hi], bank(keys_bank(b, k), 0, hi - lo)).then_inc(s_kth, 1)

            def queries_high(n, k):
                act.wait_ge(s_qk, n + 1)
                nc.scalar.activation(qkh[:, k % 2, :], QK_PS, ACT.Copy, scale=HEAD_SCALE).then_inc(s_qkh, 1)

            weights_T(0)
            for p in range(NPAIR):
                if p + 1 < NPAIR:
                    weights_T(p + 1)
                else:
                    queries_high(0, 0)
                act.wait_ge(s_ab_mm, p + 1)
                nc.scalar.copy(ab_all[:, 2 * p:2 * p + 2, 0::2, :], AB_PS[p % 2]).then_inc(s_abh, 1)
                if p % 2:
                    keys_T_high(p // 2, 0)
                    keys_T_high(p // 2, 1)
                if p % 2 and p + 1 < NPAIR:
                    kv_high(p // 2)

            def probs_T_high(n, k, j):
                act.wait_ge(s_T, n * 2 + (j + 1))
                nc.scalar.copy(pth[:, k % 2, :, j * P:(j + 1) * P],
                               PT_PS[:, 0:NK].rearrange("p (i q) -> p i q", i=KT)).then_inc(s_pth, 1)

            def exponentials(n, k, j, first):
                act.wait_ge(s_max, n * 2 + (j + 1))
                if not first:
                    act.wait_ge(s_T, n * 2 + (j - 1))
                nc.scalar.activation(probs[:, j, :], S_PS[j][:, 0:NK], ACT.Exp, bias=neg_max[:, j:j + 1],
                                     accum_out=den[:, 2 * (k % 8) + j, :]).then_inc(s_exp, 1)

            def attended_high(n, k):
                act.wait_ge(s_Y, n + 1)
                nc.scalar.copy(yh[:, k % 2, :], Y_PS).then_inc(s_yh, 1)

            def item(n, k, start=3, last=False):
                if start >= 1:
                    probs_T_high(n - 1, k - 1, 1)
                exponentials(n, k, 0, start == 0)
                if start == 0:
                    kv_high(B - 1)
                if start >= 2:
                    attended_high(n - 2, k)
                if not last:
                    queries_high(n + 1, k + 1)
                probs_T_high(n, k, 0)
                exponentials(n, k, 1, start == 0)

            for k in range(8):
                item(k, k, start=min(k, 3))
            with act.Fori(1, ITEMS // 8 - 1) as p:
                for k in range(8):
                    item(p * 8 + k, k)
            for k in range(8):
                item(ITEMS - 8 + k, k, last=k == 7)

            def w_out_T(e):
                act.wait_ge(e0_wT, e + 1)
                if e >= 2:
                    act.wait_ge(e0_m, e - 1)
                nc.scalar.copy(woT[:, e % 2, :, :], bank(e % 2).rearrange("p (t n) -> p t n", t=FT)).then_inc(e0_wTc, 1)

            probs_T_high(ITEMS - 1, 7, 1)
            w_out_T(0)
            attended_high(ITEMS - 2, 6)
            w_out_T(1)
            w_out_T(2)
            attended_high(ITEMS - 1, 7)
            for e in range(3, E):
                w_out_T(e)
            for c in range(2):
                act.wait_ge(e0_m, 4 * c + 4)
                nc.scalar.copy(moe0h[:, 4 * c:4 * c + 4, :], bank(2 + c).rearrange("p (e n) -> p e n", e=4)).then_inc(e0_mc, 1)
            act.wait_ge(c1_mm, 1)
            nc.scalar.copy(wgT[:, :, :], bank(6, 0, 2 * E).rearrange("p (a n) -> p a n", a=2)).then_inc(c1_c, 1)
            nc.scalar.copy(b1T[:, :], bank(6, 16, 16 + E * FT)).then_inc(c1_c, 1)
            nc.scalar.copy(gwT[:, :], bank(6, 128, 256)).then_inc(c1_c, 1)
            nc.scalar.copy(A1[:, :], bank(6, 256, 384)).then_inc(c1_c, 1)

            def norm_T(i, c, src):
                act.wait_ge(n_T, i + 1)
                nc.scalar.copy(xT[:, 512 * c:512 * c + 512], src).then_inc(n_Tc, 1)

            def gate_tanh(k):
                act.wait_ge(g_d, k + 1)
                nc.scalar.activation(g12[:, 2, :], g12[:, 0, :], ACT.Tanh, scale=0.5).then_inc(g_e, 1)

            for c in range(2):
                norm_T(c, c, bank(c))
                act.wait_ge(n_Tc, c + 1)
                nc.scalar.copy(xTh[:, 512 * c:512 * c + 512], xT[:, 512 * c:512 * c + 512]).then_inc(e0_xh, 1)
            gate_tanh(0)
            act.wait_ge(g_ok, 1)
            def scale_experts(t):
                act.wait_ge(f0_mm, 2 * t + 2)
                if t >= 2:
                    act.wait_ge(f0_x, t - 1)
                for e in range(4):
                    nc.scalar.activation(scaled[:, t % 2, e, :], bank(bank0(t, 1), e * D, (e + 1) * D), ACT.Copy,
                                         scale=gates[:, t, 4 + e:5 + e]).then_inc(f0_s, 1)

            def context_T(b):
                act.wait_ge(c1_mm, b + 2)
                nc.scalar.copy(ctxT[:, b, :], bank(4 + b % 2)).then_inc(c1_c, 1)

            for t in range(6):
                scale_experts(t)
            context_T(0)
            context_T(1)
            scale_experts(6)
            context_T(2)
            scale_experts(7)
            context_T(3)

            def exp1(u):
                act.wait_ge(a_max, u + 1)
                if u >= 2:
                    act.wait_ge(a_T, u - 1)
                n = key_tiles(u) * P
                nc.scalar.activation(probs[:, u % 2, 0:n], S_PS[u % 2][:, 0:n], ACT.Exp, bias=neg_max[:, u % 2:u % 2 + 1],
                                     accum_out=den[:, u, :]).then_inc(a_exp, 1)

            def probs_T1(u):
                act.wait_ge(a_T, u + 1)
                if u >= 2:
                    act.wait_ge(a_O, u - 1)
                k = key_tiles(u)
                nc.scalar.copy(pt1[:, u % 2, 0:k, :], PT_PS[:, 0:k * P].rearrange("p (i q) -> p i q", i=k)).then_inc(a_Tc, 1)

            def x_high(c):
                act.wait_ge(n_Tc, 3 + c)
                nc.scalar.copy(xTh[:, 512 * c:512 * c + 512], xT[:, 512 * c:512 * c + 512]).then_inc(f1_xh, 1)

            def high_weights(e, s, w):
                act.wait_ge(f1_wT, e * 2 + (w + 1))
                nc.scalar.copy((w1Th, w2Th)[w][:, s, :], bank(w)).then_inc(f1_wh, 1)

            def biases(e, s):
                nc.scalar.copy(b1c[:, s, :], b1T[:, at(e * FT, FT)]).then_inc(f1_b1, 1)

            def attention_inputs(c):
                act.wait_ge(l1_T, 2 * c + 1)
                nc.scalar.copy(xT[:, 512 * c:512 * c + 512], bank(6)).then_inc(l1_Tc, 1)
                act.wait_ge(l1_T, 2 * c + 2)
                nc.scalar.copy(normT[:, 512 * c:512 * c + 512], bank(7)).then_inc(l1_Tc, 1)
                act.wait_ge(l1_q, c + 1)
                nc.scalar.activation(q1T[:, 512 * c:512 * c + 512], bank(5), ACT.Copy, scale=SCALE1).then_inc(l1_qc, 1)
                act.wait_ge(l1_zb, c + 1)
                v = alpha[:, 4 * c:4 * c + 4, :]
                nc.scalar.activation(v, v, ACT.Tanh, scale=0.5).then_inc(l1_al, 1)

            attention_inputs(0)
            exp1(0)
            attention_inputs(1)
            for u in range(NT - 1):
                exp1(u + 1)
                probs_T1(u)
            norm_T(2, 0, bank(1))
            x_high(0)
            high_weights(0, 0, 0)
            probs_T1(NT - 1)
            high_weights(0, 0, 1)
            nc.scalar.activation(gelu_first[:, :], b1T[:, 0:FT], ACT.Gelu).then_inc(f1_g0, 1)

            def hidden(e, s, c, g, static, tiles=range(FT)):
                for f in tiles:
                    m = e * 8 + (4 * c + f)
                    act.wait_ge(f1_U, m + 1)
                    if not static or m >= FT:
                        act.wait_ge(f1_hl, m - (FT - 1))
                    nc.scalar.activation(hf[:, f, :], bank(hidden_bank(g, f)), ACT.Gelu,
                                         bias=b1c[:, s, f:f + 1]).then_inc(f1_gelu, 1)

            def expert(e, s, first=False, last=False):
                g, g1 = (2 * s, 2 * s + 1) if first else (None, None)
                biases(e, s)
                act.wait_ge(f1_b1, e + 1)
                hidden(e, s, 0, g, first, range(2))
                if first and s == 1:
                    gate_tanh(1)
                hidden(e, s, 0, g, first, range(2, FT))
                if first and s == 0:
                    norm_T(3, 1, bank(7))
                    x_high(1)
                if first and s == 1:
                    act.wait_ge(f1_gT, 1)
                    nc.scalar.copy(gT[:, :], ps[0:NT * E, 7, 0:P]).then_inc(f1_gTc, 1)
                if not last:
                    high_weights(e + 1, 1 - s, 0)
                    high_weights(e + 1, 1 - s, 1)
                hidden(e, s, 1, g1, first)
            for s in range(2):
                expert(s, s, first=True)
            with act.Fori(1, E // 2 - 1) as i:
                for s in range(2):
                    expert(i * 2 + s, s)
            for s in range(2):
                expert(E - 2 + s, s, last=s == 1)

        @block.vector
        def _(dve):
            chain = [0]

            def step(ins):
                chain[0] += 1
                ins.then_inc(s_v, 1)

            def settle():
                dve.wait_ge(s_v, chain[0])

            def link(ins):
                step(ins)
                settle()

            def stats_of(src, i):
                step(nc.vector.bn_stats(stats[:, i, :], src))

            def variances(lo, hi, eps, s):
                settle()
                for i in range(lo, hi):
                    step(nc.vector.bn_aggr(mv[:, i, :], stats[:, i, :]))
                settle()
                nc.vector.tensor_scalar(var_e[:, lo:hi], mv[:, lo:hi, 1], eps, None, ALU.add).then_inc(s, 1)

            def key_stats(b):
                for j in range(QT):
                    stats_of(x_cur[:, QT * b + j, :], b * KT + CT + j)
                dve.wait_ge(d_ctx[b], 16)
                for i in range(CT):
                    stats_of(ctx_sb[:, b, i, :], b * KT + i)
                variances(b * KT, (b + 1) * KT, LN_EPS, s_ve)

            def latents_second_norm(b):
                k, t = b * KT + CT, tmp8[:, QT * b:QT * b + QT]
                dve.wait_ge(s_r1, b + 1)
                link(nc.vector.tensor_tensor(t, mv[:, k:k + QT, 1], rstd[:, k:k + QT], ALU.mult))
                link(nc.vector.tensor_tensor(t, t, rstd[:, k:k + QT], ALU.mult))
                nc.vector.tensor_scalar(t, t, LN_EPS, None, ALU.add).then_inc(s_we, 1)

            def latents_rstd(b):
                k = b * KT + CT
                dve.wait_ge(s_r2, b + 1)
                link(nc.vector.tensor_tensor(rstd[:, k:k + QT], rstd[:, k:k + QT], rstd2[:, QT * b:QT * b + QT], ALU.mult))

            def key_source(b, i):
                return ctx_sb[:, b, i, :] if i < CT else x_cur[:, QT * b + i - CT, :]

            def centre_first_keys():
                dve.wait_ge(d_ln, 64)
                for i in range(KT):
                    step(nc.vector.scalar_tensor_tensor(kvf[:, 0, i, :], key_source(0, i), mv[:, i, 0:1],
                                                        ln_rows[:, 2 * (i // CT), :], ALU.subtract, ALU.mult))

            def normalise_first_keys():
                def tile(i):
                    return nc.vector.scalar_tensor_tensor(kvf[:, 0, i, :], kvf[:, 0, i, :], rstd[:, i:i + 1],
                                                          ln_rows[:, 2 * (i // CT) + 1, :], ALU.mult, ALU.add)
                settle()
                for i in range(CT - 1):
                    tile(i)
                tile(CT - 1).then_inc(s_kv0, 1)
                latents_rstd(0)
                tile(CT)
                tile(CT + 1).then_inc(s_kv0, 1)

            def normalise_keys(b):
                def tile(i):
                    k = b * KT + i
                    return nc.vector.tensor_scalar(kvf[:, b, i, :], key_source(b, i), mv[:, k, 0:1], rstd[:, k:k + 1],
                                                   ALU.subtract, ALU.mult)
                for i in range(CT - 1):
                    tile(i)
                tile(CT - 1).then_inc(s_xhat, 1)
                latents_rstd(b)
                tile(CT)
                tile(CT + 1).then_inc(s_xhat, 1)

            def head_weights_low(p):
                dve.wait_ge(s_abh, p + 1)
                nc.vector.tensor_tensor(ab_all[:, 2 * p:2 * p + 2, 1::2, :], AB_PS[p % 2],
                                        ab_all[:, 2 * p:2 * p + 2, 0::2, :], ALU.subtract).then_inc(s_abl, 1)

            def keys_T_low(b):
                for k in range(2):
                    keys_part_low(b, k)

            def keys_part_low(b, k):
                dve.wait_ge(s_kth, 2 * b + k + 1)
                lo, hi = KEY_PARTS[k]
                nc.vector.tensor_tensor(ktl[:, b, lo:hi], bank(keys_bank(b, k), 0, hi - lo), kth[:, b, lo:hi],
                                        ALU.subtract).then_inc(s_ktl, 1)

            def queries_low(n, k):
                dve.wait_ge(s_qkh, n + 1)
                nc.vector.scalar_tensor_tensor(qkl[:, k % 2, :], QK_PS, HEAD_SCALE, qkh[:, k % 2, :],
                                               ALU.mult, ALU.subtract).then_inc(s_qkl, 1)

            dve.wait_ge(d_x, 16)
            key_stats(0)
            key_stats(1)
            centre_first_keys()
            latents_second_norm(0)
            normalise_first_keys()
            latents_second_norm(1)
            head_weights_low(0)
            key_stats(2)
            normalise_keys(1)
            head_weights_low(1)
            keys_T_low(0)
            latents_second_norm(2)
            key_stats(3)
            head_weights_low(2)
            normalise_keys(2)
            head_weights_low(3)
            keys_T_low(1)
            latents_second_norm(3)
            head_weights_low(4)
            normalise_keys(3)
            head_weights_low(5)
            keys_T_low(2)
            head_weights_low(6)
            queries_low(0, 0)
            head_weights_low(7)
            keys_T_low(3)

            def maximum(n, j, first):
                dve.wait_ge(s_S, n * 2 + (j + 1))
                if not first:
                    dve.wait_ge(s_exp, n * 2 + (j - 1))
                nc.vector.tensor_reduce(neg_max[:, j:j + 1], S_PS[j][:, 0:NK], op=ALU.max, axis=AX.X,
                                        negate=True).then_inc(s_max, 1)

            def probs_T_low(n, k, j):
                dve.wait_ge(s_pth, n * 2 + (j + 1))
                q = slice(j * P, j * P + P)
                nc.vector.tensor_tensor(ptl[:, k % 2, :, q], PT_PS[:, 0:NK].rearrange("p (i q) -> p i q", i=KT),
                                        pth[:, k % 2, :, q], ALU.subtract).then_inc(s_ptl, 1)

            def attended_low(n, k):
                dve.wait_ge(s_yh, n + 1)
                nc.vector.tensor_tensor(yl[:, k % 2, :], Y_PS, yh[:, k % 2, :], ALU.subtract).then_inc(s_yl, 1)

            def accumulate(n, k, first):
                b, d = k % B, slice(2 * (k % 8), 2 * (k % 8) + 2)
                dve.wait_ge(s_exp, n * 2 + 2)
                nc.vector.reciprocal(rden[:, d, 0], den[:, d, 0]).then_inc(s_rden, 1)
                dve.wait_ge(s_O, n + 1)
                dve.wait_ge(s_rden, n + 1)
                for j in range(QT):
                    if not first:
                        dve.wait_ge(s_acc, n * 2 + (j - 2 * B + 1))
                    t = x_cur[:, QT * b + j, :]
                    nc.vector.scalar_tensor_tensor(t, O_PS[:, j * P:(j + 1) * P], rden[:, 2 * (k % 8) + j, :], t,
                                                   ALU.mult, ALU.add).then_inc(s_acc, 1)

            def item(n, k, start=3, first=False, last=False):
                maximum(n, 0, start == 0)
                if start >= 1:
                    probs_T_low(n - 1, k - 1, 1)
                if start >= 2:
                    attended_low(n - 2, k)
                if not last:
                    queries_low(n + 1, k + 1)
                maximum(n, 1, start == 0)
                probs_T_low(n, k, 0)
                if start >= 2:
                    accumulate(n - 2, (k - 2) % 8, first and k - 2 < B)

            for k in range(8):
                item(k, k, start=min(k, 3), first=True)
            with dve.Fori(1, ITEMS // 8 - 1) as p:
                for k in range(8):
                    item(p * 8 + k, k)
            for k in range(8):
                item(ITEMS - 8 + k, k, last=k == 7)

            def half_variances(c, eps, s):
                variances(4 * c, 4 * c + 4, eps, s)

            def tile_pair_stats(n):
                dve.wait_ge(s_acc, 2 * n + 2)
                for j in range(QT):
                    stats_of(x_cur[:, QT * (n % B) + j, :], QT * (n % B) + j)

            probs_T_low(ITEMS - 1, 7, 1)
            for n in (ITEMS - 4, ITEMS - 3):
                tile_pair_stats(n)
            attended_low(ITEMS - 2, 6)
            half_variances(0, LN_EPS, n_ve)
            accumulate(ITEMS - 2, 6, False)
            attended_low(ITEMS - 1, 7)
            tile_pair_stats(ITEMS - 2)
            accumulate(ITEMS - 1, 7, False)
            tile_pair_stats(ITEMS - 1)
            half_variances(1, LN_EPS, n_ve)

            def normalise(c, src, s):
                for t in range(4 * c, 4 * c + 4):
                    nc.vector.tensor_scalar(xn[:, t, :], src[:, t, :], mv[:, t, 0:1], rstd[:, t:t + 1],
                                            ALU.subtract, ALU.mult).then_inc(s, 1)

            for c in range(2):
                dve.wait_ge(n_r, c + 1)
                normalise(c, x_cur, n_xn)

            def route(k, lg):
                dve.wait_ge(g_mm, k + 1)
                if k:
                    dve.wait_ge(d_rows1, 80)
                    link(nc.vector.tensor_tensor(logits[:, :, :], lg, rb_row[:, :].unsqueeze(1).broadcast_to([P, NT, E]), ALU.add))
                else:
                    link(nc.vector.tensor_copy(logits[:, :, :], lg))
                for t in range(NT):
                    step(nc.vector.max(top8[:, t, :], logits[:, t, :]))
                settle()
                nc.vector.tensor_tensor(g12[:, 0, :], top8[:, :, 0], top8[:, :, 1], ALU.subtract).then_inc(g_d, 1)
                for t in range(NT):
                    step(nc.vector.max_index(idx8[:, t, :], top8[:, t, :], logits[:, t, :]))
                dve.wait_ge(g_e, k + 1)
                step(nc.vector.tensor_scalar(g12[:, 0, :], g12[:, 2, :], 0.5, 0.5, ALU.mult, ALU.add))
                step(nc.vector.tensor_scalar(g12[:, 1, :], g12[:, 2, :], -0.5, 0.5, ALU.mult, ALU.add))
                settle()
                link(nc.vector.tensor_copy(idxf[:, :, :], idx8[:, :, :]))
                for r in range(2):
                    step(nc.vector.tensor_tensor(hit[:, r, :, :], iota_e[:, :, :],
                                                 idxf[:, :, r:r + 1].broadcast_to([P, NT, E]), ALU.is_equal))
                settle()
                for r in range(2):
                    step(nc.vector.tensor_tensor(hit[:, r, :, :], hit[:, r, :, :],
                                                 g12[:, r, :].unsqueeze(2).broadcast_to([P, NT, E]), ALU.mult))
                settle()
                nc.vector.tensor_tensor(gates[:, :, :], hit[:, 0, :, :], hit[:, 1, :, :], ALU.add).then_inc(g_ok, 1)
                dve.wait_ge(g_ok, k + 1)

            for c in range(2):
                dve.wait_ge(e0_mc, c + 1)
                nc.vector.tensor_tensor(moe0l[:, 4 * c:4 * c + 4, :], bank(2 + c).rearrange("p (e n) -> p e n", e=4),
                                        moe0h[:, 4 * c:4 * c + 4, :], ALU.subtract).then_inc(e0_ml, 1)
            for c in range(2):
                v = slice(512 * c, 512 * c + 512)
                dve.wait_ge(e0_xh, c + 1)
                nc.vector.tensor_tensor(xTl[:, v], xT[:, v], xTh[:, v], ALU.subtract).then_inc(e0_xl, 1)
            dve.wait_ge(s_const, 6)
            route(0, bank(6, 0, NT * E).rearrange("p (t e) -> p t e", t=NT))

            def add_pair(k, experts=range(E_VECTOR)):
                done = 2 * E_VECTOR * k + 2 * experts[0]
                for e in experts:
                    for t in (2 * k, 2 * k + 1):
                        if e == 0:
                            dve.wait_ge(f0_mm, 2 * t + 1)
                        else:
                            dve.wait_ge(f0_c, done - 1)
                        if e == 4:
                            dve.wait_ge(f0_s, 4 * t + 1)
                            nc.vector.tensor_tensor(x_cur[:, t, :], x_cur[:, t, :], scaled[:, t % 2, 0, :], ALU.add).then_inc(f0_c, 1)
                        else:
                            nc.vector.scalar_tensor_tensor(x_cur[:, t, :], bank(bank0(t, 0), e * D, (e + 1) * D),
                                                           gates[:, t, e:e + 1], x_cur[:, t, :],
                                                           ALU.mult, ALU.add).then_inc(f0_c, 1)
                        done += 1

            def summed_stats(t):
                dve.wait_ge(f0_x, t + 1)
                stats_of(x_cur[:, t, :], t)

            def rms(c):
                h, r = tmp8[:, 4 * c:4 * c + 4], rstd[:, 4 * c:4 * c + 4]
                dve.wait_ge(l1_r, c + 1)
                link(nc.vector.tensor_tensor(h, mv[:, 4 * c:4 * c + 4, 1], r, ALU.mult))
                link(nc.vector.tensor_tensor(h, h, r, ALU.mult))
                nc.vector.tensor_scalar(h, h, RMS_EPS, None, ALU.add).then_inc(l1_we, 1)

            def normed_half(c):
                dve.wait_ge(l1_r2, c + 1)
                dve.wait_ge(l1_hid, 4 * c + 4)
                for t in range(4 * c, 4 * c + 4):
                    nc.vector.scalar_tensor_tensor(normed[:, t, :], xn[:, t, :], rstd2[:, t:t + 1], rows1[:, 0, :],
                                                   ALU.mult, ALU.mult).then_inc(l1_nrm, 1)

            def gate_bias(c):
                dve.wait_ge(l1_z, c + 1)
                nc.vector.tensor_tensor(alpha[:, 4 * c:4 * c + 4, :], bank(4).rearrange("p (t n) -> p t n", t=4),
                                        rows1[:, 1, :].unsqueeze(1).broadcast_to([P, 4, D]), ALU.add).then_inc(l1_zb, 1)
                v = x_cur[:, 4 * c:4 * c + 4, :]
                step(nc.vector.tensor_tensor(v, v, xn[:, 4 * c:4 * c + 4, :], ALU.add))

            def alpha_half(c):
                dve.wait_ge(l1_al, c + 1)
                v = alpha[:, 4 * c:4 * c + 4, :]
                step(nc.vector.tensor_scalar(v, v, 0.5, 0.5, ALU.mult, ALU.add))

            add_pair(0)
            add_pair(1)
            summed_stats(0)
            summed_stats(1)
            add_pair(2)
            summed_stats(2)
            summed_stats(3)
            half_variances(0, LN_EPS, l1_ve)
            add_pair(3, range(4))
            rms(0)
            normalise(0, x_cur, l1_hid)
            dve.wait_ge(d_rows1, 80)
            normed_half(0)
            add_pair(3, range(4, E_VECTOR))
            summed_stats(4)
            summed_stats(5)
            gate_bias(0)
            summed_stats(6)
            summed_stats(7)
            half_variances(1, LN_EPS, l1_ve)
            alpha_half(0)
            rms(1)
            normalise(1, x_cur, l1_hid)

            def max1(u):
                dve.wait_ge(a_S, u + 1)
                if u >= 2:
                    dve.wait_ge(a_exp, u - 1)
                n = key_tiles(u) * P
                diagonal = S_PS[u % 2][:, n - P:n]
                link(nc.vector.tensor_tensor(diagonal, diagonal, causal[:, :], ALU.add))
                nc.vector.tensor_reduce(neg_max[:, u % 2:u % 2 + 1], S_PS[u % 2][:, 0:n], op=ALU.max, axis=AX.X,
                                        negate=True).then_inc(a_max, 1)

            def finish1(u):
                dve.wait_ge(a_exp, u + 1)
                link(nc.vector.reciprocal(rden[:, u, :], den[:, u, :]))
                dve.wait_ge(a_O, u + 1)
                link(nc.vector.scalar_tensor_tensor(acc4[:, u, :], bank(6 + u % 2, 0, D), rden[:, u, :], xn[:, u, :],
                                                    ALU.mult, ALU.subtract))
                link(nc.vector.tensor_tensor(acc4[:, u, :], acc4[:, u, :], alpha[:, u, :], ALU.mult))
                nc.vector.tensor_tensor(x_cur[:, u, :], x_cur[:, u, :], acc4[:, u, :], ALU.add).then_inc(a_fin, 1)
                dve.wait_ge(a_fin, u + 1)
                stats_of(x_cur[:, u, :], u)

            def x_low(c):
                dve.wait_ge(f1_xh, c + 1)
                nc.vector.tensor_tensor(xTl[:, 512 * c:512 * c + 512], xT[:, 512 * c:512 * c + 512],
                                        xTh[:, 512 * c:512 * c + 512], ALU.subtract).then_inc(f1_xl, 1)

            def low_weights(e, s, w):
                hi, lo = ((w1Th, w1Tl), (w2Th, w2Tl))[w]
                dve.wait_ge(f1_wh, e * 2 + (w + 1))
                nc.vector.tensor_tensor(lo[:, s, :], bank(w), hi[:, s, :], ALU.subtract).then_inc(f1_wl, 1)

            max1(0)
            normed_half(1)
            max1(1)
            gate_bias(1)
            alpha_half(1)
            settle()
            for u in range(NT):
                if u + 2 < NT:
                    max1(u + 2)
                if u == NT - 1:
                    x_low(0)
                    low_weights(0, 0, 0)
                    low_weights(0, 0, 1)
                finish1(u)
                if u == 3:
                    half_variances(0, LN_EPS, n_ve)
                if u == 4:
                    dve.wait_ge(n_r, 3)
                    normalise(0, x_cur, n_xn)

            def low_hidden(e, c, static):
                if not (static and e == 0):
                    dve.wait_ge(f1_V, e * 4 + (2 * c - 2))
                for pair in range(0, FT, 2):
                    for f in (pair, pair + 1):
                        dve.wait_ge(f1_gelu, e * 8 + (4 * c + f + 1))
                        nc.vector.tensor_copy(hh[:, c, f, :], hf[:, f, :]).then_inc(f1_hh, 1)
                    for f in (pair, pair + 1):
                        dve.wait_ge(f1_hh, e * 8 + (4 * c + f + 1))
                        nc.vector.tensor_tensor(hl[:, c, f, :], hf[:, f, :], hh[:, c, f, :], ALU.subtract).then_inc(f1_hl, 1)

            def add_expert(e, c, first, tiles=range(4)):
                for q in tiles:
                    t = 4 * c + q
                    if q % 2 == 0:
                        dve.wait_ge(f1_V, e * 4 + (2 * c + q // 2 + 1))
                    if not first:
                        dve.wait_ge(f1_acc, e * 8 + (t - 7))
                    nc.vector.scalar_tensor_tensor(
                        acc4[:, t, :], bank(4 + q // 2, (q % 2) * D, (q % 2 + 1) * D), gates[:, t, at(e, 1)],
                        xn[:, t, :] if first else acc4[:, t, :], ALU.mult, ALU.add).then_inc(f1_acc, 1)

            def add_b2(c):
                dve.wait_ge(f1_b2, c + 1)
                if c == 0:
                    dve.wait_ge(f1_acc, 4)
                else:
                    dve.wait_ge(f1_acc, 8)
                v = acc4[:, 4 * c:4 * c + 4, :]
                nc.vector.tensor_tensor(v, v, bank(7).rearrange("p (t n) -> p t n", t=4), ALU.add).then_inc(f1_b2c, 1)
                dve.wait_ge(f1_b2c, c + 1)

            def expert(e, s, static=False, last=False):
                low_hidden(e, 0, static)
                if static and s == 0:
                    x_low(1)
                else:
                    add_expert(e - 1, 1, static)
                if static and s == 1:
                    add_b2(0)
                if not last:
                    low_weights(e + 1, 1 - s, 0)
                    low_weights(e + 1, 1 - s, 1)
                low_hidden(e, 1, static)
                if static and s == 0:
                    route(1, bank(7, 0, NT * E).rearrange("p (t e) -> p t e", t=NT))
                if static and s == 1:
                    add_b2(1)
                add_expert(e, 0, static and s == 0)

            half_variances(1, LN_EPS, n_ve)
            dve.wait_ge(n_r, 4)
            normalise(1, x_cur, n_xn)
            for s in range(2):
                expert(s, s, static=True)
            with dve.Fori(1, E // 2 - 1) as i:
                for s in range(2):
                    expert(i * 2 + s, s)
            for s in range(2):
                expert(E - 2 + s, s, last=s == 1)

            def last_stats(t):
                dve.wait_ge(f1_acc, (E - 1) * NT + t + 1)
                stats_of(acc4[:, t, :], t)

            def last_norm(lo, hi, count):
                dve.wait_ge(n_r, count)
                for t in range(lo, hi):
                    nc.vector.scalar_tensor_tensor(acc4[:, t, :], acc4[:, t, :], mv[:, t, 0:1], rows1[:, 2, :],
                                                   ALU.subtract, ALU.mult).then_inc(z_s, 1)
                for t in range(lo, hi):
                    dve.wait_ge(z_s, t + 1)
                    nc.vector.scalar_tensor_tensor(acc4[:, t, :], acc4[:, t, :], rstd[:, t:t + 1], xb[:, t, :],
                                                   ALU.mult, ALU.add).then_inc(z_fin, 1)

            for t in range(4):
                last_stats(t)
            half_variances(0, LN2_EPS, n_ve)
            dve.wait_ge(z_xb, 1)
            last_norm(0, 4, 5)
            for q in (0, 2):
                add_expert(E - 1, 1, False, (q, q + 1))
                last_stats(4 + q)
                last_stats(5 + q)
                variances(4 + q, 6 + q, LN2_EPS, n_ve)
            last_norm(4, 6, 6)
            last_norm(6, 8, 7)

        @block.tensor
        def _(pe):
            mm = nc.tensor.matmul

            def transpose(dst, src):
                return nc.tensor.transpose(dst, src, ident[:, :])

            pe.wait_ge(s_const, 3)
            def keep_clock(n, free_bank):
                for _ in range(n):
                    transpose(bank(free_bank, 0, P), ident[:, :])

            keep_clock(WARM_UP, 7)
            pe.wait_ge(d_w_first, 48)

            def weights_T(p):
                if p == FIRST_PAIRS:
                    pe.wait_ge(d_w_rest, 48)
                if p >= 2:
                    pe.wait_ge(s_wT, p - 1)
                c = p * P
                transpose(bank(p % 2, 0, 128), wq_sb[:, c:c + P])
                transpose(bank(p % 2, 128, 256), wkv_sb[:, c:c + P])
                transpose(bank(p % 2, 256, 384), wkv_sb[:, HEADS * DH + c:HEADS * DH + c + P]).then_inc(s_wT_mm, 1)

            def weights_AB(p):
                pe.wait_ge(s_wT, p + 1)
                if p >= 2:
                    pe.wait_ge(s_abl, p - 1)
                for h in range(2):
                    r = slice(DH * h, DH * h + DH)
                    wT = wqkvT[r, p % 2, :, :]
                    mm(AB_PS[p % 2][:, h, 0, :], wT[:, 0, :], wT[:, 1, :], start=True, stop=True)
                    last = mm(AB_PS[p % 2][:, h, 1, :], wT[:, 2, :], wout_sb[r, p, :], start=True, stop=True)
                last.then_inc(s_ab_mm, 1)

            def keys_T(b):
                for k, (lo, hi) in enumerate(KEY_PARTS):
                    wait_keys(pe, b, k + 1)
                    if b:
                        pe.wait_ge(s_ktl, 2 * b - 1 + k)
                    for i in range(lo // P, hi // P):
                        last = transpose(bank(keys_bank(b, k), i * P - lo, i * P - lo + P), kvf[:, b, i, :])
                    last.then_inc(s_kt_mm, 1)

            def queries(n, k, heads):
                hs, b = (k // B) % 2, k % B
                if b == 0:
                    pe.wait_ge(s_ab, heads + (k // B + 1))
                lat = slice(SC, NK)
                mm(QK_PS, ab[:, hs, 0, :], kth[:, b, lat], start=True, stop=False)
                mm(QK_PS, ab[:, hs, 0, :], ktl[:, b, lat], start=False, stop=False)
                mm(QK_PS, ab[:, hs, 1, :], kth[:, b, lat], start=False, stop=True).then_inc(s_qk, 1)

            weights_T(0)
            for p in range(NPAIR):
                if p + 1 < NPAIR:
                    weights_T(p + 1)
                else:
                    pe.wait_ge(s_ktl, 2 * B - 2)
                    queries(0, 0, 0)
                weights_AB(p)
                if p % 2 and p + 1 < NPAIR:
                    keys_T(p // 2)

            def scores(n, k, j, first):
                b = k % B
                if j == 0:
                    pe.wait_ge(s_qkh, n + 1)
                    pe.wait_ge(s_qkl, n + 1)
                if not first:
                    pe.wait_ge(s_exp, n * 2 + (j - 1))
                q = slice(j * P, j * P + P)
                for w, keys, start in ((qkh, kth, True), (qkh, ktl, False), (qkl, kth, False)):
                    for lo, hi in ((0, 512), (512, NK)):
                        last = mm(S_PS[j][:, lo:hi], w[:, k % 2, q], keys[:, b, lo:hi], start=start,
                                  stop=w is qkl, skip_group_check=True)
                last.then_inc(s_S, 1)

            def probs_T(n, j, first):
                pe.wait_ge(s_exp, n * 2 + (j + 1))
                if not first:
                    pe.wait_ge(s_ptl, n * 2 + j)
                for i in range(KT):
                    last = transpose(PT_PS[:, i * P:(i + 1) * P], probs[:, j, i * P:(i + 1) * P])
                last.then_inc(s_T, 1)

            def attend(n, k, half, start):
                b = k % B
                if half == 0:
                    pe.wait_ge(s_ptl, n * 2 + 2)
                    if start < B:
                        pe.wait_ge(s_kvl, start + 1)
                    if start:
                        pe.wait_ge(s_yl, n)
                for i in range(3 * half, 3 * half + 3):
                    mm(Y_PS, kvh[:, b, i, :], pth[:, k % 2, i, :], start=i == 0, stop=False, skip_group_check=True)
                    mm(Y_PS, kvh[:, b, i, :], ptl[:, k % 2, i, :], start=False, stop=False, skip_group_check=True)
                    last = mm(Y_PS, kvl[:, b, i, :], pth[:, k % 2, i, :], start=False, stop=i == KT - 1, skip_group_check=True)
                if half:
                    last.then_inc(s_Y, 1)

            def project(n, k, start):
                hs = (k // B) % 2
                pe.wait_ge(s_yl, n + 1)
                if start:
                    pe.wait_ge(s_acc, n * 2)
                for j in range(QT):
                    o, q = O_PS[:, j * P:(j + 1) * P], slice(j * P, j * P + P)
                    mm(o, yh[:, k % 2, q], ab[:, hs, 2, :], start=True, stop=False)
                    mm(o, yh[:, k % 2, q], ab[:, hs, 3, :], start=False, stop=False)
                    last = mm(o, yl[:, k % 2, q], ab[:, hs, 2, :], start=False, stop=True)
                last.then_inc(s_O, 1)

            def item(n, k, heads, start=B + 2, last=False):
                scores(n, k, 0, start == 0)
                if start == 0:
                    pe.wait_ge(s_abl, NPAIR)
                    keys_T(B - 1)
                if start >= 1:
                    probs_T(n - 1, 1, False)
                if start >= 2:
                    attend(n - 2, (k - 2) % 8, 1, start - 2)
                if not last:
                    if start >= 3:
                        pe.wait_ge(s_acc, n * 2 - 4)
                    queries(n + 1, k + 1, heads)
                scores(n, k, 1, start == 0)
                if start == 0:
                    pe.wait_ge(s_ktl, 2 * B)
                probs_T(n, 0, start == 0)
                if start >= 1:
                    attend(n - 1, (k - 1) % 8, 0, start - 1)
                if start >= 2:
                    pe.wait_ge(s_qkl, n + (1 if last else 2))
                    project(n - 2, (k - 2) % 8, start - 2)

            pe.wait_ge(s_wT, NPAIR)
            for k in range(8):
                item(k, k, 0, start=min(k, B + 2))
            with pe.Fori(1, ITEMS // 8 - 1) as p:
                for k in range(8):
                    item(p * 8 + k, k, p * 2)
            for k in range(8):
                item(ITEMS - 8 + k, k, HEADS - 2, last=k == 7)

            def w_out_T(e):
                if e >= 2:
                    pe.wait_ge(e0_wTc, e - 1)
                for f in range(FT):
                    last = transpose(bank(e % 2, f * P, (f + 1) * P), w_out_sb[:, e, f * P:(f + 1) * P])
                last.then_inc(e0_wT, 1)

            def w_in_out(e):
                if e + 1 < E:
                    w_out_T(e + 1)
                pe.wait_ge(e0_wTc, e + 1)
                for f in range(FT):
                    last = mm(bank(2 + e // 4, (e % 4) * D, (e % 4 + 1) * D), w_in_sb[:, e, f, :], woT[:, e % 2, f, :],
                              start=f == 0, stop=f == FT - 1)
                last.then_inc(e0_m, 1)

            probs_T(ITEMS - 1, 1, False)
            attend(ITEMS - 2, 6, 1, B)
            pe.wait_ge(d_win, 16)
            pe.wait_ge(d_wo0, 16)
            w_out_T(0)
            w_in_out(0)
            w_in_out(1)
            attend(ITEMS - 1, 7, 0, B)
            project(ITEMS - 2, 6, B)
            w_in_out(2)
            attend(ITEMS - 1, 7, 1, B)
            w_in_out(3)
            project(ITEMS - 1, 7, B)
            for e in range(4, E):
                w_in_out(e)
            pe.wait_ge(d_small, 48)
            pe.wait_ge(d_qk1w, 48)
            nc.tensor.transpose(bank(6, 0, E), small[:, 0:D], ident[0:E, 0:E])
            nc.tensor.transpose(bank(6, E, 2 * E), small[:, D:2 * D], ident[0:E, 0:E])
            nc.tensor.transpose(bank(6, 16, 16 + E * FT), b1n[:, :], ident[0:E * FT, 0:E * FT])
            transpose(bank(6, 128, 256), qk1w[:, 2, :])
            mm(bank(6, 256, 384), qk1w[:, 0, :], qk1w[:, 1, :], start=True, stop=True).then_inc(c1_mm, 1)

            def norm_T(need, c, dst):
                pe.wait_ge(n_xn, need)
                for q in range(4):
                    last = transpose(dst[:, q * P:(q + 1) * P], xn[:, 4 * c + q, :])
                last.then_inc(n_T, 1)

            def router(k, dst):
                for t in range(NT):
                    if t % 4 == 0:
                        pe.wait_ge(n_Tc, 2 * k + t // 4 + 1)
                    last = mm(dst[:, t * E:(t + 1) * E], xT[:, t * P:(t + 1) * P], wgT[:, k, :], start=True, stop=True)
                last.then_inc(g_mm, 1)

            pe.wait_ge(e0_wTc, E)
            norm_T(4, 0, bank(0))
            norm_T(8, 1, bank(1))
            pe.wait_ge(c1_c, 4)
            router(0, bank(6))
            pe.wait_ge(e0_ml, 2)
            pe.wait_ge(e0_xl, 2)
            pe.wait_ge(s_acc, 2 * ITEMS)

            def banks0_free(t):
                pe.wait_ge(f0_c, 2 * E_VECTOR * (t // 2 + 1))
                pe.wait_ge(f0_s, 4 * (t + 1))

            def experts0(t):
                tok = slice(t * P, (t + 1) * P)
                for c in range(2):
                    if t == 1 and c == 0:
                        pe.wait_ge(g_d, 1)
                    if t >= 4 and c == 0:
                        banks0_free(t - 4)
                    high, low = (m[:, 4 * c:4 * c + 4, :].rearrange("p e n -> p (e n)") for m in (moe0h, moe0l))
                    dst = bank(bank0(t, c))
                    mm(dst, xTh[:, tok], high, start=True, stop=False)
                    mm(dst, xTh[:, tok], low, start=False, stop=False)
                    mm(dst, xTl[:, tok], high, start=False, stop=True).then_inc(f0_mm, 1)

            def norms_T1(c):
                if c:
                    pe.wait_ge(l1_Tc, 2)
                else:
                    banks0_free(5)
                for w, (src, s) in enumerate(((xn, l1_hid), (normed, l1_nrm))):
                    keep_clock(((14, 6), (4, 12))[c][w], 6 + w)
                    pe.wait_ge(s, 4 * c + 4)
                    for q in range(4):
                        last = transpose(bank(6 + w, q * P, (q + 1) * P), src[:, 4 * c + q, :])
                    last.then_inc(l1_T, 1)

            def gate_and_queries(c):
                pe.wait_ge(l1_Tc, 2 * c + 1)
                if c:
                    pe.wait_ge(l1_zb, 1)
                else:
                    pe.wait_ge(c1_c, B + 4)
                for q in range(4):
                    t = 4 * c + q
                    last = mm(bank(4, q * D, (q + 1) * D), xT[:, t * P:(t + 1) * P], gwT[:, :], start=True, stop=True)
                last.then_inc(l1_z, 1)
                pe.wait_ge(l1_Tc, 2 * c + 2)
                if c:
                    pe.wait_ge(l1_qc, 1)
                mm(bank(5), A1[:, :], normT[:, 512 * c:512 * c + 512], start=True, stop=True).then_inc(l1_q, 1)

            def scores1(u):
                b, sp = u // 2, S_PS[u % 2]
                if u >= 2:
                    pe.wait_ge(a_exp, u - 1)
                else:
                    banks0_free(6 + u)
                pe.wait_ge(l1_qc, u // 4 + 1)
                mm(sp[:, 0:SC], q1T[:, u * P:(u + 1) * P], ctxT[:, b, :], start=True, stop=True)
                n = key_tiles(u) * P - SC
                mm(sp[:, SC:SC + n], q1T[:, u * P:(u + 1) * P], normT[:, b * SQ:b * SQ + n], start=True, stop=True).then_inc(a_S, 1)

            def probs_T1(u):
                pe.wait_ge(a_exp, u + 1)
                if u == 0:
                    pe.wait_ge(l1_qc, 2)
                    pe.wait_ge(l1_zb, 2)
                else:
                    pe.wait_ge(a_Tc, u)
                for i in range(key_tiles(u)):
                    last = transpose(PT_PS[:, i * P:(i + 1) * P], probs[:, u % 2, i * P:(i + 1) * P])
                last.then_inc(a_T, 1)

            def attend1(u):
                b = u // 2
                pe.wait_ge(a_Tc, u + 1)
                if u >= 2:
                    pe.wait_ge(a_fin, u - 1)
                for i in range(key_tiles(u)):
                    v = ctx_sb[:, b, i, :] if i < CT else normed[:, QT * b + i - CT, :]
                    last = mm(bank(6 + u % 2, 0, D), pt1[:, u % 2, i, :], v, start=i == 0, stop=i == key_tiles(u) - 1)
                last.then_inc(a_O, 1)

            for t in range(NT - 1):
                experts0(t)
            experts0(NT - 1)
            banks0_free(4)
            for b in range(B):
                if b >= 2:
                    pe.wait_ge(c1_c, b + 3)
                for i in range(CT):
                    last = transpose(bank(4 + b % 2, i * P, (i + 1) * P), ctx_sb[:, b, i, :])
                last.then_inc(c1_mm, 1)
            norms_T1(0)
            gate_and_queries(0)
            scores1(0)
            scores1(1)
            norms_T1(1)
            gate_and_queries(1)
            pe.wait_ge(l1_Tc, 4)

            def expert_T(e, s, i, w, first):
                pe.wait_ge((d_w1, d_w2)[w][s], i * 16 + 16)
                if not first:
                    pe.wait_ge(f1_wl, e * 2 + (w - 1))
                for f in range(FT):
                    src = w2n[:, s, f * P:(f + 1) * P] if w else w1n[:, s, f, :]
                    last = transpose(bank(w, f * P, (f + 1) * P), src)
                last.then_inc(f1_wT, 1)

            for u in range(NT):
                if u == NT - 1:
                    pe.wait_ge(a_exp, NT - 1)
                    norm_T(12, 0, bank(1))
                    expert_T(0, 0, 0, 0, True)
                probs_T1(u)
                if u + 2 < NT:
                    scores1(u + 2)
                if u == NT - 1:
                    pe.wait_ge(n_Tc, 3)
                    expert_T(0, 0, 0, 1, True)
                attend1(u)


            def up(e, s, c, g, static):
                if c == 0:
                    pe.wait_ge(f1_wl, e * 2 + 1)
                tok = slice(512 * c, 512 * c + 512)
                for f in range(FT):
                    if not static or 4 * (2 * e + c) + f >= 3:
                        pe.wait_ge(f1_gelu, e * 8 + (4 * c + f - (3 if g is None else 2)))
                    u, fs = bank(hidden_bank(g, f)), slice(f * P, f * P + P)
                    mm(u, w1Th[:, s, fs], xTh[:, tok], start=True, stop=False)
                    mm(u, w1Th[:, s, fs], xTl[:, tok], start=False, stop=False)
                    mm(u, w1Tl[:, s, fs], xTh[:, tok], start=False, stop=True).then_inc(f1_U, 1)

            def down(e, s, c, static):
                if c == 0:
                    pe.wait_ge(f1_wl, e * 2 + 2)
                pe.wait_ge(f1_hl, e * 8 + (4 * c + 4))
                for q in range(4):
                    if q % 2 == 0 and not (static and e == 0 and c == 0):
                        pe.wait_ge(f1_acc, e * 8 + (4 * c + q - 2))
                    o, tok = bank(4 + q // 2, (q % 2) * D, (q % 2 + 1) * D), slice(q * P, q * P + P)
                    for f in range(FT):
                        w = slice(f * D, f * D + D)
                        mm(o, hh[:, c, f, tok], w2Th[:, s, w], start=f == 0, stop=False)
                        mm(o, hh[:, c, f, tok], w2Tl[:, s, w], start=False, stop=False)
                        last = mm(o, hl[:, c, f, tok], w2Th[:, s, w], start=False, stop=f == FT - 1)
                    if q % 2:
                        last.then_inc(f1_V, 1)

            def gates_b2(c):
                pe.wait_ge(f1_gTc, 1)
                if c:
                    pe.wait_ge(f1_b2c, 1)
                mm(bank(7), gT[:, :], b2d[:, 4 * c:4 * c + 4, :].rearrange("p t d -> p (t d)"), start=True, stop=True).then_inc(f1_b2, 1)

            def expert(e, s, i, first=False, last=False):
                g, g1 = (2, 3) if first else (None, None)
                up(e, s, 0, g, first)
                if first:
                    keep_clock(16, 0)
                    pe.wait_ge(g_ok, 2)
                    pe.wait_ge(d_b2, 16 * NT)
                    transpose(ps[0:NT * E, 7, 0:P], gates[:, :, :].rearrange("p t e -> p (t e)")).then_inc(f1_gT, 1)
                down(e - 1, 1 - s, 1, first)
                if first:
                    gates_b2(0)
                if not last:
                    for w in range(2):
                        expert_T(e + 1, 1 - s, i + s, w, False)
                up(e, s, 1, g1, first)
                if first:
                    gates_b2(1)
                down(e, s, 0, first)

            def expert_0():
                up(0, 0, 0, 0, True)
                norm_T(16, 1, bank(7))
                for w in range(2):
                    expert_T(1, 1, 0, w, False)
                keep_clock(18, 4)
                down(0, 0, 0, True)
                pe.wait_ge(f1_xl, 2)
                up(0, 0, 1, 1, True)
                pe.wait_ge(n_Tc, 4)
                router(1, bank(7))

            pe.wait_ge(f1_xl, 1)
            expert_0()
            expert(1, 1, 0, first=True)
            pe.wait_ge(f1_b2c, 2)
            with pe.Fori(1, E // 2 - 1) as i:
                for s in range(2):
                    expert(i * 2 + s, s, i)
            for s in range(2):
                expert(E - 2 + s, s, E // 2 - 1, last=s == 1)
            down(E - 1, 1, 1, False)


_INS = ['x', 'ctx_1024', 'L0_xattn_ln_m_g', 'L0_xattn_ln_m_b', 'L0_xattn_ln_l_g', 'L0_xattn_ln_l_b',
        'L0_xattn_Wq', 'L0_xattn_Wkv', 'L0_xattn_Wout', 'L0_ffn_w_gate', 'L0_ffn_w_in', 'L0_ffn_w_out',
        'L1_xattn_q_w', 'L1_xattn_k_w', 'L1_xattn_norm_w', 'L1_xattn_gate_w', 'L1_xattn_gate_b',
        'L1_ffn_router_w', 'L1_ffn_router_b', 'L1_ffn_w1', 'L1_ffn_b1', 'L1_ffn_w2', 'L1_ffn_b2',
        'L1_ffn_ln_w', 'L1_ffn_ln_b']


def kernel(**inputs):
    import numpy as _np
    import concourse.bacc as _bacc
    from concourse import mybir as _mybir
    from concourse.bass_utils import run_bass_kernel_spmd as _run

    nc = _bacc.Bacc("TRN2", target_bir_lowering=False, num_devices=1)
    arrays, aps = {}, {}
    for name in _INS:
        a = _np.ascontiguousarray(inputs[name])
        arrays[f"in_{name}"] = a
        aps[name] = nc.dram_tensor(f"in_{name}", a.shape, _mybir.dt.from_np(a.dtype), kind="ExternalInput").ap()
    out = nc.dram_tensor("out_0", (B, SQ, D), _mybir.dt.float32, kind="ExternalOutput").ap()
    transformer_program(nc, aps, out)
    r = _run(nc, [arrays], core_ids=[0])
    return r.results[0]["out_0"]
```

```python
import concourse.bass as bass
from concourse import mybir
from contextlib import ExitStack

B, SQ, SC, D = 4, 256, 512, 128
P = 128
NT = B * SQ // P
CT = SC // P
QT = SQ // P
KT = CT + QT
NK = KT * P
HEADS, DH = 16, 64
NPAIR = HEADS // 2
FIRST_PAIRS = 2
WARM_UP = 28
KEY_PARTS = ((0, SC), (SC, NK))
ITEMS = HEADS * B
E, FF = 8, 512
E_VECTOR = 5
FT = FF // P
LN_EPS = 1e-5
RMS_EPS = 1e-6
LN2_EPS = 1e-12
HEAD_SCALE = DH ** -0.5
SCALE1 = D ** -0.5
MASKED = -1e30


def transformer_program(nc, A, out):
    F32, F16, U32 = mybir.dt.float32, mybir.dt.float16, mybir.dt.uint32
    ALU = mybir.AluOpType
    ACT = mybir.ActivationFunctionType
    AX = mybir.AxisListType

    ctx = ExitStack()
    with ctx:
        def sb(name, shape, dt=F32):
            return ctx.enter_context(nc.sbuf_tensor(name, shape, dt))

        def sem(name):
            return ctx.enter_context(nc.semaphore(name))

        def at(start, size):
            return bass.ds(start, size)

        ident = sb("ident", [P, P])
        causal = sb("causal", [P, P])
        minus_half = sb("minus_half", [P, B * KT])
        iota_e = sb("iota_e", [P, NT, E])
        x_cur = sb("x_cur", [P, NT, D])
        ctx_sb = sb("ctx_sb", [P, B, CT, D])
        ln_rows = sb("ln_rows", [P, 4, D])
        kvf = sb("kvf", [P, B, KT, D])
        kv = sb("kv", [P, 4, B * NK], F16)
        kvh, kvl = (kv[:, i, :].rearrange("p (b i d) -> p b i d", b=B, i=KT) for i in range(2))
        kth, ktl = (kv[:, i, :].rearrange("p (b n) -> p b n", b=B) for i in (2, 3))
        w0 = sb("w0", [P, 4 * HEADS * DH])
        wq_sb = w0[:, 0:HEADS * DH]
        wkv_sb = w0[:, HEADS * DH:3 * HEADS * DH]
        wout_sb = w0[:, 3 * HEADS * DH:4 * HEADS * DH].rearrange("p (a d) -> p a d", a=NPAIR)
        wqkvT = sb("wqkvT", [P, 2, 3, P])
        ab_all = sb("ab_all", [P, HEADS, 4, P], F16)
        ab = sb("ab", [P, 2, 4, P], F16)
        qkh = sb("qkh", [P, 2, SQ], F16)
        qkl = sb("qkl", [P, 2, SQ], F16)
        probs = sb("probs", [P, 2, NK])
        pth = sb("pth", [P, 2, KT, SQ], F16)
        ptl = sb("ptl", [P, 2, KT, SQ], F16)
        yh = sb("yh", [P, 2, SQ], F16)
        yl = sb("yl", [P, 2, SQ], F16)
        neg_max = sb("neg_max", [P, 2])
        den = sb("den", [P, 2 * E, 1])
        rden = sb("rden", [P, 2 * E, 1])
        stats = sb("stats", [P, B * KT, 6])
        mv = sb("mv", [P, B * KT, 2])
        var_e = sb("var_e", [P, B * KT])
        rstd = sb("rstd", [P, B * KT])
        rstd2 = sb("rstd2", [P, NT])
        var2 = sb("var2", [P, NT])
        w_in_sb = sb("w_in_sb", [P, E, FT, D])
        w_out_sb = w0[:, :].rearrange("p (e f) -> p e f", e=E)
        woT = sb("woT", [P, 2, FT, D])
        moe0h = sb("moe0h", [P, E, D], F16)
        moe0l = sb("moe0l", [P, E, D], F16)
        small = sb("small", [E, 2 * D])
        wgT = sb("wgT", [P, 2, E])
        b1n = sb("b1n", [E * FT, P])
        b1T = sb("b1T", [P, E * FT])
        b1c = sb("b1c", [P, 2, FT])
        xn = sb("xn", [P, NT, D])
        xT = sb("xT", [P, NT * P])
        logits = sb("logits", [P, NT, E])
        top8 = sb("top8", [P, NT, 8])
        idx8 = sb("idx8", [P, NT, 8], U32)
        idxf = sb("idxf", [P, NT, 8])
        g12 = sb("g12", [P, 3, NT])
        scaled = sb("scaled", [P, 2, E // 2, D])
        hit = sb("hit", [P, 2, NT, E])
        gates = sb("gates", [P, NT, E])
        rows1 = sb("rows1", [P, 4, D])
        rb_row = sb("rb_row", [P, E])
        qk1w = sb("qk1w", [P, 3, D])
        A1 = sb("A1", [P, D])
        gwT = sb("gwT", [P, D])
        kv32 = kv[:, :, :].rearrange("p a n -> p (a n)").bitcast(F32)
        ctxT = kv32[:, 0:B * SC].rearrange("p (b n) -> p b n", b=B)
        normT, q1T = (kv32[:, B * SC + i * NT * P:B * SC + (i + 1) * NT * P] for i in range(2))
        normed, alpha = (kv32[:, B * SC + i * NT * P:B * SC + (i + 1) * NT * P].rearrange("p (t d) -> p t d", t=NT)
                         for i in (2, 3))
        pt1 = sb("pt1", [P, 2, KT, P])
        w1n = sb("w1n", [P, 2, FT, D])
        w2n = sb("w2n", [P, 2, FF])
        w1Th = sb("w1Th", [P, 2, FF], F16)
        w1Tl = sb("w1Tl", [P, 2, FF], F16)
        w2Th = sb("w2Th", [P, 2, FT * D], F16)
        w2Tl = sb("w2Tl", [P, 2, FT * D], F16)
        xTh = sb("xTh", [P, NT * P], F16)
        xTl = sb("xTl", [P, NT * P], F16)
        hf = sb("hf", [P, FT, 512])
        gelu_first = sb("gelu_first", [P, FT])
        hh, hl = (ab_all[:, 8 * i:8 * i + 8, :, :].rearrange("p (c f) a n -> p c f (a n)", c=2) for i in range(2))
        gT = sb("gT", [NT * E, P])
        b2d = sb("b2d", [NT * E, NT, D])
        xb = sb("xb", [P, NT, D])
        acc4 = sb("acc4", [P, NT, D])

        ps = ctx.enter_context(nc.psum_tensor("ps", [P, 8, 512], F32))

        def bank(i, lo=0, hi=512):
            return ps[:, i, lo:hi]

        S_PS = [ps[:, 0:2, :].rearrange("p a n -> p (a n)"), ps[:, 2:4, :].rearrange("p a n -> p (a n)")]
        PT_PS = ps[:, 4:6, :].rearrange("p a n -> p (a n)")

        AB_PS = [ps[:, 2 + 2 * i:4 + 2 * i, 0:2 * P].rearrange("p h (a n) -> p h a n", a=2) for i in range(2)]
        Y_PS = bank(6, 0, SQ)
        QK_PS = bank(7, 0, SQ)
        O_PS = bank(7, SQ, 512)

        def sems(names):
            return (sem(n) for n in names.split())

        x_loaded, w_first_loaded, w_rest_loaded, ln_loaded = sems("x_loaded w_first_loaded w_rest_loaded ln_loaded")
        ctx_loaded = [sem(f"ctx_loaded{b}") for b in range(B)]
        w_in_loaded, w_out_loaded, small_loaded = sems("w_in_loaded w_out_loaded small_loaded")
        rows1_loaded, qk1w_loaded, b2_loaded = sems("rows1_loaded qk1w_loaded b2_loaded")
        w1_loaded = [sem("w1_loaded_a"), sem("w1_loaded_b")]
        w2_loaded = [sem("w2_loaded_a"), sem("w2_loaded_b")]
        out_stored, out_first_stored = sems("out_stored out_first_stored")
        const_ready, b2d_cleared, dve_steps = sems("const_ready b2d_cleared dve_steps")
        key_var_ready, key_rstd_ready = sems("key_var_ready key_rstd_ready")
        latent_var2_ready, latent_rstd2_ready = sems("latent_var2_ready latent_rstd2_ready")
        first_keys_ready, keys_normalised, keys_scaled, keys_ready = sems("first_keys_ready keys_normalised keys_scaled keys_ready")
        kv_high_ready, kv_low_ready = sems("kv_high_ready kv_low_ready")
        keysT_made, keysT_high_ready, keysT_low_ready = sems("keysT_made keysT_high_ready keysT_low_ready")
        pair_wT_made, pair_wT_copied, pair_ab_made = sems("pair_wT_made pair_wT_copied pair_ab_made")
        pair_ab_high_ready, pair_ab_low_ready, head_ab_ready = sems("pair_ab_high_ready pair_ab_low_ready head_ab_ready")
        queries_made, q_high_ready, q_low_ready = sems("queries_made q_high_ready q_low_ready")
        scores_ready, max_ready, probs_ready = sems("scores_ready max_ready probs_ready")
        probsT_made, probsT_high_ready, probsT_low_ready = sems("probsT_made probsT_high_ready probsT_low_ready")
        attended_made, attended_high_ready, attended_low_ready = sems("attended_made attended_high_ready attended_low_ready")
        projected_made, rden_ready, head_added = sems("projected_made rden_ready head_added")
        norm_var_ready, norm_rstd_ready, norm_ready = sems("norm_var_ready norm_rstd_ready norm_ready")
        normT_made, normT_copied = sems("normT_made normT_copied")
        logits_made, gate_gap_ready, gate_tanh_ready, gates_ready = sems("logits_made gate_gap_ready gate_tanh_ready gates_ready")
        w_outT_made, w_outT_copied, moe0_made = sems("w_outT_made w_outT_copied moe0_made")
        moe0_high_ready, moe0_low_ready = sems("moe0_high_ready moe0_low_ready")
        x0_high_ready, x0_low_ready = sems("x0_high_ready x0_low_ready")
        experts0_made, experts0_added, experts0_scaled = sems("experts0_made experts0_added experts0_scaled")
        experts0_partial, experts0_in_x = sems("experts0_partial experts0_in_x")
        setup1_made, setup1_copied = sems("setup1_made setup1_copied")
        hidden_var_ready, hidden_rstd_ready, hidden_norm_ready = sems("hidden_var_ready hidden_rstd_ready hidden_norm_ready")
        rms_var_ready, rms_rstd_ready, normed_ready = sems("rms_var_ready rms_rstd_ready normed_ready")
        inputs1T_made, inputs1T_copied = sems("inputs1T_made inputs1T_copied")
        gate1_made, gate1_biased, alpha_tanh_ready, q1T_made, q1T_ready = sems(
            "gate1_made gate1_biased alpha_tanh_ready q1T_made q1T_ready")
        scores1_ready, max1_ready, probs1_ready = sems("scores1_ready max1_ready probs1_ready")
        probs1T_made, probs1T_ready, attended1_made, x1_ready = sems("probs1T_made probs1T_ready attended1_made x1_ready")
        expert_wT_made, expert_w_high_ready, expert_w_low_ready = sems("expert_wT_made expert_w_high_ready expert_w_low_ready")
        x1_high_ready, x1_low_ready, b1_ready, gelu_loaded = sems("x1_high_ready x1_low_ready b1_ready gelu_loaded")
        up_made, gelu_ready, units_high_ready, units_low_ready = sems("up_made gelu_ready units_high_ready units_low_ready")
        down_made, expert_added = sems("down_made expert_added")
        gatesT_made, gatesT_ready, gates_b2_made, gates_b2_added = sems("gatesT_made gatesT_ready gates_b2_made gates_b2_added")
        xb_ready, out_centred, out_ready = sems("xb_ready out_centred out_ready")
        out_first_scaled, out_first_ready = sems("out_first_scaled out_first_ready")

        def load(eng, dst, src, s):
            eng.dma_start(dst, src).then_inc(s, 16)

        ctx_v = A["ctx_1024"].rearrange("b (i p) d -> p b i d", p=P)
        w1_v = A["L1_ffn_w1"].rearrange("e (t p) d -> p e t d", p=P)
        w2_v = A["L1_ffn_w2"].rearrange("e p f -> p e f")
        out_v = out.rearrange("b (j p) d -> p (b j) d", p=P)

        def key_tiles(u):
            return CT + 1 + u % 2

        def keys_bank(b, k):
            return (7, 6, 5, 4)[k + 2 * (b == B - 1)]

        def bank0(t, c):
            return (4 + 2 * t + c) % 8

        def hidden_bank(g, f):
            return (7, 3, 6, 2)[f] if g is None else (2, 3, 6)[(g * FT + f) % 3]

        def wait_keys(eng, b, parts):
            if b:
                eng.wait_ge(keys_ready, 2 * b - 2 + parts)
            else:
                eng.wait_ge(first_keys_ready, parts)

        block = ctx.enter_context(nc.Block())

        @block.sync
        def _(sp):
            wout_v = A["L0_xattn_Wout"].rearrange("(a p) d -> p a d", p=P)
            for lo, hi, s in ((0, FIRST_PAIRS, w_first_loaded), (FIRST_PAIRS, NPAIR, w_rest_loaded)):
                if lo:
                    sp.wait_ge(x_loaded, 16)
                load(sp, wq_sb[:, lo * P:hi * P], A["L0_xattn_Wq"][:, lo * P:hi * P], s)
                wkv_v = A["L0_xattn_Wkv"].rearrange("p (a n) -> p a n", a=2)
                load(sp, wkv_sb.rearrange("p (a n) -> p a n", a=2)[:, :, lo * P:hi * P], wkv_v[:, :, lo * P:hi * P], s)
                load(sp, wout_sb[:, lo:hi, :], wout_v[:, lo:hi, :], s)
            sp.wait_ge(w_rest_loaded, 48)
            for i, name in enumerate(("L0_ffn_w_gate", "L1_ffn_router_w")):
                load(sp, small[:, i * D:(i + 1) * D], A[name], small_loaded)
            load(sp, b1n[:, :], A["L1_ffn_b1"].rearrange("e (t p) -> (e t) p", p=P), small_loaded)
            for i, name in enumerate(("L1_xattn_norm_w", "L1_xattn_gate_b", "L1_ffn_ln_w", "L1_ffn_ln_b")):
                load(sp, rows1[:, i, :], A[name].partition_broadcast(P), rows1_loaded)
            load(sp, rb_row[:, :], A["L1_ffn_router_b"].partition_broadcast(P), rows1_loaded)
            load(sp, qk1w[:, 0, :], A["L1_xattn_q_w"], qk1w_loaded)
            load(sp, qk1w[:, 1, :], A["L1_xattn_k_w"], qk1w_loaded)
            load(sp, qk1w[:, 2, :], A["L1_xattn_gate_w"], qk1w_loaded)
            load(sp, w_in_sb[:, :, :, :], A["L0_ffn_w_in"].rearrange("e (t p) d -> p e t d", p=P), w_in_loaded)
            sp.wait_ge(pair_ab_made, NPAIR)
            load(sp, w_out_sb, A["L0_ffn_w_out"].rearrange("e p f -> p e f"), w_out_loaded)
            for e in range(2):
                load(sp, w1n[:, e, :, :], w1_v[:, e, :, :], w1_loaded[e])
                load(sp, w2n[:, e, :], w2_v[:, e, :], w2_loaded[e])
            sp.wait_ge(b2d_cleared, 1)
            for t in range(NT):
                load(sp, b2d[t * E:(t + 1) * E, t, :], A["L1_ffn_b2"], b2_loaded)
            with sp.Fori(1, E // 2) as i:
                for e in range(2):
                    sp.wait_ge(expert_wT_made, i * 4 + (2 * e - 2))
                    load(sp, w1n[:, e, :, :], w1_v[:, at(i * 2 + e, 1), :, :].rearrange("p a t d -> p (a t) d"), w1_loaded[e])
                    load(sp, w2n[:, e, :], w2_v[:, at(i * 2 + e, 1), :].rearrange("p a f -> p (a f)"), w2_loaded[e])
            for c in range(2, 4):
                sp.wait_ge(out_ready, 2 * c - 2)
                load(sp, out_v[:, 2 * c:2 * c + 2, :], acc4[:, 2 * c:2 * c + 2, :], out_stored)
            sp.wait_ge(out_stored, 32)
            sp.wait_ge(out_first_stored, 16)

        @block.gpsimd
        def _(pool):
            pool.memset(ident[:, :], 0.0).then_inc(const_ready, 1)
            pool.memset(minus_half[:, :], -0.5).then_inc(const_ready, 1)
            pool.wait_ge(const_ready, 2)
            pool.affine_select(out=ident[:, :], in_=ident[:, :], compare_op=ALU.not_equal, fill=1.0, base=0,
                               pattern=[[-1, P]], channel_multiplier=1).then_inc(const_ready, 1)

            def rsqrt(dst, src, s):
                pool.tensor_tensor(dst, src, minus_half[:, 0:src.shape[1]], ALU.pow).then_inc(s, 1)

            def head_weights(h):
                if h % 2 == 0:
                    pool.wait_ge(pair_ab_high_ready, h // 2 + 1)
                    pool.wait_ge(pair_ab_low_ready, h // 2 + 1)
                if h >= 2:
                    pool.wait_ge(projected_made, B * (h - 1))
                pool.tensor_copy(ab[:, h % 2, :, :].bitcast(U32), ab_all[:, h, :, :].bitcast(U32)).then_inc(head_ab_ready, 1)

            def first_rsqrt(b):
                pool.wait_ge(key_var_ready, b + 1)
                rsqrt(rstd[:, b * KT:(b + 1) * KT], var_e[:, b * KT:(b + 1) * KT], key_rstd_ready)

            def second_rsqrt(b):
                pool.wait_ge(latent_var2_ready, b + 1)
                rsqrt(rstd2[:, QT * b:QT * b + QT], var2[:, QT * b:QT * b + QT], latent_rstd2_ready)

            def affine(b):
                parts = ((0, CT), (CT, KT))
                for k, (lo, hi) in enumerate(parts):
                    pool.wait_ge(keys_normalised, 2 * b + k - 1)
                    v = kvf[:, b, lo:hi, :]
                    g = ln_rows[:, 2 * k, :].unsqueeze(1).broadcast_to([P, hi - lo, D])
                    pool.tensor_tensor(v, v, g, ALU.mult).then_inc(keys_scaled, 1)
                for k, (lo, hi) in enumerate(parts):
                    pool.wait_ge(keys_scaled, 2 * b + k - 1)
                    v = kvf[:, b, lo:hi, :]
                    h = ln_rows[:, 2 * k + 1, :].unsqueeze(1).broadcast_to([P, hi - lo, D])
                    pool.tensor_tensor(v, v, h, ALU.add).then_inc(keys_ready, 1)

            first_rsqrt(0)
            first_rsqrt(1)
            second_rsqrt(0)
            second_rsqrt(1)
            first_rsqrt(2)
            affine(1)
            head_weights(0)
            second_rsqrt(2)
            first_rsqrt(3)
            affine(2)
            second_rsqrt(3)
            affine(3)
            for b in range(B):
                pool.wait_ge(kv_high_ready, b + 1)
                pool.tensor_tensor(kvl[:, b, :, :], kvf[:, b, :, :], kvh[:, b, :, :], ALU.subtract).then_inc(kv_low_ready, 1)
            pool.memset(causal[:, :], 0.0).then_inc(const_ready, 1)
            head_weights(1)
            pool.wait_ge(const_ready, 4)
            pool.affine_select(out=causal[:, :], in_=causal[:, :], compare_op=ALU.is_ge, fill=MASKED, base=0,
                               pattern=[[-1, P]], channel_multiplier=1).then_inc(const_ready, 1)
            pool.iota(iota_e[:, :, :], pattern=[[0, NT], [1, E]], base=0, channel_multiplier=0,
                      allow_small_or_imprecise_dtypes=True).then_inc(const_ready, 1)
            pool.memset(b2d[:, :, :], 0.0).then_inc(b2d_cleared, 1)
            for h in range(2, HEADS):
                head_weights(h)

            def rsqrt_half(c, src_sem, count, dst_sem, dst=rstd, src=var_e):
                pool.wait_ge(src_sem, count)
                rsqrt(dst[:, 4 * c:4 * c + 4], src[:, 4 * c:4 * c + 4], dst_sem)

            def add_scaled(t):
                v = scaled[:, t % 2, :, :]
                for i in range(2):
                    pool.wait_ge(experts0_scaled, 4 * t + 3 + i)
                    if i:
                        pool.wait_ge(experts0_partial, 2 * t + 1)
                    pool.tensor_tensor(v[:, 1, :], v[:, 1, :], v[:, 2 + i, :], ALU.add).then_inc(experts0_partial, 1)
                pool.wait_ge(experts0_partial, 2 * t + 2)
                pool.wait_ge(experts0_added, 2 * E_VECTOR * (t // 2 + 1))
                pool.tensor_tensor(x_cur[:, t, :], x_cur[:, t, :], v[:, 1, :], ALU.add).then_inc(experts0_in_x, 1)

            for c in range(2):
                rsqrt_half(c, norm_var_ready, c + 1, norm_rstd_ready)
            for t in range(5):
                add_scaled(t)
            rsqrt_half(0, hidden_var_ready, 1, hidden_rstd_ready)
            add_scaled(5)
            rsqrt_half(0, rms_var_ready, 1, rms_rstd_ready, rstd2, var2)
            add_scaled(6)
            add_scaled(7)
            rsqrt_half(1, hidden_var_ready, 2, hidden_rstd_ready)
            rsqrt_half(1, rms_var_ready, 2, rms_rstd_ready, rstd2, var2)
            for c in range(2):
                rsqrt_half(c, norm_var_ready, 3 + c, norm_rstd_ready)
            pool.wait_ge(x1_ready, NT)
            pool.tensor_tensor(xb[:, :, :], x_cur[:, :, :], rows1[:, 3, :].unsqueeze(1).broadcast_to([P, NT, D]),
                               ALU.add).then_inc(xb_ready, 1)
            rsqrt_half(0, norm_var_ready, 5, norm_rstd_ready)
            for q in range(2):
                pool.wait_ge(norm_var_ready, 6 + q)
                v = slice(4 + 2 * q, 6 + 2 * q)
                rsqrt(rstd[:, v], var_e[:, v], norm_rstd_ready)
                if q == 0:
                    pool.wait_ge(out_first_scaled, 4)
                    pool.wait_ge(xb_ready, 1)
                    pool.tensor_tensor(acc4[:, 0:4, :], acc4[:, 0:4, :], xb[:, 0:4, :], ALU.add).then_inc(out_first_ready, 1)

        @block.scalar
        def _(act):
            load(act, x_cur[:, :, :], A["x"].rearrange("b (j p) d -> p (b j) d", p=P), x_loaded)
            for b in range(B):
                load(act, ctx_sb[:, b, :, :], ctx_v[:, b, :, :], ctx_loaded[b])
                if b == 0:
                    for i, name in enumerate(("ln_m_g", "ln_m_b", "ln_l_g", "ln_l_b")):
                        load(act, ln_rows[:, i, :], A["L0_xattn_" + name].partition_broadcast(P), ln_loaded)

            def weights_T(p):
                act.wait_ge(pair_wT_made, p + 1)
                if p >= 2:
                    act.wait_ge(pair_ab_made, p - 1)
                nc.scalar.copy(wqkvT[:, p % 2, :, :], bank(p % 2, 0, 384).rearrange("p (a n) -> p a n", a=3)).then_inc(pair_wT_copied, 1)

            def kv_high(b):
                wait_keys(act, b, 2)
                nc.scalar.copy(kvh[:, b, :, :], kvf[:, b, :, :]).then_inc(kv_high_ready, 1)

            def keys_T_high(b, k):
                act.wait_ge(keysT_made, 2 * b + k + 1)
                lo, hi = KEY_PARTS[k]
                nc.scalar.copy(kth[:, b, lo:hi], bank(keys_bank(b, k), 0, hi - lo)).then_inc(keysT_high_ready, 1)

            def queries_high(n, k):
                act.wait_ge(queries_made, n + 1)
                nc.scalar.activation(qkh[:, k % 2, :], QK_PS, ACT.Copy, scale=HEAD_SCALE).then_inc(q_high_ready, 1)

            weights_T(0)
            for p in range(NPAIR):
                if p + 1 < NPAIR:
                    weights_T(p + 1)
                else:
                    queries_high(0, 0)
                act.wait_ge(pair_ab_made, p + 1)
                nc.scalar.copy(ab_all[:, 2 * p:2 * p + 2, 0::2, :], AB_PS[p % 2]).then_inc(pair_ab_high_ready, 1)
                if p % 2:
                    keys_T_high(p // 2, 0)
                    keys_T_high(p // 2, 1)
                if p % 2 and p + 1 < NPAIR:
                    kv_high(p // 2)

            def probs_T_high(n, k, j):
                act.wait_ge(probsT_made, n * 2 + (j + 1))
                nc.scalar.copy(pth[:, k % 2, :, j * P:(j + 1) * P],
                               PT_PS[:, 0:NK].rearrange("p (i q) -> p i q", i=KT)).then_inc(probsT_high_ready, 1)

            def exponentials(n, k, j, first):
                act.wait_ge(max_ready, n * 2 + (j + 1))
                if not first:
                    act.wait_ge(probsT_made, n * 2 + (j - 1))
                nc.scalar.activation(probs[:, j, :], S_PS[j][:, 0:NK], ACT.Exp, bias=neg_max[:, j:j + 1],
                                     accum_out=den[:, 2 * (k % 8) + j, :]).then_inc(probs_ready, 1)

            def attended_high(n, k):
                act.wait_ge(attended_made, n + 1)
                nc.scalar.copy(yh[:, k % 2, :], Y_PS).then_inc(attended_high_ready, 1)

            def item(n, k, start=3, last=False):
                if start >= 1:
                    probs_T_high(n - 1, k - 1, 1)
                exponentials(n, k, 0, start == 0)
                if start == 0:
                    kv_high(B - 1)
                if start >= 2:
                    attended_high(n - 2, k)
                if not last:
                    queries_high(n + 1, k + 1)
                probs_T_high(n, k, 0)
                exponentials(n, k, 1, start == 0)

            for k in range(8):
                item(k, k, start=min(k, 3))
            with act.Fori(1, ITEMS // 8 - 1) as p:
                for k in range(8):
                    item(p * 8 + k, k)
            for k in range(8):
                item(ITEMS - 8 + k, k, last=k == 7)

            def w_out_T(e):
                act.wait_ge(w_outT_made, e + 1)
                if e >= 2:
                    act.wait_ge(moe0_made, e - 1)
                nc.scalar.copy(woT[:, e % 2, :, :], bank(e % 2).rearrange("p (t n) -> p t n", t=FT)).then_inc(w_outT_copied, 1)

            probs_T_high(ITEMS - 1, 7, 1)
            w_out_T(0)
            attended_high(ITEMS - 2, 6)
            w_out_T(1)
            w_out_T(2)
            attended_high(ITEMS - 1, 7)
            for e in range(3, E):
                w_out_T(e)
            for c in range(2):
                act.wait_ge(moe0_made, 4 * c + 4)
                nc.scalar.copy(moe0h[:, 4 * c:4 * c + 4, :], bank(2 + c).rearrange("p (e n) -> p e n", e=4)).then_inc(moe0_high_ready, 1)
            act.wait_ge(setup1_made, 1)
            nc.scalar.copy(wgT[:, :, :], bank(6, 0, 2 * E).rearrange("p (a n) -> p a n", a=2)).then_inc(setup1_copied, 1)
            nc.scalar.copy(b1T[:, :], bank(6, 16, 16 + E * FT)).then_inc(setup1_copied, 1)
            nc.scalar.copy(gwT[:, :], bank(6, 128, 256)).then_inc(setup1_copied, 1)
            nc.scalar.copy(A1[:, :], bank(6, 256, 384)).then_inc(setup1_copied, 1)

            def norm_T(i, c, src):
                act.wait_ge(normT_made, i + 1)
                nc.scalar.copy(xT[:, 512 * c:512 * c + 512], src).then_inc(normT_copied, 1)

            def gate_tanh(k):
                act.wait_ge(gate_gap_ready, k + 1)
                nc.scalar.activation(g12[:, 2, :], g12[:, 0, :], ACT.Tanh, scale=0.5).then_inc(gate_tanh_ready, 1)

            for c in range(2):
                norm_T(c, c, bank(c))
                act.wait_ge(normT_copied, c + 1)
                nc.scalar.copy(xTh[:, 512 * c:512 * c + 512], xT[:, 512 * c:512 * c + 512]).then_inc(x0_high_ready, 1)
            gate_tanh(0)
            act.wait_ge(gates_ready, 1)
            def scale_experts(t):
                act.wait_ge(experts0_made, 2 * t + 2)
                if t >= 2:
                    act.wait_ge(experts0_in_x, t - 1)
                for e in range(4):
                    nc.scalar.activation(scaled[:, t % 2, e, :], bank(bank0(t, 1), e * D, (e + 1) * D), ACT.Copy,
                                         scale=gates[:, t, 4 + e:5 + e]).then_inc(experts0_scaled, 1)

            def context_T(b):
                act.wait_ge(setup1_made, b + 2)
                nc.scalar.copy(ctxT[:, b, :], bank(4 + b % 2)).then_inc(setup1_copied, 1)

            for t in range(6):
                scale_experts(t)
            context_T(0)
            context_T(1)
            scale_experts(6)
            context_T(2)
            scale_experts(7)
            context_T(3)

            def exp1(u):
                act.wait_ge(max1_ready, u + 1)
                if u >= 2:
                    act.wait_ge(probs1T_made, u - 1)
                n = key_tiles(u) * P
                nc.scalar.activation(probs[:, u % 2, 0:n], S_PS[u % 2][:, 0:n], ACT.Exp, bias=neg_max[:, u % 2:u % 2 + 1],
                                     accum_out=den[:, u, :]).then_inc(probs1_ready, 1)

            def probs_T1(u):
                act.wait_ge(probs1T_made, u + 1)
                if u >= 2:
                    act.wait_ge(attended1_made, u - 1)
                k = key_tiles(u)
                nc.scalar.copy(pt1[:, u % 2, 0:k, :], PT_PS[:, 0:k * P].rearrange("p (i q) -> p i q", i=k)).then_inc(probs1T_ready, 1)

            def x_high(c):
                act.wait_ge(normT_copied, 3 + c)
                nc.scalar.copy(xTh[:, 512 * c:512 * c + 512], xT[:, 512 * c:512 * c + 512]).then_inc(x1_high_ready, 1)

            def high_weights(e, s, w):
                act.wait_ge(expert_wT_made, e * 2 + (w + 1))
                nc.scalar.copy((w1Th, w2Th)[w][:, s, :], bank(w)).then_inc(expert_w_high_ready, 1)

            def biases(e, s):
                nc.scalar.copy(b1c[:, s, :], b1T[:, at(e * FT, FT)]).then_inc(b1_ready, 1)

            def norms_T1(c):
                act.wait_ge(inputs1T_made, 2 * c + 1)
                nc.scalar.copy(xT[:, 512 * c:512 * c + 512], bank(6)).then_inc(inputs1T_copied, 1)
                act.wait_ge(inputs1T_made, 2 * c + 2)
                nc.scalar.copy(normT[:, 512 * c:512 * c + 512], bank(7)).then_inc(inputs1T_copied, 1)

            def queries_and_gate(c):
                act.wait_ge(q1T_made, c + 1)
                nc.scalar.activation(q1T[:, 512 * c:512 * c + 512], bank(5 + 2 * c), ACT.Copy, scale=SCALE1).then_inc(q1T_ready, 1)
                act.wait_ge(gate1_biased, c + 1)
                v = alpha[:, 4 * c:4 * c + 4, :]
                nc.scalar.activation(v, v, ACT.Tanh, scale=0.5).then_inc(alpha_tanh_ready, 1)

            norms_T1(0)
            queries_and_gate(0)
            exp1(0)
            norms_T1(1)
            probs_T1(0)
            exp1(1)
            queries_and_gate(1)
            for u in range(1, NT - 1):
                exp1(u + 1)
                probs_T1(u)
            norm_T(2, 0, bank(1))
            x_high(0)
            high_weights(0, 0, 0)
            probs_T1(NT - 1)
            high_weights(0, 0, 1)
            nc.scalar.activation(gelu_first[:, :], b1T[:, 0:FT], ACT.Gelu).then_inc(gelu_loaded, 1)

            def hidden(e, s, c, g, static, tiles=range(FT)):
                for f in tiles:
                    m = e * 8 + (4 * c + f)
                    act.wait_ge(up_made, m + 1)
                    if not static or m >= FT:
                        act.wait_ge(units_low_ready, m - (FT - 1))
                    nc.scalar.activation(hf[:, f, :], bank(hidden_bank(g, f)), ACT.Gelu,
                                         bias=b1c[:, s, f:f + 1]).then_inc(gelu_ready, 1)

            def expert(e, s, first=False, last=False):
                g, g1 = (2 * s, 2 * s + 1) if first else (None, None)
                biases(e, s)
                act.wait_ge(b1_ready, e + 1)
                hidden(e, s, 0, g, first, range(2))
                if first and s == 1:
                    gate_tanh(1)
                hidden(e, s, 0, g, first, range(2, FT))
                if first and s == 0:
                    norm_T(3, 1, bank(7))
                    x_high(1)
                if first and s == 1:
                    act.wait_ge(gatesT_made, 1)
                    nc.scalar.copy(gT[:, :], ps[0:NT * E, 7, 0:P]).then_inc(gatesT_ready, 1)
                if not last:
                    high_weights(e + 1, 1 - s, 0)
                    high_weights(e + 1, 1 - s, 1)
                hidden(e, s, 1, g1, first)
            for s in range(2):
                expert(s, s, first=True)
            with act.Fori(1, E // 2 - 1) as i:
                for s in range(2):
                    expert(i * 2 + s, s)
            for s in range(2):
                expert(E - 2 + s, s, last=s == 1)
            act.wait_ge(norm_rstd_ready, 5)
            for t in range(4):
                act.wait_ge(out_centred, t + 1)
                nc.scalar.activation(acc4[:, t, :], acc4[:, t, :], ACT.Copy, scale=rstd[:, t:t + 1]).then_inc(out_first_scaled, 1)
            act.wait_ge(out_first_ready, 1)
            load(act, out_v[:, 0:4, :], acc4[:, 0:4, :], out_first_stored)

        @block.vector
        def _(dve):
            chain = [0]

            def step(ins):
                chain[0] += 1
                ins.then_inc(dve_steps, 1)

            def settle():
                dve.wait_ge(dve_steps, chain[0])

            def link(ins):
                step(ins)
                settle()

            def stats_of(src, i):
                step(nc.vector.bn_stats(stats[:, i, :], src))

            def variances(lo, hi, eps, s):
                settle()
                for i in range(lo, hi):
                    step(nc.vector.bn_aggr(mv[:, i, :], stats[:, i, :]))
                settle()
                nc.vector.tensor_scalar(var_e[:, lo:hi], mv[:, lo:hi, 1], eps, None, ALU.add).then_inc(s, 1)

            def key_stats(b):
                for j in range(QT):
                    stats_of(x_cur[:, QT * b + j, :], b * KT + CT + j)
                dve.wait_ge(ctx_loaded[b], 16)
                for i in range(CT):
                    stats_of(ctx_sb[:, b, i, :], b * KT + i)
                variances(b * KT, (b + 1) * KT, LN_EPS, key_var_ready)

            def latents_second_norm(b):
                k, t = b * KT + CT, var2[:, QT * b:QT * b + QT]
                dve.wait_ge(key_rstd_ready, b + 1)
                link(nc.vector.tensor_tensor(t, mv[:, k:k + QT, 1], rstd[:, k:k + QT], ALU.mult))
                link(nc.vector.tensor_tensor(t, t, rstd[:, k:k + QT], ALU.mult))
                nc.vector.tensor_scalar(t, t, LN_EPS, None, ALU.add).then_inc(latent_var2_ready, 1)

            def latents_rstd(b):
                k = b * KT + CT
                dve.wait_ge(latent_rstd2_ready, b + 1)
                link(nc.vector.tensor_tensor(rstd[:, k:k + QT], rstd[:, k:k + QT], rstd2[:, QT * b:QT * b + QT], ALU.mult))

            def key_source(b, i):
                return ctx_sb[:, b, i, :] if i < CT else x_cur[:, QT * b + i - CT, :]

            def centre_first_keys():
                dve.wait_ge(ln_loaded, 64)
                for i in range(KT):
                    step(nc.vector.scalar_tensor_tensor(kvf[:, 0, i, :], key_source(0, i), mv[:, i, 0:1],
                                                        ln_rows[:, 2 * (i // CT), :], ALU.subtract, ALU.mult))

            def normalise_first_keys():
                def tile(i):
                    return nc.vector.scalar_tensor_tensor(kvf[:, 0, i, :], kvf[:, 0, i, :], rstd[:, i:i + 1],
                                                          ln_rows[:, 2 * (i // CT) + 1, :], ALU.mult, ALU.add)
                settle()
                for i in range(CT - 1):
                    tile(i)
                tile(CT - 1).then_inc(first_keys_ready, 1)
                latents_rstd(0)
                tile(CT)
                tile(CT + 1).then_inc(first_keys_ready, 1)

            def normalise_keys(b):
                def tile(i):
                    k = b * KT + i
                    return nc.vector.tensor_scalar(kvf[:, b, i, :], key_source(b, i), mv[:, k, 0:1], rstd[:, k:k + 1],
                                                   ALU.subtract, ALU.mult)
                for i in range(CT - 1):
                    tile(i)
                tile(CT - 1).then_inc(keys_normalised, 1)
                latents_rstd(b)
                tile(CT)
                tile(CT + 1).then_inc(keys_normalised, 1)

            def head_weights_low(p):
                dve.wait_ge(pair_ab_high_ready, p + 1)
                nc.vector.tensor_tensor(ab_all[:, 2 * p:2 * p + 2, 1::2, :], AB_PS[p % 2],
                                        ab_all[:, 2 * p:2 * p + 2, 0::2, :], ALU.subtract).then_inc(pair_ab_low_ready, 1)

            def keys_T_low(b):
                for k in range(2):
                    keys_part_low(b, k)

            def keys_part_low(b, k):
                dve.wait_ge(keysT_high_ready, 2 * b + k + 1)
                lo, hi = KEY_PARTS[k]
                nc.vector.tensor_tensor(ktl[:, b, lo:hi], bank(keys_bank(b, k), 0, hi - lo), kth[:, b, lo:hi],
                                        ALU.subtract).then_inc(keysT_low_ready, 1)

            def queries_low(n, k):
                dve.wait_ge(q_high_ready, n + 1)
                nc.vector.scalar_tensor_tensor(qkl[:, k % 2, :], QK_PS, HEAD_SCALE, qkh[:, k % 2, :],
                                               ALU.mult, ALU.subtract).then_inc(q_low_ready, 1)

            dve.wait_ge(x_loaded, 16)
            key_stats(0)
            key_stats(1)
            centre_first_keys()
            latents_second_norm(0)
            normalise_first_keys()
            latents_second_norm(1)
            head_weights_low(0)
            key_stats(2)
            normalise_keys(1)
            head_weights_low(1)
            keys_T_low(0)
            latents_second_norm(2)
            key_stats(3)
            head_weights_low(2)
            normalise_keys(2)
            head_weights_low(3)
            keys_T_low(1)
            latents_second_norm(3)
            head_weights_low(4)
            normalise_keys(3)
            head_weights_low(5)
            keys_T_low(2)
            head_weights_low(6)
            queries_low(0, 0)
            head_weights_low(7)
            keys_T_low(3)

            def maximum(n, j, first):
                dve.wait_ge(scores_ready, n * 2 + (j + 1))
                if not first:
                    dve.wait_ge(probs_ready, n * 2 + (j - 1))
                nc.vector.tensor_reduce(neg_max[:, j:j + 1], S_PS[j][:, 0:NK], op=ALU.max, axis=AX.X,
                                        negate=True).then_inc(max_ready, 1)

            def probs_T_low(n, k, j):
                dve.wait_ge(probsT_high_ready, n * 2 + (j + 1))
                q = slice(j * P, j * P + P)
                nc.vector.tensor_tensor(ptl[:, k % 2, :, q], PT_PS[:, 0:NK].rearrange("p (i q) -> p i q", i=KT),
                                        pth[:, k % 2, :, q], ALU.subtract).then_inc(probsT_low_ready, 1)

            def attended_low(n, k):
                dve.wait_ge(attended_high_ready, n + 1)
                nc.vector.tensor_tensor(yl[:, k % 2, :], Y_PS, yh[:, k % 2, :], ALU.subtract).then_inc(attended_low_ready, 1)

            def accumulate(n, k, first):
                b, d = k % B, slice(2 * (k % 8), 2 * (k % 8) + 2)
                dve.wait_ge(probs_ready, n * 2 + 2)
                nc.vector.reciprocal(rden[:, d, 0], den[:, d, 0]).then_inc(rden_ready, 1)
                dve.wait_ge(projected_made, n + 1)
                dve.wait_ge(rden_ready, n + 1)
                for j in range(QT):
                    if not first:
                        dve.wait_ge(head_added, n * 2 + (j - 2 * B + 1))
                    t = x_cur[:, QT * b + j, :]
                    nc.vector.scalar_tensor_tensor(t, O_PS[:, j * P:(j + 1) * P], rden[:, 2 * (k % 8) + j, :], t,
                                                   ALU.mult, ALU.add).then_inc(head_added, 1)

            def item(n, k, start=3, first=False, last=False):
                maximum(n, 0, start == 0)
                if start >= 1:
                    probs_T_low(n - 1, k - 1, 1)
                if start >= 2:
                    attended_low(n - 2, k)
                if not last:
                    queries_low(n + 1, k + 1)
                maximum(n, 1, start == 0)
                probs_T_low(n, k, 0)
                if start >= 2:
                    accumulate(n - 2, (k - 2) % 8, first and k - 2 < B)

            for k in range(8):
                item(k, k, start=min(k, 3), first=True)
            with dve.Fori(1, ITEMS // 8 - 1) as p:
                for k in range(8):
                    item(p * 8 + k, k)
            for k in range(8):
                item(ITEMS - 8 + k, k, last=k == 7)

            def half_variances(c, eps, s):
                variances(4 * c, 4 * c + 4, eps, s)

            def tile_pair_stats(n):
                dve.wait_ge(head_added, 2 * n + 2)
                for j in range(QT):
                    stats_of(x_cur[:, QT * (n % B) + j, :], QT * (n % B) + j)

            probs_T_low(ITEMS - 1, 7, 1)
            for n in (ITEMS - 4, ITEMS - 3):
                tile_pair_stats(n)
            attended_low(ITEMS - 2, 6)
            half_variances(0, LN_EPS, norm_var_ready)
            accumulate(ITEMS - 2, 6, False)
            attended_low(ITEMS - 1, 7)
            tile_pair_stats(ITEMS - 2)
            accumulate(ITEMS - 1, 7, False)
            tile_pair_stats(ITEMS - 1)
            half_variances(1, LN_EPS, norm_var_ready)

            def normalise(c, src, s):
                for t in range(4 * c, 4 * c + 4):
                    nc.vector.tensor_scalar(xn[:, t, :], src[:, t, :], mv[:, t, 0:1], rstd[:, t:t + 1],
                                            ALU.subtract, ALU.mult).then_inc(s, 1)

            for c in range(2):
                dve.wait_ge(norm_rstd_ready, c + 1)
                normalise(c, x_cur, norm_ready)

            def route(k, lg):
                dve.wait_ge(logits_made, k + 1)
                if k:
                    dve.wait_ge(rows1_loaded, 80)
                    link(nc.vector.tensor_tensor(logits[:, :, :], lg, rb_row[:, :].unsqueeze(1).broadcast_to([P, NT, E]), ALU.add))
                else:
                    link(nc.vector.tensor_copy(logits[:, :, :], lg))
                for t in range(NT):
                    step(nc.vector.max(top8[:, t, :], logits[:, t, :]))
                settle()
                nc.vector.tensor_tensor(g12[:, 0, :], top8[:, :, 0], top8[:, :, 1], ALU.subtract).then_inc(gate_gap_ready, 1)
                for t in range(NT):
                    step(nc.vector.max_index(idx8[:, t, :], top8[:, t, :], logits[:, t, :]))
                dve.wait_ge(gate_tanh_ready, k + 1)
                step(nc.vector.tensor_scalar(g12[:, 0, :], g12[:, 2, :], 0.5, 0.5, ALU.mult, ALU.add))
                step(nc.vector.tensor_scalar(g12[:, 1, :], g12[:, 2, :], -0.5, 0.5, ALU.mult, ALU.add))
                settle()
                link(nc.vector.tensor_copy(idxf[:, :, :], idx8[:, :, :]))
                for r in range(2):
                    step(nc.vector.tensor_tensor(hit[:, r, :, :], iota_e[:, :, :],
                                                 idxf[:, :, r:r + 1].broadcast_to([P, NT, E]), ALU.is_equal))
                settle()
                for r in range(2):
                    step(nc.vector.tensor_tensor(hit[:, r, :, :], hit[:, r, :, :],
                                                 g12[:, r, :].unsqueeze(2).broadcast_to([P, NT, E]), ALU.mult))
                settle()
                nc.vector.tensor_tensor(gates[:, :, :], hit[:, 0, :, :], hit[:, 1, :, :], ALU.add).then_inc(gates_ready, 1)
                dve.wait_ge(gates_ready, k + 1)

            for c in range(2):
                dve.wait_ge(moe0_high_ready, c + 1)
                nc.vector.tensor_tensor(moe0l[:, 4 * c:4 * c + 4, :], bank(2 + c).rearrange("p (e n) -> p e n", e=4),
                                        moe0h[:, 4 * c:4 * c + 4, :], ALU.subtract).then_inc(moe0_low_ready, 1)
            for c in range(2):
                v = slice(512 * c, 512 * c + 512)
                dve.wait_ge(x0_high_ready, c + 1)
                nc.vector.tensor_tensor(xTl[:, v], xT[:, v], xTh[:, v], ALU.subtract).then_inc(x0_low_ready, 1)
            dve.wait_ge(const_ready, 6)
            route(0, bank(6, 0, NT * E).rearrange("p (t e) -> p t e", t=NT))

            def add_pair(k, experts=range(E_VECTOR)):
                done = 2 * E_VECTOR * k + 2 * experts[0]
                for e in experts:
                    for t in (2 * k, 2 * k + 1):
                        if e == 0:
                            dve.wait_ge(experts0_made, 2 * t + 1)
                        else:
                            dve.wait_ge(experts0_added, done - 1)
                        if e == 4:
                            dve.wait_ge(experts0_scaled, 4 * t + 1)
                            nc.vector.tensor_tensor(x_cur[:, t, :], x_cur[:, t, :], scaled[:, t % 2, 0, :], ALU.add).then_inc(experts0_added, 1)
                        else:
                            nc.vector.scalar_tensor_tensor(x_cur[:, t, :], bank(bank0(t, 0), e * D, (e + 1) * D),
                                                           gates[:, t, e:e + 1], x_cur[:, t, :],
                                                           ALU.mult, ALU.add).then_inc(experts0_added, 1)
                        done += 1

            def summed_stats(t):
                dve.wait_ge(experts0_in_x, t + 1)
                stats_of(x_cur[:, t, :], t)

            def rms(c):
                h, r = var2[:, 4 * c:4 * c + 4], rstd[:, 4 * c:4 * c + 4]
                dve.wait_ge(hidden_rstd_ready, c + 1)
                link(nc.vector.tensor_tensor(h, mv[:, 4 * c:4 * c + 4, 1], r, ALU.mult))
                link(nc.vector.tensor_tensor(h, h, r, ALU.mult))
                nc.vector.tensor_scalar(h, h, RMS_EPS, None, ALU.add).then_inc(rms_var_ready, 1)

            def normed_half(c):
                dve.wait_ge(rms_rstd_ready, c + 1)
                dve.wait_ge(hidden_norm_ready, 4 * c + 4)
                for t in range(4 * c, 4 * c + 4):
                    nc.vector.scalar_tensor_tensor(normed[:, t, :], xn[:, t, :], rstd2[:, t:t + 1], rows1[:, 0, :],
                                                   ALU.mult, ALU.mult).then_inc(normed_ready, 1)

            def gate_bias(c):
                dve.wait_ge(gate1_made, c + 1)
                nc.vector.tensor_tensor(alpha[:, 4 * c:4 * c + 4, :], bank(4 + 2 * c).rearrange("p (t n) -> p t n", t=4),
                                        rows1[:, 1, :].unsqueeze(1).broadcast_to([P, 4, D]), ALU.add).then_inc(gate1_biased, 1)
                v = x_cur[:, 4 * c:4 * c + 4, :]
                step(nc.vector.tensor_tensor(v, v, xn[:, 4 * c:4 * c + 4, :], ALU.add))

            def alpha_half(c):
                dve.wait_ge(alpha_tanh_ready, c + 1)
                v = alpha[:, 4 * c:4 * c + 4, :]
                step(nc.vector.tensor_scalar(v, v, 0.5, 0.5, ALU.mult, ALU.add))

            add_pair(0)
            add_pair(1)
            summed_stats(0)
            summed_stats(1)
            add_pair(2)
            summed_stats(2)
            summed_stats(3)
            half_variances(0, LN_EPS, hidden_var_ready)
            add_pair(3, range(4))
            rms(0)
            normalise(0, x_cur, hidden_norm_ready)
            dve.wait_ge(rows1_loaded, 80)
            normed_half(0)
            add_pair(3, range(4, E_VECTOR))
            summed_stats(4)
            summed_stats(5)
            gate_bias(0)
            summed_stats(6)
            summed_stats(7)
            half_variances(1, LN_EPS, hidden_var_ready)
            alpha_half(0)
            rms(1)
            normalise(1, x_cur, hidden_norm_ready)

            def max1(u):
                dve.wait_ge(scores1_ready, u + 1)
                if u >= 2:
                    dve.wait_ge(probs1_ready, u - 1)
                n = key_tiles(u) * P
                diagonal = S_PS[u % 2][:, n - P:n]
                link(nc.vector.tensor_tensor(diagonal, diagonal, causal[:, :], ALU.add))
                nc.vector.tensor_reduce(neg_max[:, u % 2:u % 2 + 1], S_PS[u % 2][:, 0:n], op=ALU.max, axis=AX.X,
                                        negate=True).then_inc(max1_ready, 1)

            def finish1(u):
                dve.wait_ge(probs1_ready, u + 1)
                link(nc.vector.reciprocal(rden[:, u, :], den[:, u, :]))
                dve.wait_ge(attended1_made, u + 1)
                link(nc.vector.scalar_tensor_tensor(acc4[:, u, :], bank(6 + u % 2, 0, D), rden[:, u, :], xn[:, u, :],
                                                    ALU.mult, ALU.subtract))
                link(nc.vector.tensor_tensor(acc4[:, u, :], acc4[:, u, :], alpha[:, u, :], ALU.mult))
                nc.vector.tensor_tensor(x_cur[:, u, :], x_cur[:, u, :], acc4[:, u, :], ALU.add).then_inc(x1_ready, 1)
                dve.wait_ge(x1_ready, u + 1)
                stats_of(x_cur[:, u, :], u)

            def x_low(c):
                dve.wait_ge(x1_high_ready, c + 1)
                nc.vector.tensor_tensor(xTl[:, 512 * c:512 * c + 512], xT[:, 512 * c:512 * c + 512],
                                        xTh[:, 512 * c:512 * c + 512], ALU.subtract).then_inc(x1_low_ready, 1)

            def low_weights(e, s, w):
                hi, lo = ((w1Th, w1Tl), (w2Th, w2Tl))[w]
                dve.wait_ge(expert_w_high_ready, e * 2 + (w + 1))
                nc.vector.tensor_tensor(lo[:, s, :], bank(w), hi[:, s, :], ALU.subtract).then_inc(expert_w_low_ready, 1)

            max1(0)
            normed_half(1)
            max1(1)
            gate_bias(1)
            alpha_half(1)
            settle()
            for u in range(NT):
                if u + 2 < NT:
                    max1(u + 2)
                if u == NT - 1:
                    x_low(0)
                    low_weights(0, 0, 0)
                    low_weights(0, 0, 1)
                finish1(u)
                if u == 3:
                    half_variances(0, LN_EPS, norm_var_ready)
                if u == 4:
                    dve.wait_ge(norm_rstd_ready, 3)
                    normalise(0, x_cur, norm_ready)

            def low_hidden(e, c, static):
                if not (static and e == 0):
                    dve.wait_ge(down_made, e * 4 + (2 * c - 2))
                for pair in range(0, FT, 2):
                    for f in (pair, pair + 1):
                        dve.wait_ge(gelu_ready, e * 8 + (4 * c + f + 1))
                        nc.vector.tensor_copy(hh[:, c, f, :], hf[:, f, :]).then_inc(units_high_ready, 1)
                    for f in (pair, pair + 1):
                        dve.wait_ge(units_high_ready, e * 8 + (4 * c + f + 1))
                        nc.vector.tensor_tensor(hl[:, c, f, :], hf[:, f, :], hh[:, c, f, :], ALU.subtract).then_inc(units_low_ready, 1)

            def add_expert(e, c, first, tiles=range(4)):
                for q in tiles:
                    t = 4 * c + q
                    if q % 2 == 0:
                        dve.wait_ge(down_made, e * 4 + (2 * c + q // 2 + 1))
                    if not first:
                        dve.wait_ge(expert_added, e * 8 + (t - 7))
                    nc.vector.scalar_tensor_tensor(
                        acc4[:, t, :], bank(4 + q // 2, (q % 2) * D, (q % 2 + 1) * D), gates[:, t, at(e, 1)],
                        xn[:, t, :] if first else acc4[:, t, :], ALU.mult, ALU.add).then_inc(expert_added, 1)

            def add_b2(c):
                dve.wait_ge(gates_b2_made, c + 1)
                if c == 0:
                    dve.wait_ge(expert_added, 4)
                else:
                    dve.wait_ge(expert_added, 8)
                v = acc4[:, 4 * c:4 * c + 4, :]
                nc.vector.tensor_tensor(v, v, bank(7).rearrange("p (t n) -> p t n", t=4), ALU.add).then_inc(gates_b2_added, 1)
                dve.wait_ge(gates_b2_added, c + 1)

            def expert(e, s, static=False, last=False):
                low_hidden(e, 0, static)
                if static and s == 0:
                    x_low(1)
                else:
                    add_expert(e - 1, 1, static)
                if static and s == 1:
                    add_b2(0)
                if not last:
                    low_weights(e + 1, 1 - s, 0)
                    low_weights(e + 1, 1 - s, 1)
                low_hidden(e, 1, static)
                if static and s == 0:
                    route(1, bank(7, 0, NT * E).rearrange("p (t e) -> p t e", t=NT))
                if static and s == 1:
                    add_b2(1)
                add_expert(e, 0, static and s == 0)

            half_variances(1, LN_EPS, norm_var_ready)
            dve.wait_ge(norm_rstd_ready, 4)
            normalise(1, x_cur, norm_ready)
            for s in range(2):
                expert(s, s, static=True)
            with dve.Fori(1, E // 2 - 1) as i:
                for s in range(2):
                    expert(i * 2 + s, s)
            for s in range(2):
                expert(E - 2 + s, s, last=s == 1)

            def last_stats(t):
                dve.wait_ge(expert_added, (E - 1) * NT + t + 1)
                stats_of(acc4[:, t, :], t)

            def centre(lo, hi):
                for t in range(lo, hi):
                    nc.vector.scalar_tensor_tensor(acc4[:, t, :], acc4[:, t, :], mv[:, t, 0:1], rows1[:, 2, :],
                                                   ALU.subtract, ALU.mult).then_inc(out_centred, 1)

            def scale_and_add(lo, hi, count):
                dve.wait_ge(norm_rstd_ready, count)
                for t in range(lo, hi):
                    dve.wait_ge(out_centred, t + 1)
                    nc.vector.scalar_tensor_tensor(acc4[:, t, :], acc4[:, t, :], rstd[:, t:t + 1], xb[:, t, :],
                                                   ALU.mult, ALU.add).then_inc(out_ready, 1)

            for t in range(4):
                last_stats(t)
            half_variances(0, LN2_EPS, norm_var_ready)
            centre(0, 4)
            for q in (0, 2):
                add_expert(E - 1, 1, False, (q, q + 1))
                last_stats(4 + q)
                last_stats(5 + q)
                variances(4 + q, 6 + q, LN2_EPS, norm_var_ready)
                centre(4 + q, 6 + q)
            dve.wait_ge(xb_ready, 1)
            scale_and_add(4, 6, 6)
            scale_and_add(6, 8, 7)

        @block.tensor
        def _(pe):
            mm = nc.tensor.matmul

            def transpose(dst, src):
                return nc.tensor.transpose(dst, src, ident[:, :])

            pe.wait_ge(const_ready, 3)

            def keep_clock(n, free_bank):
                for _ in range(n):
                    transpose(bank(free_bank, 0, P), ident[:, :])

            keep_clock(WARM_UP, 7)
            pe.wait_ge(w_first_loaded, 48)

            def weights_T(p):
                if p == FIRST_PAIRS:
                    pe.wait_ge(w_rest_loaded, 48)
                if p >= 2:
                    pe.wait_ge(pair_wT_copied, p - 1)
                c = p * P
                transpose(bank(p % 2, 0, 128), wq_sb[:, c:c + P])
                transpose(bank(p % 2, 128, 256), wkv_sb[:, c:c + P])
                transpose(bank(p % 2, 256, 384), wkv_sb[:, HEADS * DH + c:HEADS * DH + c + P]).then_inc(pair_wT_made, 1)

            def weights_AB(p):
                pe.wait_ge(pair_wT_copied, p + 1)
                if p >= 2:
                    pe.wait_ge(pair_ab_low_ready, p - 1)
                for h in range(2):
                    r = slice(DH * h, DH * h + DH)
                    wT = wqkvT[r, p % 2, :, :]
                    mm(AB_PS[p % 2][:, h, 0, :], wT[:, 0, :], wT[:, 1, :], start=True, stop=True)
                    last = mm(AB_PS[p % 2][:, h, 1, :], wT[:, 2, :], wout_sb[r, p, :], start=True, stop=True)
                last.then_inc(pair_ab_made, 1)

            def keys_T(b):
                for k, (lo, hi) in enumerate(KEY_PARTS):
                    wait_keys(pe, b, k + 1)
                    if b:
                        pe.wait_ge(keysT_low_ready, 2 * b - 1 + k)
                    for i in range(lo // P, hi // P):
                        last = transpose(bank(keys_bank(b, k), i * P - lo, i * P - lo + P), kvf[:, b, i, :])
                    last.then_inc(keysT_made, 1)

            def queries(n, k, heads):
                hs, b = (k // B) % 2, k % B
                if b == 0:
                    pe.wait_ge(head_ab_ready, heads + (k // B + 1))
                lat = slice(SC, NK)
                mm(QK_PS, ab[:, hs, 0, :], kth[:, b, lat], start=True, stop=False)
                mm(QK_PS, ab[:, hs, 0, :], ktl[:, b, lat], start=False, stop=False)
                mm(QK_PS, ab[:, hs, 1, :], kth[:, b, lat], start=False, stop=True).then_inc(queries_made, 1)

            weights_T(0)
            for p in range(NPAIR):
                if p + 1 < NPAIR:
                    weights_T(p + 1)
                else:
                    pe.wait_ge(keysT_low_ready, 2 * B - 2)
                    queries(0, 0, 0)
                weights_AB(p)
                if p % 2 and p + 1 < NPAIR:
                    keys_T(p // 2)

            def scores(n, k, j, first):
                b = k % B
                if j == 0:
                    pe.wait_ge(q_high_ready, n + 1)
                    pe.wait_ge(q_low_ready, n + 1)
                if not first:
                    pe.wait_ge(probs_ready, n * 2 + (j - 1))
                q = slice(j * P, j * P + P)
                for w, keys, start in ((qkh, kth, True), (qkh, ktl, False), (qkl, kth, False)):
                    for lo, hi in ((0, 512), (512, NK)):
                        last = mm(S_PS[j][:, lo:hi], w[:, k % 2, q], keys[:, b, lo:hi], start=start,
                                  stop=w is qkl, skip_group_check=True)
                last.then_inc(scores_ready, 1)

            def probs_T(n, j, first):
                pe.wait_ge(probs_ready, n * 2 + (j + 1))
                if not first:
                    pe.wait_ge(probsT_low_ready, n * 2 + j)
                for i in range(KT):
                    last = transpose(PT_PS[:, i * P:(i + 1) * P], probs[:, j, i * P:(i + 1) * P])
                last.then_inc(probsT_made, 1)

            def attend(n, k, half, start):
                b = k % B
                if half == 0:
                    pe.wait_ge(probsT_low_ready, n * 2 + 2)
                    if start < B:
                        pe.wait_ge(kv_low_ready, start + 1)
                    if start:
                        pe.wait_ge(attended_low_ready, n)
                for i in range(3 * half, 3 * half + 3):
                    mm(Y_PS, kvh[:, b, i, :], pth[:, k % 2, i, :], start=i == 0, stop=False, skip_group_check=True)
                    mm(Y_PS, kvh[:, b, i, :], ptl[:, k % 2, i, :], start=False, stop=False, skip_group_check=True)
                    last = mm(Y_PS, kvl[:, b, i, :], pth[:, k % 2, i, :], start=False, stop=i == KT - 1, skip_group_check=True)
                if half:
                    last.then_inc(attended_made, 1)

            def project(n, k, start):
                hs = (k // B) % 2
                pe.wait_ge(attended_low_ready, n + 1)
                if start:
                    pe.wait_ge(head_added, n * 2)
                for j in range(QT):
                    o, q = O_PS[:, j * P:(j + 1) * P], slice(j * P, j * P + P)
                    mm(o, yh[:, k % 2, q], ab[:, hs, 2, :], start=True, stop=False)
                    mm(o, yh[:, k % 2, q], ab[:, hs, 3, :], start=False, stop=False)
                    last = mm(o, yl[:, k % 2, q], ab[:, hs, 2, :], start=False, stop=True)
                last.then_inc(projected_made, 1)

            def item(n, k, heads, start=B + 2, last=False):
                scores(n, k, 0, start == 0)
                if start == 0:
                    pe.wait_ge(pair_ab_low_ready, NPAIR)
                    keys_T(B - 1)
                if start >= 1:
                    probs_T(n - 1, 1, False)
                if start >= 2:
                    attend(n - 2, (k - 2) % 8, 1, start - 2)
                if not last:
                    if start >= 3:
                        pe.wait_ge(head_added, n * 2 - 4)
                    queries(n + 1, k + 1, heads)
                scores(n, k, 1, start == 0)
                if start == 0:
                    pe.wait_ge(keysT_low_ready, 2 * B)
                probs_T(n, 0, start == 0)
                if start >= 1:
                    attend(n - 1, (k - 1) % 8, 0, start - 1)
                if start >= 2:
                    pe.wait_ge(q_low_ready, n + (1 if last else 2))
                    project(n - 2, (k - 2) % 8, start - 2)

            pe.wait_ge(pair_wT_copied, NPAIR)
            for k in range(8):
                item(k, k, 0, start=min(k, B + 2))
            with pe.Fori(1, ITEMS // 8 - 1) as p:
                for k in range(8):
                    item(p * 8 + k, k, p * 2)
            for k in range(8):
                item(ITEMS - 8 + k, k, HEADS - 2, last=k == 7)

            def w_out_T(e):
                if e >= 2:
                    pe.wait_ge(w_outT_copied, e - 1)
                for f in range(FT):
                    last = transpose(bank(e % 2, f * P, (f + 1) * P), w_out_sb[:, e, f * P:(f + 1) * P])
                last.then_inc(w_outT_made, 1)

            def w_in_out(e):
                if e + 1 < E:
                    w_out_T(e + 1)
                pe.wait_ge(w_outT_copied, e + 1)
                for f in range(FT):
                    last = mm(bank(2 + e // 4, (e % 4) * D, (e % 4 + 1) * D), w_in_sb[:, e, f, :], woT[:, e % 2, f, :],
                              start=f == 0, stop=f == FT - 1)
                last.then_inc(moe0_made, 1)

            probs_T(ITEMS - 1, 1, False)
            attend(ITEMS - 2, 6, 1, B)
            pe.wait_ge(w_in_loaded, 16)
            pe.wait_ge(w_out_loaded, 16)
            w_out_T(0)
            w_in_out(0)
            w_in_out(1)
            attend(ITEMS - 1, 7, 0, B)
            project(ITEMS - 2, 6, B)
            w_in_out(2)
            attend(ITEMS - 1, 7, 1, B)
            w_in_out(3)
            project(ITEMS - 1, 7, B)
            for e in range(4, E):
                w_in_out(e)
            pe.wait_ge(small_loaded, 48)
            pe.wait_ge(qk1w_loaded, 48)
            nc.tensor.transpose(bank(6, 0, E), small[:, 0:D], ident[0:E, 0:E])
            nc.tensor.transpose(bank(6, E, 2 * E), small[:, D:2 * D], ident[0:E, 0:E])
            nc.tensor.transpose(bank(6, 16, 16 + E * FT), b1n[:, :], ident[0:E * FT, 0:E * FT])
            transpose(bank(6, 128, 256), qk1w[:, 2, :])
            mm(bank(6, 256, 384), qk1w[:, 0, :], qk1w[:, 1, :], start=True, stop=True).then_inc(setup1_made, 1)

            def norm_T(need, c, dst):
                pe.wait_ge(norm_ready, need)
                for q in range(4):
                    last = transpose(dst[:, q * P:(q + 1) * P], xn[:, 4 * c + q, :])
                last.then_inc(normT_made, 1)

            def router(k, dst):
                for t in range(NT):
                    if t % 4 == 0:
                        pe.wait_ge(normT_copied, 2 * k + t // 4 + 1)
                    last = mm(dst[:, t * E:(t + 1) * E], xT[:, t * P:(t + 1) * P], wgT[:, k, :], start=True, stop=True)
                last.then_inc(logits_made, 1)

            pe.wait_ge(w_outT_copied, E)
            norm_T(4, 0, bank(0))
            norm_T(8, 1, bank(1))
            pe.wait_ge(setup1_copied, 4)
            router(0, bank(6))
            pe.wait_ge(moe0_low_ready, 2)
            pe.wait_ge(x0_low_ready, 2)
            pe.wait_ge(head_added, 2 * ITEMS)

            def banks0_free(t):
                pe.wait_ge(experts0_added, 2 * E_VECTOR * (t // 2 + 1))
                pe.wait_ge(experts0_scaled, 4 * (t + 1))

            def experts0(t):
                tok = slice(t * P, (t + 1) * P)
                for c in range(2):
                    if t == 1 and c == 0:
                        pe.wait_ge(gate_gap_ready, 1)
                    if t >= 4 and c == 0:
                        banks0_free(t - 4)
                    high, low = (m[:, 4 * c:4 * c + 4, :].rearrange("p e n -> p (e n)") for m in (moe0h, moe0l))
                    dst = bank(bank0(t, c))
                    mm(dst, xTh[:, tok], high, start=True, stop=False)
                    mm(dst, xTh[:, tok], low, start=False, stop=False)
                    mm(dst, xTl[:, tok], high, start=False, stop=True).then_inc(experts0_made, 1)

            def norms_T1(c):
                if c:
                    pe.wait_ge(inputs1T_copied, 2)
                else:
                    banks0_free(5)
                for w, (src, s) in enumerate(((xn, hidden_norm_ready), (normed, normed_ready))):
                    keep_clock(((14, 6), (4, 12))[c][w], 6 + w)
                    pe.wait_ge(s, 4 * c + 4)
                    for q in range(4):
                        last = transpose(bank(6 + w, q * P, (q + 1) * P), src[:, 4 * c + q, :])
                    last.then_inc(inputs1T_made, 1)

            def gate_and_queries(c):
                pe.wait_ge(inputs1T_copied, 2 * c + 1)
                if c == 0:
                    pe.wait_ge(setup1_copied, B + 4)
                for q in range(4):
                    t = 4 * c + q
                    last = mm(bank(4 + 2 * c, q * D, (q + 1) * D), xT[:, t * P:(t + 1) * P], gwT[:, :], start=True, stop=True)
                last.then_inc(gate1_made, 1)
                pe.wait_ge(inputs1T_copied, 2 * c + 2)
                mm(bank(5 + 2 * c), A1[:, :], normT[:, 512 * c:512 * c + 512], start=True, stop=True).then_inc(q1T_made, 1)

            def scores1(u):
                b, sp = u // 2, S_PS[u % 2]
                if u >= 2:
                    pe.wait_ge(probs1_ready, u - 1)
                else:
                    banks0_free(6 + u)
                pe.wait_ge(q1T_ready, u // 4 + 1)
                mm(sp[:, 0:SC], q1T[:, u * P:(u + 1) * P], ctxT[:, b, :], start=True, stop=True)
                n = key_tiles(u) * P - SC
                mm(sp[:, SC:SC + n], q1T[:, u * P:(u + 1) * P], normT[:, b * SQ:b * SQ + n], start=True, stop=True).then_inc(scores1_ready, 1)

            def probs_T1(u):
                pe.wait_ge(probs1_ready, u + 1)
                if u == 0:
                    pe.wait_ge(q1T_ready, 1)
                    pe.wait_ge(gate1_biased, 1)
                else:
                    pe.wait_ge(probs1T_ready, u)
                for i in range(key_tiles(u)):
                    last = transpose(PT_PS[:, i * P:(i + 1) * P], probs[:, u % 2, i * P:(i + 1) * P])
                last.then_inc(probs1T_made, 1)

            def attend1(u):
                b = u // 2
                pe.wait_ge(probs1T_ready, u + 1)
                if u >= 2:
                    pe.wait_ge(x1_ready, u - 1)
                else:
                    pe.wait_ge((gate1_biased, q1T_ready)[u], 2)
                for i in range(key_tiles(u)):
                    v = ctx_sb[:, b, i, :] if i < CT else normed[:, QT * b + i - CT, :]
                    last = mm(bank(6 + u % 2, 0, D), pt1[:, u % 2, i, :], v, start=i == 0, stop=i == key_tiles(u) - 1)
                last.then_inc(attended1_made, 1)

            for t in range(NT - 1):
                experts0(t)
            experts0(NT - 1)
            banks0_free(4)
            for b in range(B):
                if b >= 2:
                    pe.wait_ge(setup1_copied, b + 3)
                for i in range(CT):
                    last = transpose(bank(4 + b % 2, i * P, (i + 1) * P), ctx_sb[:, b, i, :])
                last.then_inc(setup1_made, 1)
            norms_T1(0)
            gate_and_queries(0)
            scores1(0)
            scores1(1)
            norms_T1(1)
            probs_T1(0)
            gate_and_queries(1)

            def expert_T(e, s, i, w, first):
                pe.wait_ge((w1_loaded, w2_loaded)[w][s], i * 16 + 16)
                if not first:
                    pe.wait_ge(expert_w_low_ready, e * 2 + (w - 1))
                for f in range(FT):
                    src = w2n[:, s, f * P:(f + 1) * P] if w else w1n[:, s, f, :]
                    last = transpose(bank(w, f * P, (f + 1) * P), src)
                last.then_inc(expert_wT_made, 1)

            for u in range(NT):
                if u:
                    probs_T1(u)
                if u == NT - 2:
                    norm_T(12, 0, bank(1))
                    expert_T(0, 0, 0, 0, True)
                if u + 2 < NT:
                    scores1(u + 2)
                if u == NT - 1:
                    pe.wait_ge(normT_copied, 3)
                    expert_T(0, 0, 0, 1, True)
                attend1(u)


            def up(e, s, c, g, static):
                if c == 0:
                    pe.wait_ge(expert_w_low_ready, e * 2 + 1)
                tok = slice(512 * c, 512 * c + 512)
                for f in range(FT):
                    if not static or 4 * (2 * e + c) + f >= 3:
                        pe.wait_ge(gelu_ready, e * 8 + (4 * c + f - (3 if g is None else 2)))
                    u, fs = bank(hidden_bank(g, f)), slice(f * P, f * P + P)
                    mm(u, w1Th[:, s, fs], xTh[:, tok], start=True, stop=False)
                    mm(u, w1Th[:, s, fs], xTl[:, tok], start=False, stop=False)
                    mm(u, w1Tl[:, s, fs], xTh[:, tok], start=False, stop=True).then_inc(up_made, 1)

            def down(e, s, c, static):
                if c == 0:
                    pe.wait_ge(expert_w_low_ready, e * 2 + 2)
                pe.wait_ge(units_low_ready, e * 8 + (4 * c + 4))
                for q in range(4):
                    if q % 2 == 0 and not (static and e == 0 and c == 0):
                        pe.wait_ge(expert_added, e * 8 + (4 * c + q - 2))
                    o, tok = bank(4 + q // 2, (q % 2) * D, (q % 2 + 1) * D), slice(q * P, q * P + P)
                    for f in range(FT):
                        w = slice(f * D, f * D + D)
                        mm(o, hh[:, c, f, tok], w2Th[:, s, w], start=f == 0, stop=False)
                        mm(o, hh[:, c, f, tok], w2Tl[:, s, w], start=False, stop=False)
                        last = mm(o, hl[:, c, f, tok], w2Th[:, s, w], start=False, stop=f == FT - 1)
                    if q % 2:
                        last.then_inc(down_made, 1)

            def gates_b2(c):
                pe.wait_ge(gatesT_ready, 1)
                if c:
                    pe.wait_ge(gates_b2_added, 1)
                mm(bank(7), gT[:, :], b2d[:, 4 * c:4 * c + 4, :].rearrange("p t d -> p (t d)"), start=True, stop=True).then_inc(gates_b2_made, 1)

            def expert(e, s, i, first=False, last=False):
                g, g1 = (2, 3) if first else (None, None)
                up(e, s, 0, g, first)
                if first:
                    keep_clock(16, 0)
                    pe.wait_ge(gates_ready, 2)
                    pe.wait_ge(b2_loaded, 16 * NT)
                    transpose(ps[0:NT * E, 7, 0:P], gates[:, :, :].rearrange("p t e -> p (t e)")).then_inc(gatesT_made, 1)
                down(e - 1, 1 - s, 1, first)
                if first:
                    gates_b2(0)
                if not last:
                    for w in range(2):
                        expert_T(e + 1, 1 - s, i + s, w, False)
                up(e, s, 1, g1, first)
                if first:
                    gates_b2(1)
                down(e, s, 0, first)

            def expert_0():
                up(0, 0, 0, 0, True)
                for w in range(2):
                    expert_T(1, 1, 0, w, False)
                norm_T(16, 1, bank(7))
                keep_clock(18, 4)
                down(0, 0, 0, True)
                pe.wait_ge(x1_low_ready, 2)
                up(0, 0, 1, 1, True)
                pe.wait_ge(normT_copied, 4)
                router(1, bank(7))

            pe.wait_ge(x1_low_ready, 1)
            expert_0()
            expert(1, 1, 0, first=True)
            pe.wait_ge(gates_b2_added, 2)
            with pe.Fori(1, E // 2 - 1) as i:
                for s in range(2):
                    expert(i * 2 + s, s, i)
            for s in range(2):
                expert(E - 2 + s, s, E // 2 - 1, last=s == 1)
            down(E - 1, 1, 1, False)


_INS = ['x', 'ctx_1024', 'L0_xattn_ln_m_g', 'L0_xattn_ln_m_b', 'L0_xattn_ln_l_g', 'L0_xattn_ln_l_b',
        'L0_xattn_Wq', 'L0_xattn_Wkv', 'L0_xattn_Wout', 'L0_ffn_w_gate', 'L0_ffn_w_in', 'L0_ffn_w_out',
        'L1_xattn_q_w', 'L1_xattn_k_w', 'L1_xattn_norm_w', 'L1_xattn_gate_w', 'L1_xattn_gate_b',
        'L1_ffn_router_w', 'L1_ffn_router_b', 'L1_ffn_w1', 'L1_ffn_b1', 'L1_ffn_w2', 'L1_ffn_b2',
        'L1_ffn_ln_w', 'L1_ffn_ln_b']


def kernel(**inputs):
    import numpy as _np
    import concourse.bacc as _bacc
    from concourse import mybir as _mybir
    from concourse.bass_utils import run_bass_kernel_spmd as _run

    nc = _bacc.Bacc("TRN2", target_bir_lowering=False, num_devices=1)
    arrays, aps = {}, {}
    for name in _INS:
        a = _np.ascontiguousarray(inputs[name])
        arrays[f"in_{name}"] = a
        aps[name] = nc.dram_tensor(f"in_{name}", a.shape, _mybir.dt.from_np(a.dtype), kind="ExternalInput").ap()
    out = nc.dram_tensor("out_0", (B, SQ, D), _mybir.dt.float32, kind="ExternalOutput").ap()
    transformer_program(nc, aps, out)
    r = _run(nc, [arrays], core_ids=[0])
    return r.results[0]["out_0"]
```
